# Optimizing a Trainium2 kernel written in Bass

```python
import numpy as np
import jax
import jax.numpy as jnp

def _softmax(x, axis=-1):
    return jax.nn.softmax(x, axis=axis)

def _gelu(x):
    return jax.nn.gelu(x, approximate=True)

def _silu(x):
    return jax.nn.silu(x)

def _sigmoid(x):
    return jax.nn.sigmoid(x)

def _layernorm(x, axis=-1, eps=1e-05):
    m = jnp.mean(x, axis=axis, keepdims=True)
    v = jnp.var(x, axis=axis, keepdims=True)
    return (x - m) / jnp.sqrt(v + eps)

def _scatter_add(tgt, idx, src, axis=0):
    return tgt.at[idx].add(src)

def _segment_sum(src, seg, n):
    return jax.ops.segment_sum(src, seg, n)
kernel_name = 'mk_gps_d1_gnn_r8_bff6d9'

def setup_inputs(seed: int=0):
    np.random.seed(seed)
    _w = jnp.asarray

    def _rec_inputs():
        import jax
        import jax.numpy as jnp
        _gk = jax.random.key(seed)
        x = -0.0005963 + 1.001 * jax.random.normal(jax.random.fold_in(_gk, 1), (384, 1024), jnp.float32)
        src = jax.random.randint(jax.random.fold_in(_gk, 2), (12288,), 0, 384, jnp.int32)
        dst = jax.random.randint(jax.random.fold_in(_gk, 3), (12288,), 0, 384, jnp.int32)
        _o = jnp.argsort(dst, stable=True)
        src = src[_o]
        dst = dst[_o]
        edge_type_5 = jax.random.randint(jax.random.fold_in(_gk, 12), (12288,), 0, 5, jnp.int32)
        return (x, src, dst, edge_type_5)
    x, src, dst, edge_type_5 = _rec_inputs()

    def _L0_gnn_setup():
        import jax, jax.numpy as jnp
        import numpy as np
        N = 384
        E = 12288
        IN_F = 1024
        OUT_F = 1024
        H = 16
        D = OUT_F // H
        NUM_ETYPES = 4

        def _build_mask(edge_index, edge_type, edge_type_weights, dtype):
            src, dst = (edge_index[0], edge_index[1])
            w = jax.nn.softplus(edge_type_weights)
            mask = jnp.full((N, N), -jnp.inf, dtype=dtype)
            mask = mask.at[src, dst].set(w[edge_type - 1])
            diag = jnp.diagonal(mask)
            idx = jnp.arange(N)
            mask = mask.at[idx, idx].set(jnp.where(jnp.isneginf(diag), w[3], diag))
            return mask
        key = jax.random.key(seed)
        ks = jax.random.split(key, 20)
        p = lambda k, shape: jax.random.normal(k, shape, dtype=jnp.float32) * 0.02
        return {'x': jax.random.normal(ks[0], (N, IN_F), dtype=jnp.float32), 'edge_index': jax.random.randint(ks[1], (2, E), 0, N), 'edge_type': jax.random.randint(ks[2], (E,), 1, NUM_ETYPES + 1), 'edge_type_weights': jnp.ones((NUM_ETYPES,), jnp.float32) + 0.1 * jax.random.normal(ks[3], (NUM_ETYPES,), dtype=jnp.float32), 'wq': p(ks[4], (OUT_F, IN_F)), 'bq': p(ks[5], (OUT_F,)), 'wk': p(ks[6], (OUT_F, IN_F)), 'bk': p(ks[7], (OUT_F,)), 'wv': p(ks[8], (OUT_F, IN_F)), 'bv': p(ks[9], (OUT_F,)), 'wiq': p(ks[10], (OUT_F, OUT_F)), 'biq': p(ks[11], (OUT_F,)), 'wik': p(ks[12], (OUT_F, OUT_F)), 'bik': p(ks[13], (OUT_F,)), 'wiv': p(ks[14], (OUT_F, OUT_F)), 'biv': p(ks[15], (OUT_F,)), 'wo': p(ks[16], (OUT_F, OUT_F)), 'bo': p(ks[17], (OUT_F,))}
    _L0_gnn_all = _L0_gnn_setup()
    _L0_gnn_in = {k: v for k, v in _L0_gnn_all.items() if k in ('edge_type_weights', 'wq', 'bq', 'wk', 'bk', 'wv', 'bv', 'wiq', 'biq', 'wik', 'bik', 'wiv', 'biv', 'wo', 'bo')}
    del _L0_gnn_all

    def _L0_mix_setup():
        import jax, jax.numpy as jnp
        import numpy as np
        B, S, D = (4, 512, 1024)
        H = 16
        HD = D // H

        def feature_map(x):
            return jnp.exp(-jnp.square(x) * 0.5)
        key = jax.random.key(seed)
        ks = jax.random.split(key, 9)
        s = 1.0 / np.sqrt(D)
        return {'x': jax.random.normal(ks[0], (B, S, D), dtype=jnp.float32), 'Wq': jax.random.normal(ks[1], (D, D), dtype=jnp.float32) * s, 'bq': jax.random.normal(ks[2], (D,), dtype=jnp.float32) * s, 'Wk': jax.random.normal(ks[3], (D, D), dtype=jnp.float32) * s, 'bk': jax.random.normal(ks[4], (D,), dtype=jnp.float32) * s, 'Wv': jax.random.normal(ks[5], (D, D), dtype=jnp.float32) * s, 'bv': jax.random.normal(ks[6], (D,), dtype=jnp.float32) * s, 'Wo': jax.random.normal(ks[7], (D, D), dtype=jnp.float32) * s, 'bo': jax.random.normal(ks[8], (D,), dtype=jnp.float32) * s}
    _L0_mix_all = _L0_mix_setup()
    _L0_mix_in = {k: v for k, v in _L0_mix_all.items() if k in ('Wq', 'bq', 'Wk', 'bk', 'Wv', 'bv', 'Wo', 'bo')}
    del _L0_mix_all

    def _L0_ffn_setup():
        import jax, jax.numpy as jnp
        import numpy as np
        B, T, D, R, E = (32, 1024, 1024, 64, 8)
        key = jax.random.key(seed)
        ks = jax.random.split(key, 12)
        inp = {}
        inp['x'] = jax.random.normal(ks[0], (B, T, D), dtype=jnp.float32)
        inp['base_W'] = jax.random.normal(ks[1], (D, D), dtype=jnp.float32) * (1.0 / np.sqrt(D))
        inp['base_b'] = jax.random.normal(ks[2], (D,), dtype=jnp.float32) * 0.01
        inp['disc_mu'] = jax.random.normal(ks[3], (E, D), dtype=jnp.float32) * 0.5
        inp['disc_sigma'] = jax.random.uniform(ks[4], (E, D), dtype=jnp.float32, minval=0.5, maxval=1.5)
        inp['down_W'] = jax.random.normal(ks[5], (E, D, R), dtype=jnp.float32) * (1.0 / np.sqrt(D))
        inp['down_b'] = jax.random.normal(ks[6], (E, R), dtype=jnp.float32) * 0.01
        inp['up_W'] = jax.random.normal(ks[7], (E, R, D), dtype=jnp.float32) * (1.0 / np.sqrt(R))
        inp['up_b'] = jax.random.normal(ks[8], (E, D), dtype=jnp.float32) * 0.01
        inp['conv_W'] = jax.random.normal(ks[9], (E, D, D), dtype=jnp.float32) * 0.02
        inp['conv_b'] = jax.random.normal(ks[10], (E, D), dtype=jnp.float32) * 0.01
        return inp
    _L0_ffn_all = _L0_ffn_setup()
    _L0_ffn_in = {k: v for k, v in _L0_ffn_all.items() if k in ('base_W', 'base_b', 'disc_mu', 'disc_sigma', 'down_W', 'down_b', 'up_W', 'up_b', 'conv_W', 'conv_b')}
    del _L0_ffn_all
    return {'x': x, 'src': src, 'dst': dst, 'edge_type_5': edge_type_5, 'L0_gnn_edge_type_weights': _L0_gnn_in['edge_type_weights'], 'L0_gnn_wq': _L0_gnn_in['wq'], 'L0_gnn_bq': _L0_gnn_in['bq'], 'L0_gnn_wk': _L0_gnn_in['wk'], 'L0_gnn_bk': _L0_gnn_in['bk'], 'L0_gnn_wv': _L0_gnn_in['wv'], 'L0_gnn_bv': _L0_gnn_in['bv'], 'L0_gnn_wiq': _L0_gnn_in['wiq'], 'L0_gnn_biq': _L0_gnn_in['biq'], 'L0_gnn_wik': _L0_gnn_in['wik'], 'L0_gnn_bik': _L0_gnn_in['bik'], 'L0_gnn_wiv': _L0_gnn_in['wiv'], 'L0_gnn_biv': _L0_gnn_in['biv'], 'L0_gnn_wo': _L0_gnn_in['wo'], 'L0_gnn_bo': _L0_gnn_in['bo'], 'L0_mix_Wq': _L0_mix_in['Wq'], 'L0_mix_bq': _L0_mix_in['bq'], 'L0_mix_Wk': _L0_mix_in['Wk'], 'L0_mix_bk': _L0_mix_in['bk'], 'L0_mix_Wv': _L0_mix_in['Wv'], 'L0_mix_bv': _L0_mix_in['bv'], 'L0_mix_Wo': _L0_mix_in['Wo'], 'L0_mix_bo': _L0_mix_in['bo'], 'L0_ffn_base_W': _L0_ffn_in['base_W'], 'L0_ffn_base_b': _L0_ffn_in['base_b'], 'L0_ffn_disc_mu': _L0_ffn_in['disc_mu'], 'L0_ffn_disc_sigma': _L0_ffn_in['disc_sigma'], 'L0_ffn_down_W': _L0_ffn_in['down_W'], 'L0_ffn_down_b': _L0_ffn_in['down_b'], 'L0_ffn_up_W': _L0_ffn_in['up_W'], 'L0_ffn_up_b': _L0_ffn_in['up_b'], 'L0_ffn_conv_W': _L0_ffn_in['conv_W'], 'L0_ffn_conv_b': _L0_ffn_in['conv_b']}

def reference(x, src, dst, edge_type_5, L0_gnn_edge_type_weights, L0_gnn_wq, L0_gnn_bq, L0_gnn_wk, L0_gnn_bk, L0_gnn_wv, L0_gnn_bv, L0_gnn_wiq, L0_gnn_biq, L0_gnn_wik, L0_gnn_bik, L0_gnn_wiv, L0_gnn_biv, L0_gnn_wo, L0_gnn_bo, L0_mix_Wq, L0_mix_bq, L0_mix_Wk, L0_mix_bk, L0_mix_Wv, L0_mix_bv, L0_mix_Wo, L0_mix_bo, L0_ffn_base_W, L0_ffn_base_b, L0_ffn_disc_mu, L0_ffn_disc_sigma, L0_ffn_down_W, L0_ffn_down_b, L0_ffn_up_W, L0_ffn_up_b, L0_ffn_conv_W, L0_ffn_conv_b):
    import jax
    import jax.numpy as jnp

    def _L0_gnn_ref(x, edge_index, edge_type, edge_type_weights, wq, bq, wk, bk, wv, bv, wiq, biq, wik, bik, wiv, biv, wo, bo):
        import jax, jax.numpy as jnp
        import numpy as np
        N = 384
        E = 12288
        IN_F = 1024
        OUT_F = 1024
        H = 16
        D = OUT_F // H
        NUM_ETYPES = 4

        def _build_mask(edge_index, edge_type, edge_type_weights, dtype):
            src, dst = (edge_index[0], edge_index[1])
            w = jax.nn.softplus(edge_type_weights)
            mask = jnp.full((N, N), -jnp.inf, dtype=dtype)
            mask = mask.at[src, dst].set(w[edge_type - 1])
            diag = jnp.diagonal(mask)
            idx = jnp.arange(N)
            mask = mask.at[idx, idx].set(jnp.where(jnp.isneginf(diag), w[3], diag))
            return mask
        q = x @ wq.T + bq
        k = x @ wk.T + bk
        v = x @ wv.T + bv
        q2 = (q @ wiq.T + biq).reshape(N, H, D).transpose(1, 0, 2)
        k2 = (k @ wik.T + bik).reshape(N, H, D).transpose(1, 0, 2)
        v2 = (v @ wiv.T + biv).reshape(N, H, D).transpose(1, 0, 2)
        mask = _build_mask(edge_index, edge_type, edge_type_weights, x.dtype)
        scale = 1.0 / np.sqrt(D).astype(np.float32)
        scores = jnp.einsum('hnd,hmd->hnm', q2, k2) * scale + mask[None]
        attn = jax.nn.softmax(scores, axis=-1)
        out = jnp.einsum('hnm,hmd->hnd', attn, v2)
        out = out.transpose(1, 0, 2).reshape(N, OUT_F)
        return out @ wo.T + bo

    def _L0_mix_ref(x, Wq, bq, Wk, bk, Wv, bv, Wo, bo):
        import jax, jax.numpy as jnp
        import numpy as np
        B, S, D = (4, 512, 1024)
        H = 16
        HD = D // H

        def feature_map(x):
            return jnp.exp(-jnp.square(x) * 0.5)
        b, s, _ = x.shape
        q = feature_map((x @ Wq + bq).reshape(b, s, H, HD))
        k = feature_map((x @ Wk + bk).reshape(b, s, H, HD))
        v = (x @ Wv + bv).reshape(b, s, H, HD)
        coeff = jnp.sum(q * k, axis=-1, keepdims=True)
        qkv = coeff * v
        out = qkv.reshape(b, s, H * HD)
        return out @ Wo + bo

    def _L0_ffn_ref(x, base_W, base_b, disc_mu, disc_sigma, down_W, down_b, up_W, up_b, conv_W, conv_b):
        import jax, jax.numpy as jnp
        import numpy as np
        B, T, D, R, E = (32, 1024, 1024, 64, 8)
        base = jnp.einsum('btd,od->bto', x, base_W) + base_b
        m1 = x.mean(axis=1)
        m2 = (x * x).mean(axis=1)
        inv_var = 1.0 / (disc_sigma * disc_sigma)
        losses = (jnp.einsum('bd,ed->eb', m2, inv_var) - 2.0 * jnp.einsum('bd,ed->eb', m1, disc_mu * inv_var) + jnp.sum(disc_mu * disc_mu * inv_var, axis=1)[:, None]) / D
        idx = jnp.argmin(losses, axis=0)
        Wd, bd = (down_W[idx], down_b[idx])
        Wu, bu = (up_W[idx], up_b[idx])
        Wc, bc = (conv_W[idx], conv_b[idx])
        h = jax.nn.relu(jnp.einsum('btd,bdr->btr', x, Wd) + bd[:, None, :])
        a = jnp.einsum('btr,brd->btd', h, Wu) + bu[:, None, :]
        y = jnp.einsum('btd,bod->bto', a, Wc) + bc[:, None, :]
        return base + y
    edge_index = jnp.stack([src, dst])
    xn = _layernorm(x, axis=-1)
    x = x + _L0_gnn_ref(xn, edge_index, edge_type_5, L0_gnn_edge_type_weights, L0_gnn_wq, L0_gnn_bq, L0_gnn_wk, L0_gnn_bk, L0_gnn_wv, L0_gnn_bv, L0_gnn_wiq, L0_gnn_biq, L0_gnn_wik, L0_gnn_bik, L0_gnn_wiv, L0_gnn_biv, L0_gnn_wo, L0_gnn_bo) + _L0_mix_ref(xn[None], L0_mix_Wq, L0_mix_bq, L0_mix_Wk, L0_mix_bk, L0_mix_Wv, L0_mix_bv, L0_mix_Wo, L0_mix_bo)[0]
    x = x + _L0_ffn_ref(_layernorm(x, axis=-1)[None], L0_ffn_base_W, L0_ffn_base_b, L0_ffn_disc_mu, L0_ffn_disc_sigma, L0_ffn_down_W, L0_ffn_down_b, L0_ffn_up_W, L0_ffn_up_b, L0_ffn_conv_W, L0_ffn_conv_b)[0]
    return x

_drawn_inputs = setup_inputs


def setup_inputs(seed=0):
    import zlib

    import numpy as np

    out = dict(_drawn_inputs(seed))
    spreads = {}
    factors = {'L0_gnn_edge_type_weights': 8.0,
     'L0_gnn_wq': 8.0,
     'L0_gnn_bq': 8.0,
     'L0_gnn_wk': 8.0,
     'L0_gnn_bk': 200.0,
     'L0_gnn_wv': 8.0,
     'L0_gnn_bv': 8.0,
     'L0_gnn_wiq': 8.0,
     'L0_gnn_biq': 8.0,
     'L0_gnn_wik': 8.0,
     'L0_gnn_bik': 200.0,
     'L0_gnn_wiv': 8.0,
     'L0_gnn_biv': 64.0,
     'L0_gnn_wo': 8.0,
     'L0_gnn_bo': 200.0,
     'L0_mix_bq': 200.0,
     'L0_mix_bk': 200.0,
     'L0_mix_bo': 200.0,
     'L0_ffn_base_b': 200.0,
     'L0_ffn_disc_mu': 4.055,
     'L0_ffn_disc_sigma': 4.109,
     'L0_ffn_down_W': 4.945,
     'L0_ffn_down_b': 64.0,
     'L0_ffn_up_W': 4.186,
     'L0_ffn_up_b': 200.0,
     'L0_ffn_conv_W': 4.069,
     'L0_ffn_conv_b': 200.0,
     'L0_mix_Wq': 35.282,
     'L0_mix_Wk': 35.782,
     'L0_mix_bv': 63.2,
     'L0_ffn_base_W': 8.0,
     'L0_mix_Wv': 2.84,
     'L0_mix_Wo': 2.758}
    for name, (base, spread) in spreads.items():
        noise = np.random.default_rng([zlib.crc32(name.encode()), seed]).standard_normal(out[name].shape)
        drawn = base * np.exp(spread * noise) if base else spread * noise
        out[name] = jnp.asarray(drawn.astype(out[name].dtype))
    for name, factor in factors.items():
        out[name] = (out[name] * factor).astype(out[name].dtype)
    return out
```

```python
from contextlib import ExitStack

import concourse.bass as bass
from concourse import mybir

F32 = mybir.dt.float32
F32R = mybir.dt.float32r
BF16 = mybir.dt.bfloat16
F16 = mybir.dt.float16
I32 = mybir.dt.int32
U32 = mybir.dt.uint32
ALU = mybir.AluOpType
ACT = mybir.ActivationFunctionType
X = mybir.AxisListType.X
ds = bass.ds

P = 128
N = 384
D = 1024
NT = N // P
KB = D // P
HD = 64
HALF = 512
E = 12288
CH = E // P
GCH = CH // 2
EXPERTS = 8
R = 64
EPS = 1e-5
SCALE = 1.0 / HD ** 0.5
ABSENT = -1e30
SLOTS = 3

A_BASE = [4 * m for m in range(6)]
B_BASE = [24, 24, 0]
C_BASE = 32
E_BASE = 40
V_BASE = 44

C_ID, C_IOTA, C_TRI, C_POW, C_ONES, C_EIDX, C_ONE, C_ALL = 0, 128, 512, 640, 736, 864, 872, 1000


def gps_layer(nc, x, out, weights, conv, down, upT, up_b, down_b, conv_b, disc, bias_cols,
              rows, edge_weights, edge_rows, edge_cols, consts):
    with ExitStack() as ctx:
        def sb(name, shape, dt):
            return ctx.enter_context(nc.sbuf_tensor(name, shape, dt))

        def sem(name):
            return ctx.enter_context(nc.semaphore(name))

        key_dram = nc.dram_tensor("key_dram", [CH, P], F32, kind="Internal").ap()

        raw = [sb(f"raw{s}", [P, D], F32) for s in range(SLOTS)]
        w_hi = [sb(f"w_hi{s}", [P, D], F32R) for s in range(SLOTS)]
        w_lo = [sb(f"w_lo{s}", [P, D], F32R) for s in range(SLOTS)]
        xT = [sb(f"xT_{c}", [P, KB, N], F32R) for c in ("hi", "lo")]
        T0 = [sb(f"T0_{c}", [P, KB, N], F32R) for c in ("hi", "lo")]
        T1 = [sb(f"T1_{c}", [P, KB, N], F32R) for c in ("hi", "lo")]
        Q2 = sb("Q2", [P, KB, N], F32)
        K2 = sb("K2", [P, KB, N], F32)
        V2 = sb("V2", [P, KB, N], F32)
        mask = sb("mask", [P, NT, N], F32)
        U = sb("U", [P, 6 * D], F32)
        x_rows = U[:, 0:NT * D].rearrange("p (t d) -> p t d", t=NT)
        xn_rows = U[:, NT * D:2 * NT * D].rearrange("p (t d) -> p t d", t=NT)
        src_hot = U[:, 0:2 * N].bitcast(BF16).rearrange("p (s c n) -> p s c n", s=2, c=2)
        dst_hot = U[:, 2 * N:4 * N].bitcast(BF16).rearrange("p (s c n) -> p s c n", s=2, c=2)
        key_row = U[:, 3456:3968].rearrange("p (s n) -> p s n", s=2)
        key_junk = U[:, 3968:4096]
        table2 = U[:, 0:NT * N].rearrange("p (t n) -> p t n", t=NT)
        codes = U[:, NT * N:2 * NT * N].rearrange("p (t n) -> p t n", t=NT)
        pick = U[:, 4608:4608 + NT * N].rearrange("p (t n) -> p t n", t=NT)
        prob = U[:, 0:2 * NT * N].rearrange("p (h t n) -> p h t n", h=2, t=NT)
        sq_q = U[:, 2304:2688]
        sq_k = U[:, 2688:3072]
        mix_v = U[:, 3072:3456]
        pv_low = U[:, 3456:3840]
        attn_o = U[:, 3840:4224]
        v_cur = U[:, 4224:4608]
        qh, ql = sb("qh", [P, N], F32R), sb("ql", [P, N], F32R)
        kzh = [sb(f"kzh{h}", [P, N], F32R) for h in range(2)]
        kzl = [sb(f"kzl{h}", [P, N], F32R) for h in range(2)]
        vs = sb("vs", [P, NT, 2, P], F32R)
        probT = [sb(f"probT_{c}", [P, NT, N], F32R) for c in ("hi", "lo")]
        feat = [sb(f"feat_{c}", [P, N], F32R) for c in ("hi", "lo")]
        cst = sb("cst", [P, C_ALL], F32)
        ident = cst[:, C_ID:C_ID + P]
        tri = cst[:, C_TRI:C_TRI + P]
        eidx = cst[:, C_EIDX:C_EIDX + EXPERTS]
        ones_f32 = cst[:, C_ONE:C_ONE + P]
        iota16 = sb("iota16", [P, N], F16)
        zero16 = sb("zero16", [P, P], BF16)
        head_ones = sb("head_ones", [P, P], F32R)
        bias = sb("bias", [P, 9 * KB], F32)
        ew = sb("ew", [P, 4], F32)
        ew_t = sb("ew_t", [P, 8], F32)
        v2f = V2[:].rearrange("p k n -> p (k n)")
        erow_i = v2f[0:CH, 0:2 * P].bitcast(I32)
        erow = v2f[0:CH, 2 * P:4 * P]
        ecol_i = v2f[:, 4 * P:4 * P + 3 * CH].bitcast(I32)
        ecol = sb("ecol", [P, 3 * CH], F32)
        ekey = sb("ekey", [P, CH], F32)
        etype = sb("etype", [P, CH], F32)
        digit = [etype[:]] + [v2f[:, 1024 + c * CH:1024 + (c + 1) * CH] for c in range(4)]
        diag16 = v2f[:, 1408:1408 + 320].bitcast(BF16)
        diag_w = v2f[:, 1728:1728 + 64].bitcast(BF16)
        dup = sb("dup", [P, CH], F32)
        live_w = sb("live_w", [P, CH], F32)
        stats = sb("stats", [P, NT, 2, 6], F32)
        mv = sb("mv", [P, NT, 2], F32)
        rstd = sb("rstd", [P, 3, NT], F32)
        smax = sb("smax", [P, 2, NT], F32)
        nmax = sb("nmax", [P, 2, NT], F32)
        ssum = sb("ssum", [P, 2, NT], F32)
        rsum = sb("rsum", [P, 2, NT], F32)
        tiny = sb("tiny", [P, 24], F32)
        PS = ctx.enter_context(nc.psum_tensor("PS", [P, 8, HALF], F32))

        row_bo = Q2[:].rearrange("p k n -> p (k n)")[:, 0:3 * D].rearrange("p (r d) -> p r d", r=3)
        k2f = K2[:].rearrange("p k n -> p (k n)")
        conv_row = k2f[:, 0:D]
        raw_down = k2f[:, D:D + KB * R].rearrange("p (k r) -> p k r", k=KB)
        raw_up = k2f[:, D + 512:D + 512 + KB * R].rearrange("p (k r) -> p k r", k=KB)
        raw_upb = k2f[:, 2 * D:2 * D + KB]
        raw_downb = k2f[:, 2 * D + 8:2 * D + 9]
        h_low = k2f[:, 2 * D + 16:2 * D + 16 + N]
        h_sum = k2f[:, 2 * D + 400:2 * D + 400 + N]
        sq_junk = v2f[:, 0:N]
        t0h = T0[0][:].rearrange("p k n -> p (k n)")
        t0l = T0[1][:].rearrange("p k n -> p (k n)")
        wd = t0h[:, 0:KB * P].rearrange("p (k m) -> p k m", k=KB)
        hT = [t0h[:, D:D + N], t0h[:, D + N:D + 2 * N]]
        aug = [t0l[:, c * D:(c + 1) * D].rearrange("p (k m) -> p k m", k=KB) for c in range(2)]
        pc = [T1[c][:].rearrange("p k n -> p (k n)")[:, 0:D] for c in range(2)]
        disc_in = sb("disc_in", [P, 2, EXPERTS, KB], F32)
        dterm = sb("dterm", [P, 5, EXPERTS, KB], F32)
        moments = sb("moments", [P, 4, KB], F32)
        loss = sb("loss", [P, 5, EXPERTS], F32)
        pick_i = sb("pick_i", [P, 1], I32)

        w_in = [sem(f"w_in{s}") for s in range(SLOTS)]
        hi_ready = [sem(f"hi_ready{s}") for s in range(SLOTS)]
        lo_ready = [sem(f"lo_ready{s}") for s in range(SLOTS)]
        w_used = [sem(f"w_used{s}") for s in range(SLOTS)]
        keys_zeroed = sem("keys_zeroed")
        const_in = sem("const_in")
        edges_in = sem("edges_in")
        x_in = sem("x_in")
        key_out = sem("key_out")
        key_calc = sem("key_calc")
        key_in = [sem(f"key_in{s}") for s in range(2)]
        prep = sem("prep")
        aprep = sem("aprep")
        norm_step = sem("norm_step")
        rstd_guess = sem("rstd_guess")
        xn_ready = sem("xn_ready")
        xt_turned = sem("xt_turned")
        xt_hi = sem("xt_hi")
        xt_done = sem("xt_done")
        evac_hi = sem("evac_hi")
        evac_done = sem("evac_done")
        dup_ready = sem("dup_ready")
        live_ready = sem("live_ready")
        hot_ready = sem("hot_ready")
        hot_used = sem("hot_used")
        table_done = sem("table_done")
        table1_read = sem("table1_read")
        table2_read = sem("table2_read")
        mask_step = sem("mask_step")
        v_in = sem("v_in")
        v_turned = sem("v_turned")
        vh_ready = sem("vh_ready")
        vs_ready = sem("vs_ready")
        qk_hi = sem("qk_hi")
        ql_ready = sem("ql_ready")
        kl_ready = sem("kl_ready")
        score_done = sem("score_done")
        score_read = sem("score_read")
        nmax_ready = sem("nmax_ready")
        exp_done = sem("exp_done")
        recip_done = sem("recip_done")
        prob_ready = sem("prob_ready")
        prob_turned = sem("prob_turned")
        pT_hi = sem("pT_hi")
        pT_ready = sem("pT_ready")
        pv_done = sem("pv_done")
        pv_copied = sem("pv_copied")
        o_summed = sem("o_summed")
        oh_ready = sem("oh_ready")
        ol_ready = sem("ol_ready")
        sq_done = sem("sq_done")
        sq_summed = sem("sq_summed")
        feat_exp = sem("feat_exp")
        feat_hi = sem("feat_hi")
        feat_ready = sem("feat_ready")
        coeff_done = sem("coeff_done")
        mixv_ready = sem("mixv_ready")
        mix_ready = sem("mix_ready")
        mh_ready = sem("mh_ready")
        ml_ready = sem("ml_ready")
        rows_in = sem("rows_in")
        xr_in = sem("xr_in")
        res_ready = sem("res_ready")
        x2_ready = sem("x2_ready")
        x2n_ready = sem("x2n_ready")
        x2_turned = sem("x2_turned")
        x2_hi = sem("x2_hi")
        x2_done = sem("x2_done")
        moment_done = sem("moment_done")
        loss_step = sem("loss_step")
        loss_sum = sem("loss_sum")
        idx_ready = sem("idx_ready")
        small_in = sem("small_in")
        convb_in = sem("convb_in")
        down_hi = sem("down_hi")
        down_ready = sem("down_ready")
        aug_hi = sem("aug_hi")
        aug_ready = sem("aug_ready")
        aug_zero = sem("aug_zero")
        hdown_done = sem("hdown_done")
        hlow_ready = sem("hlow_ready")
        h_step = sem("h_step")
        hT_hi = sem("hT_hi")
        hT_ready = sem("hT_ready")
        pc_hi = sem("pc_hi")
        pc_ready = sem("pc_ready")
        y_done = sem("y_done")
        y_ready = sem("y_ready")
        stored = sem("stored")

        block = ctx.enter_context(nc.Block())

        @block.sync
        def _(sp):
            def load_weights(slot, use, src):
                sp.wait_ge(lo_ready[slot], use + 1)
                sp.dma_start(raw[slot][:], src).then_inc(w_in[slot], 16)

            sp.dma_start(x_rows, x.rearrange("(t p) d -> p t d", p=P)).then_inc(x_in, 16)
            sp.dma_start(cst[:], consts).then_inc(const_in, 16)
            sp.dma_start(erow_i, edge_rows).then_inc(edges_in, 16)
            sp.dma_start(ecol_i, edge_cols).then_inc(edges_in, 16)
            sp.dma_start(bias[:], bias_cols).then_inc(const_in, 16)
            sp.dma_start(ew[:], edge_weights.partition_broadcast(P)).then_inc(const_in, 16)
            sp.dma_start(disc_in[:], disc).then_inc(const_in, 16)
            for m in range(6):
                with sp.Fori(0, KB // 2) as i:
                    for s in range(2):
                        load_weights(s, A_BASE[m] + i, weights[ds(i * 2 + (8 * m + s), 1)]
                                     .rearrange("a p n -> (a p) n"))
                        sp.wait_ge(key_out, 16)
                        sp.wait_ge(xt_done, KB)
                        sp.wait_ge(live_ready, i * 2 + (8 * m + s + 1))
                        sp.dma_start(key_row[:, s, :],
                                     key_dram[ds(i * 4 + (16 * m + 2 * s), 2), :]
                                     .rearrange("c e -> (c e)").partition_broadcast(P)
                                     ).then_inc(key_in[s], 16)
            with sp.Fori(0, KB) as j:
                sp.wait_ge(v_turned, j + 1)
                sp.wait_ge(evac_done, 48 + 2)
                sp.dma_start(v_cur, V2[:, ds(j, 1), :].rearrange("p a n -> p (a n)")).then_inc(v_in, 16)
                for t in range(3):
                    load_weights(t, B_BASE[t] + j, weights[ds(j + (48 + 8 * t), 1)]
                                 .rearrange("a p n -> (a p) n"))
            with sp.Fori(0, 2) as half:
                for b in range(8):
                    load_weights(b % 2, half * 4 + (C_BASE + b // 2),
                                 weights[ds(half * 8 + (72 + b), 1)].rearrange("a p n -> (a p) n"))
            with sp.Fori(0, 2) as half:
                for b in range(4):
                    load_weights(b % 2, half * 2 + (E_BASE + b // 2),
                                 weights[ds(half * 4 + (88 + b), 1)].rearrange("a p n -> (a p) n"))
            sp.wait_ge(idx_ready, 1)
            expert = sp.value_load(pick_i[0:1, 0:1], min_val=0, max_val=EXPERTS - 1)
            sp.dma_start(raw_down, down[ds(expert, 1)].rearrange("a p k r -> (a p) k r")).then_inc(small_in, 16)
            sp.dma_start(raw_up, upT[ds(expert, 1)].rearrange("a p k r -> (a p) k r")).then_inc(small_in, 16)
            sp.dma_start(raw_upb, up_b[ds(expert, 1)].rearrange("a p k -> (a p) k")).then_inc(small_in, 16)
            sp.dma_start(raw_downb[0:R, :], down_b[ds(expert, 1)].rearrange("a r o -> (a r) o")).then_inc(small_in, 16)
            sp.dma_start(conv_row, conv_b[ds(expert, 1)].rearrange("a d -> (a d)").partition_broadcast(P)
                         ).then_inc(convb_in, 16)
            for half in range(2):
                for b in range(4):
                    load_weights(b % 2, V_BASE + half * 2 + b // 2,
                                 conv[ds(expert * 8 + (half * 4 + b), 1)].rearrange("a p n -> (a p) n"))
            for t in range(NT):
                sp.wait_ge(y_ready, 2 * t + 2)
                sp.dma_start(out[t * P:(t + 1) * P, :], x_rows[:, t, :]).then_inc(stored, 16)
            sp.wait_ge(stored, 16 * NT)

        @block.gpsimd
        def _(pool):
            def split_lo(slot, use):
                pool.wait_ge(hi_ready[slot], use + 1)
                pool.tensor_tensor(w_lo[slot][:], raw[slot][:], w_hi[slot][:].bitcast(F32),
                                   ALU.subtract).then_inc(lo_ready[slot], 1)

            given = [(lo_ready[s], 1) for s in range(SLOTS)] + [(w_used[s], 1) for s in range(SLOTS)] + [
                (live_ready, 2), (evac_done, 2), (hot_used, 2), (v_turned, 1), (score_read, 1),
                (mixv_ready, 1), (mix_ready, 1), (o_summed, 1)]
            for n, (s, k) in enumerate(given):
                pool.memset(tiny[:, n:n + 1], 0.0).then_inc(s, k)
            pool.wait_ge(key_calc, 1)
            pool.dma_start(key_dram, erow[:, 0:P]).then_inc(key_out, 16)
            split_lo(0, 0)
            for m in range(6):
                with pool.Fori(0, KB // 2) as i:
                    split_lo(1, A_BASE[m] + i)
                    split_lo(0, A_BASE[m] + i + 1)
            with pool.Fori(0, KB) as j:
                pool.wait_ge(qk_hi, j * 3 + 1)
                q_j = Q2[:, ds(j, 1), :].rearrange("p a n -> p (a n)")
                pool.tensor_tensor(ql[:], q_j, qh[:].bitcast(F32), ALU.subtract).then_inc(ql_ready, 1)
                split_lo(1, B_BASE[1] + j)
                split_lo(2, B_BASE[2] + j)
                pool.wait_ge(feat_hi, j + 1)
                pool.tensor_tensor(feat[1][:], sq_q, feat[0][:].bitcast(F32),
                                   ALU.subtract).then_inc(feat_ready, 1)
                split_lo(0, B_BASE[0] + j + 1)
            pool.wait_ge(ql_ready, KB)
            pool.dma_start(row_bo, rows.partition_broadcast(P)).then_inc(rows_in, 16)
            pool.wait_ge(ol_ready, KB)
            pool.wait_ge(ml_ready, KB)
            pool.dma_start(x_rows, x.rearrange("(t p) d -> p t d", p=P)).then_inc(xr_in, 16)
            with pool.Fori(0, 2) as half:
                for b in range(1, 9):
                    split_lo(b % 2, half * 4 + (C_BASE + b // 2))
            with pool.Fori(0, 2) as half:
                for b in range(1, 4):
                    split_lo(b % 2, half * 2 + (E_BASE + b // 2))
                split_lo(0, half * 2 + (E_BASE + 2))
            for b in range(1, 8):
                split_lo(b % 2, V_BASE + b // 2)

        @block.scalar
        def _(act):
            def split_hi(slot, use):
                act.wait_ge(w_in[slot], use * 16 + 16)
                act.wait_ge(w_used[slot], use + 1)
                act.activation(w_hi[slot][:], raw[slot][:], ACT.Copy).then_inc(hi_ready[slot], 1)

            def guess_rstd(which):
                act.wait_ge(norm_step, 14 * which + 10)
                act.activation(rstd[:, 1, :], rstd[:, 0, :], ACT.Ln).then_inc(rstd_guess, 1)
                act.wait_ge(rstd_guess, 2 * which + 1)
                act.activation(rstd[:, 1, :], rstd[:, 1, :], ACT.Exp, scale=-0.5).then_inc(rstd_guess, 1)

            act.wait_ge(prep, 3)
            act.activation(ew_t[:, 0:4], ew_t[:, 0:4], ACT.Exp).then_inc(aprep, 1)
            act.wait_ge(aprep, 1)
            act.activation(ew_t[:, 0:4], ew_t[:, 0:4], ACT.Ln, bias=1.0).then_inc(aprep, 1)
            act.wait_ge(const_in, 64)
            act.activation(head_ones[:], cst[:, C_ONES:C_ONES + P], ACT.Copy).then_inc(aprep, 1)
            split_hi(0, 0)
            guess_rstd(0)
            for k in range(KB):
                act.wait_ge(xt_turned, k + 1)
                act.activation(xT[0][:, k, :], PS[:, 2 + k % 4, 0:N], ACT.Copy).then_inc(xt_hi, 1)

            def table_out(dst, done):
                for t in range(NT):
                    last = act.activation(dst[:, t, :], PS[:, 2 + t, 0:N], ACT.Copy)
                last.then_inc(done, 1)

            for m in range(6):
                dst = {0: T0, 1: T1, 3: T0}.get(m)
                with act.Fori(0, KB // 2) as i:
                    for s in range(2):
                        split_hi(1 - s, A_BASE[m] + i + s)
                        if dst:
                            act.wait_ge(w_used[s], A_BASE[m] + i + 2)
                            act.activation(dst[0][:, ds(i * 2 + s, 1), :].rearrange("p a n -> p (a n)"),
                                           PS[:, s, 0:N], ACT.Identity,
                                           bias=bias[:, ds(i * 2 + (8 * m + s), 1)]).then_inc(evac_hi, 1)
                if m == 2:
                    act.wait_ge(table_done, 1)
                    table_out(mask, table1_read)
            act.wait_ge(table_done, 2)
            table_out(table2, table2_read)

            with act.Fori(0, KB) as j:
                act.wait_ge(evac_done, 2 + 48)
                act.wait_ge(score_read, j * 6 + 1)
                act.activation(qh[:], Q2[:, ds(j, 1), :].rearrange("p a n -> p (a n)"), ACT.Copy).then_inc(qk_hi, 1)
                for h in range(2):
                    r = slice(64 * h, 64 * h + 64)
                    act.activation(kzh[h][r, :], K2[r, ds(j, 1), :].rearrange("p a n -> p (a n)"),
                                   ACT.Copy).then_inc(qk_hi, 1)
                split_hi(1, B_BASE[1] + j)
                act.wait_ge(w_used[0], B_BASE[0] + j + 2)
                act.activation(sq_q, PS[:, 0, 0:N], ACT.Square, bias=bias[:, ds(j + 6 * KB, 1)]).then_inc(sq_done, 1)
                act.wait_ge(v_turned, j + 2)
                act.activation(vs[:, :, :, 0:HD], PS[:, 7, 0:N].rearrange("p (t h d) -> p t h d", t=NT, h=2),
                               ACT.Copy).then_inc(vh_ready, 1)
                for h in range(2):
                    act.wait_ge(nmax_ready, j * 2 + (h + 1))
                    for t in range(NT):
                        act.activation(prob[:, h, t, :], prob[:, h, t, :], ACT.Exp, bias=nmax[:, h, t:t + 1],
                                       scale=SCALE, accum_out=ssum[:, h, t:t + 1]).then_inc(exp_done, 1)
                    if h == 0:
                        split_hi(2, B_BASE[2] + j)
                act.wait_ge(w_used[1], B_BASE[1] + j + 2)
                act.activation(sq_k, PS[:, 1, 0:N], ACT.Square, bias=bias[:, ds(j + 7 * KB, 1)]).then_inc(sq_done, 1)

                def turned_hi(h):
                    for t in range(NT):
                        act.wait_ge(prob_turned, j * 6 + (3 * h + t + 1))
                        act.wait_ge(pv_done, j * 2 + h)  if h else None
                        act.activation(probT[0][:, t, :], PS[:, 5 + t % 2 if t < 2 else 4, 0:N],
                                       ACT.Copy).then_inc(pT_hi, 1)

                turned_hi(0)
                act.wait_ge(sq_summed, j + 1)
                act.activation(sq_q, sq_q, ACT.Exp, scale=-0.5).then_inc(feat_exp, 1)
                act.wait_ge(feat_exp, j + 1)
                act.activation(feat[0][:], sq_q, ACT.Copy).then_inc(feat_hi, 1)
                split_hi(0, B_BASE[0] + j + 1)

                def pv_copy(h):
                    act.wait_ge(pv_done, j * 2 + (h + 1))
                    rows_in_psum = slice(64 * (1 - h), 64 * (1 - h) + 64)
                    act.activation(pv_low[64 * h:64 * h + 64, :], PS[rows_in_psum, 7, 0:N],
                                   ACT.Copy).then_inc(pv_copied, 1)

                pv_copy(0)
                turned_hi(1)
                act.wait_ge(w_used[2], B_BASE[2] + j + 2)
                act.activation(mix_v, PS[:, 0, 0:N], ACT.Identity, bias=bias[:, ds(j + 8 * KB, 1)]).then_inc(mixv_ready, 1)
                act.wait_ge(mix_ready, j + 2)
                act.activation(T1[0][:, ds(j, 1), :].rearrange("p a n -> p (a n)"), mix_v, ACT.Copy).then_inc(mh_ready, 1)
                pv_copy(1)
                act.wait_ge(o_summed, j * 2 + 3)
                act.activation(T0[0][:, ds(j, 1), :].rearrange("p a n -> p (a n)"), attn_o, ACT.Copy).then_inc(oh_ready, 1)

            with act.Fori(0, 2) as half:
                for b in range(1, 9):
                    split_hi(b % 2, half * 4 + (C_BASE + b // 2))
            guess_rstd(1)
            for k in range(KB):
                act.wait_ge(x2_turned, k + 1)
                act.activation(xT[0][:, k, :], PS[:, k % 4, 0:N], ACT.Copy,
                               accum_out=moments[:, 0, k:k + 1]).then_inc(x2_hi, 1)
                if k:
                    act.wait_ge(moment_done, k)
                act.activation(sq_junk, PS[:, k % 4, 0:N], ACT.Square,
                               accum_out=moments[:, 1, k:k + 1]).then_inc(moment_done, 1)
            with act.Fori(0, 2) as half:
                for b in range(1, 4):
                    split_hi(b % 2, half * 2 + (E_BASE + b // 2))
                split_hi(0, half * 2 + (E_BASE + 2))
            act.wait_ge(hdown_done, 1)
            act.activation(h_low[0:R, :], PS[R:2 * R, 6, 0:N], ACT.Copy).then_inc(hlow_ready, 1)
            split_hi(1, V_BASE)
            act.wait_ge(h_step, 2)
            act.activation(hT[0][0:R, :], h_sum[0:R, :], ACT.Copy).then_inc(hT_hi, 1)
            for b in range(2, 8):
                split_hi(b % 2, V_BASE + b // 2)
            for half in range(2):
                act.wait_ge(w_used[1], 1 + V_BASE + 2 * half + 2)
                act.activation(pc[0][:, half * HALF:(half + 1) * HALF], PS[:, 6 + half, :], ACT.Copy).then_inc(pc_hi, 1)

        @block.vector
        def _(dve):
            for h in range(2):
                z = slice(64 * (1 - h), 64 * (1 - h) + 64)
                dve.memset(kzh[h][z, :].bitcast(F32), 0.0)
                dve.memset(kzl[h][z, :].bitcast(F32), 0.0).then_inc(keys_zeroed, 1)
            dve.wait_ge(const_in, 64)
            dve.tensor_scalar(ew_t[:, 0:4], ew[:], -1.0, None, ALU.mult).then_inc(prep, 1)
            dve.wait_ge(prep, 1)
            dve.tensor_tensor(ew_t[:, 0:4], ew_t[:, 0:4], ew[:], ALU.min).then_inc(prep, 1)
            dve.tensor_scalar(ew_t[:, 4:8], ew[:], 0.0, None, ALU.max).then_inc(prep, 1)
            dve.tensor_copy(iota16[:], cst[:, C_IOTA:C_IOTA + N]).then_inc(prep, 1)
            dve.memset(zero16[:], 0.0)
            dve.memset(diag16, 0.0).then_inc(prep, 1)
            dve.tensor_scalar(diag_w, ident, 2.0 ** -96, None, ALU.mult).then_inc(prep, 1)
            dve.wait_ge(prep, 6)
            dve.tensor_copy(diag16[:, 2 * P:3 * P], ident).then_inc(prep, 1)

            def layer_norm(src, dst, done, which):
                def step(ins, wait=True):
                    normed[0] += 1
                    ins.then_inc(norm_step, 1)
                    if wait:
                        dve.wait_ge(norm_step, normed[0])

                for t in range(NT):
                    for c in range(2):
                        step(dve.bn_stats(stats[:, t, c, :], src[:, t, c * HALF:(c + 1) * HALF]), wait=c == 1)
                    step(dve.bn_aggr(mv[:, t, :], stats[:, t, :, :].rearrange("p c s -> p (c s)")), wait=t == 2)
                step(dve.tensor_scalar(rstd[:, 0, :], mv[:, :, 1], EPS, None, ALU.add))
                dve.wait_ge(rstd_guess, 2 * which + 2)
                step(dve.tensor_tensor(rstd[:, 2, :], rstd[:, 1, :], rstd[:, 1, :], ALU.mult))
                step(dve.tensor_tensor(rstd[:, 2, :], rstd[:, 2, :], rstd[:, 0, :], ALU.mult))
                step(dve.tensor_scalar(rstd[:, 2, :], rstd[:, 2, :], -0.5, 1.5, ALU.mult, ALU.add))
                step(dve.tensor_tensor(rstd[:, 2, :], rstd[:, 2, :], rstd[:, 1, :], ALU.mult))
                for t in range(NT):
                    dve.tensor_scalar(dst[:, t, :], src[:, t, :], mv[:, t, 0:1], rstd[:, 2, t:t + 1],
                                      ALU.subtract, ALU.mult).then_inc(done, 1)

            normed = [0]
            dve.wait_ge(x_in, 16)
            layer_norm(x_rows, xn_rows, xn_ready, 0)
            dve.wait_ge(edges_in, 32)
            dve.tensor_copy(erow, erow_i).then_inc(prep, 1)
            dve.tensor_copy(ecol[:], ecol_i).then_inc(prep, 1)
            dve.wait_ge(prep, 9)
            dve.scalar_tensor_tensor(out=erow[:, 0:P], in0=erow[:, 0:P], scalar=float(N), in1=erow[:, P:2 * P],
                                     op0=ALU.mult, op1=ALU.add).then_inc(key_calc, 1)
            for k in range(KB):
                dve.wait_ge(xt_hi, k + 1)
                dve.tensor_tensor(xT[1][:, k, :], PS[:, 2 + k % 4, 0:N], xT[0][:, k, :].bitcast(F32),
                                  ALU.subtract).then_inc(xt_done, 1)
            src_c, dst_c, type_c = (ecol[:, c * CH:(c + 1) * CH] for c in range(3))
            dve.scalar_tensor_tensor(out=ekey[:], in0=src_c, scalar=float(N), in1=dst_c,
                                     op0=ALU.mult, op1=ALU.add).then_inc(prep, 1)
            dve.tensor_scalar(digit[0], type_c, 1.0, 1.0, ALU.is_equal, ALU.mult).then_inc(prep, 1)
            dve.tensor_scalar(digit[1], type_c, 2.0, 2.0, ALU.is_equal, ALU.mult).then_inc(prep, 1)
            dve.tensor_scalar(digit[2], type_c, 3.0, 4.0, ALU.is_equal, ALU.mult).then_inc(prep, 1)
            dve.tensor_scalar(digit[3], type_c, 4.0, 8.0, ALU.is_ge, ALU.mult).then_inc(prep, 1)
            dve.tensor_scalar(digit[4], type_c, 0.0, 8.0, ALU.is_le, ALU.mult).then_inc(prep, 1)
            for c in range(1, 5):
                dve.wait_ge(prep, 14 + c)
                dve.tensor_tensor(digit[0], digit[0], digit[c], ALU.add).then_inc(prep, 1)
            dve.wait_ge(prep, 19)
            dve.tensor_tensor(digit[0], digit[0], cst[:, C_POW:C_POW + CH], ALU.mult).then_inc(prep, 1)
            mu, sg = disc_in[:, 0], disc_in[:, 1]
            dve.tensor_tensor(dterm[:, 3], sg, sg, ALU.mult).then_inc(prep, 1)
            dve.wait_ge(prep, 21)
            dve.reciprocal(dterm[:, 0], dterm[:, 3]).then_inc(prep, 1)
            dve.wait_ge(prep, 22)
            dve.tensor_tensor(dterm[:, 1], dterm[:, 0], mu, ALU.mult).then_inc(prep, 1)
            dve.wait_ge(prep, 23)
            dve.tensor_tensor(dterm[:, 2], dterm[:, 1], mu, ALU.mult).then_inc(prep, 1)
            dve.wait_ge(aprep, 2)
            dve.tensor_tensor(ew[:], ew_t[:, 0:4], ew_t[:, 4:8], ALU.add).then_inc(prep, 1)
            dve.wait_ge(prep, 25)
            dve.tensor_scalar(ew[:], ew[:], 1.0 / SCALE, None, ALU.mult).then_inc(prep, 1)

            dve.wait_ge(prep, 26)
            for m in range(6):
                dst = {0: T0, 1: T1, 2: Q2, 3: T0, 4: K2, 5: V2}[m]
                splits_before = {0: 0, 1: 8, 3: 16}.get(m)
                with dve.Fori(0, KB // 2) as i:
                    for s in range(2):
                        job = i * 2 + (8 * m + s)
                        dve.wait_ge(key_in[s], i * 16 + (64 * m + 16))
                        for c in range(2):
                            ch = i * 4 + (16 * m + 2 * s + c)
                            if c:
                                dve.wait_ge(dup_ready, job * 2 + 1)
                            last = dve.scalar_tensor_tensor(
                                out=key_junk, in0=key_row[:, s, c * P:(c + 1) * P], scalar=ekey[:, ds(ch, 1)],
                                in1=tri, op0=ALU.is_equal, op1=ALU.mult, accum_out=dup[:, ds(ch, 1)])
                            last.then_inc(dup_ready, 1)
                        dve.wait_ge(dup_ready, job * 2 + 2)
                        two = ds(i * 4 + (16 * m + 2 * s), 2)
                        dve.scalar_tensor_tensor(out=live_w[:, two], in0=dup[:, two], scalar=0.0,
                                                 in1=etype[:, two], op0=ALU.is_equal,
                                                 op1=ALU.mult).then_inc(live_ready, 1)
                        dve.wait_ge(hot_used, job + 1)
                        for c in range(2):
                            ch = i * 4 + (16 * m + 2 * s + c)
                            dve.tensor_scalar(dst_hot[:, s, c, :], iota16[:], ecol[:, ds(ch + CH, 1)], None,
                                              ALU.is_equal).then_inc(hot_ready, 1)
                        dve.wait_ge(live_ready, job + 3)
                        for c in range(2):
                            ch = i * 4 + (16 * m + 2 * s + c)
                            last = dve.tensor_scalar(src_hot[:, s, c, :], iota16[:], ecol[:, ds(ch, 1)],
                                                     live_w[:, ds(ch, 1)], ALU.is_equal, ALU.mult)
                            last.then_inc(hot_ready, 1)
                        if splits_before is not None:
                            dve.wait_ge(evac_hi, i * 2 + (splits_before + s + 1))
                            j1 = ds(i * 2 + s, 1)
                            dve.scalar_tensor_tensor(
                                out=dst[1][:, j1, :].rearrange("p a n -> p (a n)"), in0=PS[:, s, 0:N],
                                scalar=bias[:, ds(job, 1)],
                                in1=dst[0][:, j1, :].rearrange("p a n -> p (a n)").bitcast(F32),
                                op0=ALU.add, op1=ALU.subtract).then_inc(evac_done, 1)
                        else:
                            dve.wait_ge(w_used[s], A_BASE[m] + i + 2)
                            dve.tensor_scalar(dst[:, ds(i * 2 + s, 1), :].rearrange("p a n -> p (a n)"),
                                              PS[:, s, 0:N], bias[:, ds(job, 1)], None,
                                              ALU.add).then_inc(evac_done, 1)
            dve.wait_ge(table2_read, 1)
            dve.wait_ge(table1_read, 1)
            step = [0]

            def masked(ins):
                step[0] += 1
                ins.then_inc(mask_step, 1)
                dve.wait_ge(mask_step, step[0])

            for t in range(NT):
                last = dve.copy_predicated(mask[:, t, :], PS[:, 2 + t, 0:N].bitcast(U32), table2[:, t, :])
            masked(last)
            masked(dve.tensor_scalar(codes.bitcast(I32), mask[:].bitcast(I32), 23, 3,
                                     ALU.logical_shift_right, ALU.bitwise_and))
            masked(dve.tensor_scalar(mask[:], mask[:], 0.0, ABSENT, ALU.is_equal, ALU.mult))
            for w in range(4):
                masked(dve.tensor_scalar(pick, codes.bitcast(I32), float(w), ew[:, w:w + 1],
                                         ALU.is_equal, ALU.mult))
                masked(dve.tensor_tensor(mask[:], mask[:], pick, ALU.add))

            with dve.Fori(0, KB) as j:
                def softmax_in(h):
                    for t in range(NT):
                        dve.wait_ge(score_done, j * 6 + (3 * h + t + 1))
                        dve.memset(tiny[:, 16 + 3 * h + t:17 + 3 * h + t], 0.0)
                        dve.tensor_tensor_reduce(prob[:, h, t, :], PS[:, 2 + t, 0:N], mask[:, t, :], 1.0,
                                                 3.0 * ABSENT, ALU.add, ALU.max,
                                                 smax[:, h, t:t + 1]).then_inc(score_read, 1)
                    dve.wait_ge(score_read, j * 6 + (3 * h + 4))
                    dve.tensor_scalar(nmax[:, h, :], smax[:, h, :], -SCALE, None, ALU.mult).then_inc(nmax_ready, 1)

                def normalise(h):
                    dve.wait_ge(exp_done, j * 6 + (3 * h + 3))
                    dve.reciprocal(rsum[:, h, :], ssum[:, h, :]).then_inc(recip_done, 1)
                    dve.wait_ge(recip_done, j * 2 + (h + 1))
                    for t in range(NT):
                        dve.tensor_scalar(prob[:, h, t, :], prob[:, h, t, :], rsum[:, h, t:t + 1], None,
                                          ALU.mult).then_inc(prob_ready, 1)

                def turned_lo(h):
                    for t in range(NT):
                        dve.wait_ge(pT_hi, j * 6 + (3 * h + t + 1))
                        dve.tensor_tensor(probT[1][:, t, :], PS[:, 5 + t % 2 if t < 2 else 4, 0:N],
                                          probT[0][:, t, :].bitcast(F32), ALU.subtract).then_inc(pT_ready, 1)

                def pv_sum(h):
                    r = slice(64 * h, 64 * h + 64)
                    dve.wait_ge(pv_copied, j * 2 + (h + 1))
                    dve.tensor_tensor(attn_o[r, :], PS[r, 7, 0:N], pv_low[r, :], ALU.add).then_inc(o_summed, 1)

                for h in range(2):
                    r = slice(64 * h, 64 * h + 64)
                    dve.wait_ge(qk_hi, j * 3 + (h + 2))
                    dve.tensor_tensor(kzl[h][r, :], K2[r, ds(j, 1), :].rearrange("p a n -> p (a n)"),
                                      kzh[h][r, :].bitcast(F32), ALU.subtract).then_inc(kl_ready, 1)
                dve.wait_ge(vh_ready, j + 1)
                dve.tensor_tensor(vs[:, :, :, HD:P], PS[:, 7, 0:N].rearrange("p (t h d) -> p t h d", t=NT, h=2),
                                  vs[:, :, :, 0:HD].bitcast(F32), ALU.subtract).then_inc(vs_ready, 1)
                softmax_in(0)
                softmax_in(1)
                normalise(0)
                normalise(1)
                dve.wait_ge(sq_done, j * 2 + 2)
                dve.tensor_tensor(sq_q, sq_q, sq_k, ALU.add).then_inc(sq_summed, 1)
                turned_lo(0)
                pv_sum(0)
                turned_lo(1)
                dve.wait_ge(coeff_done, j + 1)
                dve.wait_ge(mixv_ready, j + 2)
                dve.tensor_tensor(mix_v, PS[:, 2, 0:N], mix_v, ALU.mult).then_inc(mix_ready, 1)
                dve.wait_ge(mh_ready, j + 1)
                j1 = ds(j, 1)
                dve.tensor_tensor(T1[1][:, j1, :].rearrange("p a n -> p (a n)"), mix_v,
                                  T1[0][:, j1, :].rearrange("p a n -> p (a n)").bitcast(F32),
                                  ALU.subtract).then_inc(ml_ready, 1)
                pv_sum(1)
                dve.wait_ge(oh_ready, j + 1)
                dve.tensor_tensor(T0[1][:, j1, :].rearrange("p a n -> p (a n)"), attn_o,
                                  T0[0][:, j1, :].rearrange("p a n -> p (a n)").bitcast(F32),
                                  ALU.subtract).then_inc(ol_ready, 1)

            dve.wait_ge(rows_in, 16)
            dve.wait_ge(xr_in, 16)
            for r in range(2):
                if r:
                    dve.wait_ge(res_ready, NT)
                for t in range(NT):
                    dve.tensor_tensor(x_rows[:, t, :], x_rows[:, t, :], row_bo[:, r, :], ALU.add).then_inc(res_ready, 1)
            dve.wait_ge(res_ready, 2 * NT)
            for half in range(2):
                dve.wait_ge(w_used[1], 1 + C_BASE + 4 * half + 4)
                c = slice(half * HALF, (half + 1) * HALF)
                for t in range(NT):
                    dve.tensor_tensor(x_rows[:, t, c], PS[:, 3 * half + t, :], x_rows[:, t, c],
                                      ALU.add).then_inc(x2_ready, 1)
            dve.wait_ge(x2_ready, 2 * NT)
            layer_norm(x_rows, xn_rows, x2n_ready, 1)
            for k in range(KB):
                dve.wait_ge(moment_done, k + 1)
                dve.tensor_tensor(xT[1][:, k, :], PS[:, k % 4, 0:N], xT[0][:, k, :].bitcast(F32),
                                  ALU.subtract).then_inc(x2_done, 1)
            ls = [0]

            def lstep(ins):
                ls[0] += 1
                ins.then_inc(loss_step, 1)
                dve.wait_ge(loss_step, ls[0])

            dve.wait_ge(moment_done, KB)
            lstep(dve.tensor_scalar(moments[:, 2, :], moments[:, 1, :], 1.0 / N, None, ALU.mult))
            lstep(dve.tensor_scalar(moments[:, 3, :], moments[:, 0, :], -2.0 / N, None, ALU.mult))
            m2 = moments[:, 2:3, :].broadcast_to([P, EXPERTS, KB])
            m1 = moments[:, 3:4, :].broadcast_to([P, EXPERTS, KB])
            lstep(dve.tensor_tensor(dterm[:, 3], dterm[:, 0], m2, ALU.mult))
            lstep(dve.tensor_tensor(dterm[:, 4], dterm[:, 1], m1, ALU.mult))
            lstep(dve.tensor_tensor(dterm[:, 3], dterm[:, 3], dterm[:, 4], ALU.add))
            lstep(dve.tensor_tensor(dterm[:, 3], dterm[:, 3], dterm[:, 2], ALU.add))
            lstep(dve.tensor_reduce(loss[:, 0, :], dterm[:, 3], X, ALU.add))
            dve.wait_ge(loss_sum, 1)
            lstep(dve.tensor_copy(loss[:, 1, :], PS[:, 7, 0:EXPERTS]))
            lstep(dve.tensor_reduce(loss[:, 2, 0:1], loss[:, 1, :], X, ALU.min))
            lstep(dve.tensor_scalar(loss[:, 3, :], loss[:, 1, :], loss[:, 2, 0:1], 100.0, ALU.is_gt, ALU.mult))
            lstep(dve.tensor_tensor(loss[:, 3, :], loss[:, 3, :], eidx, ALU.add))
            lstep(dve.tensor_reduce(loss[:, 4, 0:1], loss[:, 3, :], X, ALU.min))
            lstep(dve.tensor_scalar(loss[:, 4, 0:1], loss[:, 4, 0:1], float(EXPERTS - 1), None, ALU.min))
            dve.tensor_copy(pick_i[:], loss[:, 4, 0:1]).then_inc(idx_ready, 1)
            for t in range(NT):
                dve.tensor_tensor(x_rows[:, t, :], x_rows[:, t, :], row_bo[:, 2, :], ALU.add).then_inc(res_ready, 1)
            dve.memset(t0l[:, 0:2 * D].bitcast(F32), 0.0).then_inc(aug_zero, 1)
            dve.memset(hT[0][R:P, :].bitcast(F32), 0.0)
            dve.memset(hT[1][R:P, :].bitcast(F32), 0.0).then_inc(aug_zero, 1)
            dve.wait_ge(aug_zero, 2)
            dve.memset(hT[0][R:R + 1, :].bitcast(F32), 1.0).then_inc(aug_zero, 1)
            dve.wait_ge(small_in, 64)
            dve.tensor_copy(wd[:, :, 0:R], raw_down).then_inc(down_hi, 1)
            dve.tensor_copy(aug[0][:, :, 0:R], raw_up).then_inc(aug_hi, 1)
            dve.tensor_copy(aug[0][:, :, R:R + 1], raw_upb.unsqueeze(2)).then_inc(aug_hi, 1)
            dve.wait_ge(down_hi, 1)
            dve.tensor_tensor(wd[:, :, R:P], raw_down, wd[:, :, 0:R].bitcast(F32), ALU.subtract).then_inc(down_ready, 1)
            dve.wait_ge(aug_hi, 2)
            dve.tensor_tensor(aug[1][:, :, 0:R], raw_up, aug[0][:, :, 0:R].bitcast(F32), ALU.subtract).then_inc(aug_ready, 1)
            dve.tensor_tensor(aug[1][:, :, R:R + 1], raw_upb.unsqueeze(2), aug[0][:, :, R:R + 1].bitcast(F32),
                              ALU.subtract).then_inc(aug_ready, 1)
            dve.wait_ge(convb_in, 16)
            dve.wait_ge(res_ready, 3 * NT)
            for t in range(NT):
                dve.tensor_tensor(x_rows[:, t, :], x_rows[:, t, :], conv_row, ALU.add).then_inc(res_ready, 1)
            dve.wait_ge(hlow_ready, 1)
            dve.tensor_tensor(h_sum[0:R, :], PS[0:R, 6, 0:N], h_low[0:R, :], ALU.add).then_inc(h_step, 1)
            dve.wait_ge(h_step, 1)
            dve.tensor_scalar(h_sum[0:R, :], h_sum[0:R, :], raw_downb[0:R, :], 0.0, ALU.add, ALU.max).then_inc(h_step, 1)
            dve.wait_ge(hT_hi, 1)
            dve.tensor_tensor(hT[1][0:R, :], h_sum[0:R, :], hT[0][0:R, :].bitcast(F32), ALU.subtract).then_inc(hT_ready, 1)
            for half in range(2):
                c = slice(half * HALF, (half + 1) * HALF)
                dve.wait_ge(pc_hi, half + 1)
                dve.tensor_tensor(pc[1][:, c], PS[:, 6 + half, :], pc[0][:, c].bitcast(F32), ALU.subtract).then_inc(pc_ready, 1)
            dve.wait_ge(res_ready, 4 * NT)
            for t in range(NT):
                for half in range(2):
                    c = slice(half * HALF, (half + 1) * HALF)
                    dve.wait_ge(y_done, 2 * t + half + 1)
                    dve.tensor_tensor(x_rows[:, t, c], PS[:, 3 * half + t, :], x_rows[:, t, c],
                                      ALU.add).then_inc(y_ready, 1)

        @block.tensor
        def _(pe):
            def turn(rows_tile, first_bank, ready, turned, freed):
                for k in range(KB):
                    if k >= 4:
                        for f in freed:
                            pe.wait_ge(f, k - 3)
                    for t in range(NT):
                        if k == 0:
                            pe.wait_ge(ready, t + 1)
                        last = pe.transpose(PS[:, first_bank + k % 4, t * P:(t + 1) * P],
                                            rows_tile[:, t, k * P:(k + 1) * P], ident)
                    last.then_inc(turned, 1)

            def column_job(slot, use, src, bank, ks=range(KB)):
                o = PS[:, bank, 0:N]
                pe.wait_ge(hi_ready[slot], use + 1)
                for k in ks:
                    wh = w_hi[slot][:, k * P:(k + 1) * P]
                    pe.matmul(o, wh, src[0][:, k, :], start=(k == 0), stop=False)
                    pe.matmul(o, wh, src[1][:, k, :], start=False, stop=False)
                pe.wait_ge(lo_ready[slot], use + 2)
                for k in ks:
                    wl = w_lo[slot][:, k * P:(k + 1) * P]
                    last = pe.matmul(o, wl, src[0][:, k, :], start=False, stop=(k == KB - 1))
                if ks[-1] == KB - 1:
                    last.then_inc(w_used[slot], 1)

            def row_block(slot, use, src, half, kp, first, final):
                def go(part, weights_in, is_first, is_last):
                    for k2 in range(2):
                        for t in range(NT):
                            lhs = src[part][:, 2 * kp + k2, t * P:(t + 1) * P]
                            rhs = weights_in[slot][:, k2 * HALF:(k2 + 1) * HALF]
                            bank = PS[:, ds(half * 3 + t, 1), :].rearrange("p a n -> p (a n)")
                            last = pe.matmul(bank, lhs, rhs, start=is_first and k2 == 0,
                                             stop=is_last and k2 == 1)
                    return last
                pe.wait_ge(hi_ready[slot], use + 1)
                go(0, w_hi, first, False)
                go(1, w_hi, False, False)
                pe.wait_ge(lo_ready[slot], use + 2)
                go(0, w_lo, False, final).then_inc(w_used[slot], 1)

            pe.wait_ge(const_in, 64)
            turn(xn_rows, 2, xn_ready, xt_turned, [xt_done])

            pe.wait_ge(xt_done, KB)
            for m in range(6):
                src = [xT, xT, T0, xT, T1, T0][m]
                if m == 0:
                    pe.wait_ge(prep, 7)
                    for t in range(NT):
                        pe.matmul(PS[:, 2 + t, 0:N], diag_w, diag16[:, (2 - t) * P:(5 - t) * P],
                                  start=True, stop=False)
                if m == 3:
                    pe.wait_ge(table1_read, 1)
                    for t in range(NT):
                        pe.matmul(PS[:, 2 + t, 0:N], diag16[:, 0:P], diag16[:, 0:N], start=True, stop=False)
                with pe.Fori(0, KB // 2) as i:
                    for s in range(2):
                        job = i * 2 + (8 * m + s)
                        pe.wait_ge(evac_done, job + 1)
                        column_job(s, A_BASE[m] + i, src, s)
                        pe.wait_ge(hot_ready, job * 4 + 4)
                        for c in range(2):
                            for t in range(NT):
                                last = pe.matmul(PS[:, 2 + t, 0:N], src_hot[:, s, c, t * P:(t + 1) * P],
                                                 dst_hot[:, s, c, :], start=False, stop=False)
                        last.then_inc(hot_used, 1)
                if m in (2, 5):
                    for t in range(NT):
                        last = pe.matmul(PS[:, 2 + t, 0:N], zero16[:], dst_hot[:, 1, 1, :], start=False,
                                         stop=True)
                    last.then_inc(table_done, 1)

            pe.wait_ge(keys_zeroed, 2)
            pe.wait_ge(aprep, 3)
            pe.wait_ge(evac_done, 2 + 48)
            with pe.Fori(0, KB) as j:
                pe.wait_ge(mixv_ready, j + 1)
                column_job(0, B_BASE[0] + j, xT, 0)
                pe.wait_ge(v_in, j * 16 + 16)
                pe.wait_ge(o_summed, j * 2 + 1)
                for t in range(NT):
                    last = pe.transpose(PS[:, 7, t * P:(t + 1) * P], v_cur[:, t * P:(t + 1) * P], ident)
                last.then_inc(v_turned, 1)
                pe.wait_ge(ql_ready, j + 1)
                pe.wait_ge(kl_ready, j * 2 + 2)
                pe.wait_ge(mask_step, 1)
                pe.wait_ge(mix_ready, j + 1)
                for h in range(2):
                    for t in range(NT):
                        pe.wait_ge(score_read, j * 6 + (1 + (t + 1 if h else 0)))
                        r = slice(t * P, (t + 1) * P)
                        pe.matmul(PS[:, 2 + t, 0:N], qh[:, r], kzh[h][:], start=True, stop=False)
                        pe.matmul(PS[:, 2 + t, 0:N], ql[:, r], kzh[h][:], start=False, stop=False)
                        pe.matmul(PS[:, 2 + t, 0:N], qh[:, r], kzl[h][:], start=False,
                                  stop=True).then_inc(score_done, 1)
                column_job(1, B_BASE[1] + j, xT, 1)

                def turn_probs(h):
                    pe.wait_ge(prob_ready, j * 6 + (3 * h + 3))
                    for m in range(NT):
                        bank = 5 + m % 2 if m < 2 else 4
                        if h:
                            pe.wait_ge(pT_ready, j * 6 + (m + 1))
                        for t in range(NT):
                            last = pe.transpose(PS[:, bank, t * P:(t + 1) * P],
                                                prob[:, h, t, m * P:(m + 1) * P], ident)
                        last.then_inc(prob_turned, 1)

                def pv(h):
                    pe.wait_ge(pT_ready, j * 6 + (3 * h + 3))
                    for m in range(NT):
                        for part in range(2):
                            last = pe.matmul(PS[:, 7, 0:N], vs[:, m, h, :], probT[part][:, m, :],
                                             start=(m == 0 and part == 0), stop=(m == NT - 1 and part == 1))
                    last.then_inc(pv_done, 1)

                pe.wait_ge(score_read, j * 6 + 7)
                turn_probs(0)
                pe.wait_ge(sq_done, j * 2 + 1)
                column_job(2, B_BASE[2] + j, xT, 0, range(0, KB // 2))
                pe.wait_ge(vs_ready, j + 1)
                pv(0)
                pe.wait_ge(feat_ready, j + 1)
                pe.matmul(PS[:, 2, 0:N], head_ones[:], feat[0][:], start=True, stop=False)
                pe.matmul(PS[:, 2, 0:N], head_ones[:], feat[1][:], start=False, stop=True).then_inc(coeff_done, 1)
                turn_probs(1)
                column_job(2, B_BASE[2] + j, xT, 0, range(KB // 2, KB))
                pe.wait_ge(o_summed, j * 2 + 2)
                pv(1)

            pe.wait_ge(ol_ready, KB)
            pe.wait_ge(ml_ready, KB)
            with pe.Fori(0, 2) as half:
                for b in range(8):
                    row_block(b % 2, half * 4 + (C_BASE + b // 2), T0 if b < 4 else T1, half, b % 4,
                              b == 0, b == 7)
            turn(xn_rows, 0, x2n_ready, x2_turned, [x2_done])
            pe.wait_ge(x2_done, KB)
            pe.wait_ge(loss_step, 7)
            pe.matmul(PS[:, 7, 0:EXPERTS], ones_f32, loss[:, 0, :], start=True, stop=True).then_inc(loss_sum, 1)
            with pe.Fori(0, 2) as half:
                for b in range(4):
                    row_block(b % 2, half * 2 + (E_BASE + b // 2), xT, half, b, b == 0, False)
            pe.wait_ge(down_ready, 1)
            for k in range(KB):
                for part in range(2):
                    last = pe.matmul(PS[:, 6, 0:N], wd[:, k, :], xT[part][:, k, :],
                                     start=(k == 0 and part == 0), stop=(k == KB - 1 and part == 1))
            last.then_inc(hdown_done, 1)
            pe.wait_ge(aug_ready, 2)
            pe.wait_ge(h_step, 1)
            for half in range(2):
                o = PS[:, 6 + half, :]
                for b in range(4):
                    s, use = b % 2, V_BASE + half * 2 + b // 2
                    pe.wait_ge(hi_ready[s], use + 1)
                    for k2 in range(2):
                        for part in range(2):
                            pe.matmul(o, aug[part][:, 2 * b + k2, :], w_hi[s][:, k2 * HALF:(k2 + 1) * HALF],
                                      start=(b == 0 and k2 == 0 and part == 0), stop=False)
                    pe.wait_ge(lo_ready[s], use + 2)
                    for k2 in range(2):
                        last = pe.matmul(o, aug[0][:, 2 * b + k2, :], w_lo[s][:, k2 * HALF:(k2 + 1) * HALF],
                                         start=False, stop=(b == 3 and k2 == 1))
                    last.then_inc(w_used[s], 1)
            pe.wait_ge(hT_ready, 1)
            pe.wait_ge(aug_zero, 3)
            pe.wait_ge(pc_ready, 2)
            for t in range(NT):
                r = slice(t * P, (t + 1) * P)
                for half in range(2):
                    c = slice(half * HALF, (half + 1) * HALF)
                    o = PS[:, 3 * half + t, :]
                    pe.matmul(o, hT[0][:, r], pc[0][:, c], start=False, stop=False)
                    pe.matmul(o, hT[1][:, r], pc[0][:, c], start=False, stop=False)
                    pe.matmul(o, hT[0][:, r], pc[1][:, c], start=False, stop=True).then_inc(y_done, 1)


def columns(w):
    return w.reshape(KB, P, KB, P).transpose(2, 1, 0, 3).reshape(KB, P, D)


def halves(w):
    return w.reshape(4, 2, P, 2, HALF).transpose(3, 0, 2, 1, 4).reshape(8, P, D)


def kernel(**inputs):
    import numpy as np
    import concourse.bacc as bacc
    from concourse.bass_utils import run_bass_kernel_spmd

    a = {k.replace("L0_", ""): np.asarray(v) for k, v in inputs.items()}
    first = [columns(a["gnn_" + n].T) for n in ("wq", "wk", "wiq", "wv", "wik", "wiv")]
    mixer = [columns(a["mix_" + n]) for n in ("Wq", "Wk", "Wv")]
    wo, mo = halves(a["gnn_wo"].T), halves(a["mix_Wo"])
    outs = [wo[0:4], mo[0:4], wo[4:8], mo[4:8]]
    weights = np.concatenate(first + mixer + outs + [halves(a["ffn_base_W"].T)])
    conv = np.concatenate([halves(a["ffn_conv_W"][e].T) for e in range(EXPERTS)])
    names = ["gnn_bq", "gnn_bk", "gnn_biq", "gnn_bv", "gnn_bik", "gnn_biv", "mix_bq", "mix_bk", "mix_bv"]
    disc = np.stack([a["ffn_disc_mu"], a["ffn_disc_sigma"]]).reshape(2, EXPERTS, KB, P)
    edges = [a["src"], a["dst"], a["edge_type_5"]]
    lane = np.arange(P)
    consts = np.zeros((P, C_ALL), np.float32)
    consts[:, C_ID:C_ID + P] = np.eye(P)
    consts[:, C_IOTA:C_IOTA + N] = np.arange(N)
    consts[:, C_TRI:C_TRI + P] = lane[None, :] > lane[:, None]
    consts[:, C_POW:C_POW + CH] = 2.0 ** (4.0 * (np.arange(CH) % GCH) - 95)
    consts[:, C_ONES:C_ONES + P] = lane[None, :] // HD == lane[:, None] // HD
    consts[:, C_EIDX:C_EIDX + EXPERTS] = np.arange(EXPERTS)
    consts[:, C_ONE:C_ONE + P] = 1.0
    arrays = {
        "x": a["x"],
        "weights": weights,
        "conv": conv,
        "down": a["ffn_down_W"].reshape(EXPERTS, KB, P, R).transpose(0, 2, 1, 3),
        "upT": a["ffn_up_W"].reshape(EXPERTS, R, KB, P).transpose(0, 3, 2, 1),
        "up_b": a["ffn_up_b"].reshape(EXPERTS, KB, P).transpose(0, 2, 1),
        "down_b": a["ffn_down_b"].reshape(EXPERTS, R, 1),
        "conv_b": a["ffn_conv_b"],
        "disc": disc.transpose(3, 0, 1, 2),
        "bias_cols": np.concatenate([a[n].reshape(KB, P) for n in names]).T,
        "rows": np.stack([a["gnn_bo"], a["mix_bo"], a["ffn_base_b"]]),
        "edge_weights": a["gnn_edge_type_weights"],
        "edge_rows": np.concatenate([e.reshape(CH, P) for e in edges[:2]], axis=1),
        "edge_cols": np.concatenate([e.reshape(CH, P).T for e in edges], axis=1),
        "consts": consts,
    }
    arrays = {k: np.ascontiguousarray(v) for k, v in arrays.items()}
    nc = bacc.Bacc("TRN2", target_bir_lowering=False, num_devices=1)
    args = {k: nc.dram_tensor(k, v.shape, mybir.dt.from_np(v.dtype), kind="ExternalInput").ap()
            for k, v in arrays.items()}
    out = nc.dram_tensor("out", (N, D), F32, kind="ExternalOutput").ap()
    gps_layer(nc, out=out, **args)
    r = run_bass_kernel_spmd(nc, [arrays], core_ids=[0])
    return r.results[0]["out"]
```

```python
from contextlib import ExitStack

import concourse.bass as bass
from concourse import mybir

F32 = mybir.dt.float32
F32R = mybir.dt.float32r
BF16 = mybir.dt.bfloat16
F16 = mybir.dt.float16
I32 = mybir.dt.int32
U32 = mybir.dt.uint32
ALU = mybir.AluOpType
ACT = mybir.ActivationFunctionType
X = mybir.AxisListType.X
ds = bass.ds

P = 128
N = 384
D = 1024
NT = N // P
KB = D // P
HD = 64
HALF = 512
E = 12288
CH = E // P
GCH = CH // 2
CJ = 3
EXPERTS = 8
R = 64
EPS = 1e-5
SCALE = 1.0 / HD ** 0.5
ABSENT = -1e30
SLOTS = 3

A_BASE = [4 * m for m in range(6)]
B_BASE = [24, 24, 0]
C_BASE = 32
E_BASE = 40
V_USES = [(b % 3, (44, 44, 8)[b % 3] + b // 3) for b in range(8)]
TURN_BANKS = (5, 6, 4)
LN_BANKS = (6, 0, 2)

C_ID, C_IOTA, C_TRI, C_POW, C_ONES, C_EIDX, C_ONE, C_ALL = 0, 128, 512, 640, 736, 864, 872, 1000


def gps_layer(nc, x, out, weights, conv, down, upT, up_b, down_b, conv_b, disc, bias_cols,
              rows, edge_weights, edge_rows, edge_cols, consts):
    with ExitStack() as ctx:
        def sb(name, shape, dt):
            return ctx.enter_context(nc.sbuf_tensor(name, shape, dt))

        def sem(name):
            return ctx.enter_context(nc.semaphore(name))

        key_dram = nc.dram_tensor("key_dram", [CH, P], F32, kind="Internal").ap()

        raw = [sb(f"raw{s}", [P, D], F32) for s in range(SLOTS)]
        w_hi = [sb(f"w_hi{s}", [P, D], F32R) for s in range(SLOTS)]
        w_lo = [sb(f"w_lo{s}", [P, D], F32R) for s in range(SLOTS)]
        xT = [sb(f"xT_{c}", [P, KB, N], F32R) for c in ("hi", "lo")]
        T0 = [sb(f"T0_{c}", [P, KB, N], F32R) for c in ("hi", "lo")]
        T1 = [sb(f"T1_{c}", [P, KB, N], F32R) for c in ("hi", "lo")]
        Q2 = sb("Q2", [P, KB, N], F32)
        K2 = sb("K2", [P, KB, N], F32)
        V2 = sb("V2", [P, KB, N], F32)
        mask = sb("mask", [P, NT, N], F32)
        U = sb("U", [P, 6 * D], F32)
        x_rows = U[:, 0:NT * D].rearrange("p (t d) -> p t d", t=NT)
        xn_rows = U[:, NT * D:2 * NT * D].rearrange("p (t d) -> p t d", t=NT)
        src_hot = U[:, 0:CJ * N].bitcast(BF16).rearrange("p (s c n) -> p s c n", s=2, c=CJ)
        dst_hot = U[:, CJ * N:2 * CJ * N].bitcast(BF16).rearrange("p (s c n) -> p s c n", s=2, c=CJ)
        key_row = U[:, 3456:3456 + 2 * CJ * P].rearrange("p (s n) -> p s n", s=2)
        key_junk = U[:, 4224:4352]
        table2 = U[:, 0:NT * N].rearrange("p (t n) -> p t n", t=NT)
        codes = U[:, NT * N:2 * NT * N].rearrange("p (t n) -> p t n", t=NT)
        pick = U[:, 4608:4608 + NT * N].rearrange("p (t n) -> p t n", t=NT)
        prob = U[:, 0:2 * NT * N].rearrange("p (h t n) -> p h t n", h=2, t=NT)
        sq_q = U[:, 2304:2688]
        sq_k = U[:, 2688:3072]
        mix_v = U[:, 3072:3456]
        pv_low = U[:, 3456:3840]
        attn_o = U[:, 3840:4224]
        v_cur = U[:, 4224:4608]
        qh, ql = sb("qh", [P, N], F32R), sb("ql", [P, N], F32R)
        kzh = [sb(f"kzh{h}", [P, N], F32R) for h in range(2)]
        kzl = [sb(f"kzl{h}", [P, N], F32R) for h in range(2)]
        vs = sb("vs", [P, NT, 2, P], F32R)
        probT = [sb(f"probT_{c}", [P, NT, N], F32R) for c in ("hi", "lo")]
        feat = [sb(f"feat_{c}", [P, N], F32R) for c in ("hi", "lo")]
        cst = sb("cst", [P, C_ALL], F32)
        ident = cst[:, C_ID:C_ID + P]
        tri = cst[:, C_TRI:C_TRI + P]
        eidx = cst[:, C_EIDX:C_EIDX + EXPERTS]
        ones_f32 = cst[:, C_ONE:C_ONE + P]
        iota16 = sb("iota16", [P, N], F16)
        zero16 = sb("zero16", [P, P], BF16)
        head_ones = sb("head_ones", [P, P], F32R)
        bias = sb("bias", [P, 9 * KB], F32)
        ew = sb("ew", [P, 4], F32)
        ew_t = sb("ew_t", [P, 8], F32)
        v2f = V2[:].rearrange("p k n -> p (k n)")
        erow_i = v2f[0:CH, 0:2 * P].bitcast(I32)
        erow = v2f[0:CH, 2 * P:4 * P]
        ecol_i = v2f[:, 4 * P:4 * P + 3 * CH].bitcast(I32)
        ecol = sb("ecol", [P, 3 * CH], F32)
        ekey = sb("ekey", [P, CH], F32)
        etype = sb("etype", [P, CH], F32)
        digit = [etype[:]] + [v2f[:, 1024 + c * CH:1024 + (c + 1) * CH] for c in range(4)]
        diag16 = v2f[:, 1408:1408 + 320].bitcast(BF16)
        diag_w = v2f[:, 1728:1728 + 64].bitcast(BF16)
        dup = sb("dup", [P, CH], F32)
        live_w = sb("live_w", [P, CH], F32)
        stats = sb("stats", [P, NT, 2, 6], F32)
        mv = sb("mv", [P, NT, 2], F32)
        rstd = sb("rstd", [P, 4, NT], F32)
        smax = sb("smax", [P, 2, NT], F32)
        nmax = sb("nmax", [P, 2, NT], F32)
        ssum = sb("ssum", [P, 2, NT], F32)
        rsum = sb("rsum", [P, 2, NT], F32)
        tiny = sb("tiny", [P, 24], F32)
        PS = ctx.enter_context(nc.psum_tensor("PS", [P, 8, HALF], F32))

        row_bo = Q2[:].rearrange("p k n -> p (k n)")[:, 0:3 * D].rearrange("p (r d) -> p r d", r=3)
        k2f = K2[:].rearrange("p k n -> p (k n)")
        conv_row = k2f[:, 0:D]
        raw_down = k2f[:, D:D + KB * R].rearrange("p (k r) -> p k r", k=KB)
        raw_up = k2f[:, D + 512:D + 512 + KB * R].rearrange("p (k r) -> p k r", k=KB)
        raw_upb = k2f[:, 2 * D:2 * D + KB]
        raw_downb = k2f[:, 2 * D + 8:2 * D + 9]
        h_low = k2f[:, 2 * D + 16:2 * D + 16 + N]
        h_sum = k2f[:, 2 * D + 400:2 * D + 400 + N]
        xn_T = V2[:]
        sq_junk = k2f[:, 2 * D + 16:2 * D + 16 + N]
        t0h = T0[0][:].rearrange("p k n -> p (k n)")
        t0l = T0[1][:].rearrange("p k n -> p (k n)")
        wd = t0h[:, 0:KB * P].rearrange("p (k m) -> p k m", k=KB)
        hT = [t0h[:, D:D + N], t0h[:, D + N:D + 2 * N]]
        aug = [t0l[:, c * D:(c + 1) * D].rearrange("p (k m) -> p k m", k=KB) for c in range(2)]
        pc = [T1[c][:].rearrange("p k n -> p (k n)")[:, 0:D] for c in range(2)]
        disc_in = sb("disc_in", [P, 2, EXPERTS, KB], F32)
        dterm = sb("dterm", [P, 5, EXPERTS, KB], F32)
        moments = sb("moments", [P, 4, KB], F32)
        loss = sb("loss", [P, 5, EXPERTS], F32)
        pick_i = sb("pick_i", [P, 1], I32)

        w_in = [sem(f"w_in{s}") for s in range(SLOTS)]
        hi_ready = [sem(f"hi_ready{s}") for s in range(SLOTS)]
        lo_ready = [sem(f"lo_ready{s}") for s in range(SLOTS)]
        w_used = [sem(f"w_used{s}") for s in range(SLOTS)]
        keys_zeroed = sem("keys_zeroed")
        const_in = sem("const_in")
        edges_in = sem("edges_in")
        x_in = [sem(f"x_in{t}") for t in range(NT)]
        key_out = sem("key_out")
        key_calc = sem("key_calc")
        key_in = [sem(f"key_in{s}") for s in range(2)]
        prep = sem("prep")
        aprep = sem("aprep")
        norm_step = sem("norm_step")
        var_ready = sem("var_ready")
        rstd_guess = sem("rstd_guess")
        rstd_ready = sem("rstd_ready")
        xn_ready = sem("xn_ready")
        xn_mid = sem("xn_mid")
        xt_turned = sem("xt_turned")
        xt_hi = sem("xt_hi")
        xt_done = sem("xt_done")
        evac_hi = sem("evac_hi")
        bank_free = [sem(f"bank_free{s}") for s in range(2)]
        dup_ready = sem("dup_ready")
        live_ready = sem("live_ready")
        hot_ready = sem("hot_ready")
        hot_used = sem("hot_used")
        table_done = sem("table_done")
        table1_read = sem("table1_read")
        table2_read = sem("table2_read")
        mask_step = sem("mask_step")
        v_in = sem("v_in")
        v_turned = sem("v_turned")
        vh_ready = sem("vh_ready")
        vs_ready = sem("vs_ready")
        qk_hi = sem("qk_hi")
        ql_ready = sem("ql_ready")
        kl_ready = sem("kl_ready")
        score_done = sem("score_done")
        score_read = sem("score_read")
        nmax_ready = sem("nmax_ready")
        exp_done = sem("exp_done")
        recip_done = sem("recip_done")
        prob_ready = sem("prob_ready")
        prob_turned = sem("prob_turned")
        pT_hi = sem("pT_hi")
        pT_ready = sem("pT_ready")
        pv_done = sem("pv_done")
        pv_copied = sem("pv_copied")
        o_summed = sem("o_summed")
        oh_ready = sem("oh_ready")
        ol_ready = sem("ol_ready")
        sq_done = sem("sq_done")
        sq_summed = sem("sq_summed")
        feat_exp = sem("feat_exp")
        feat_hi = sem("feat_hi")
        feat_ready = sem("feat_ready")
        coeff_done = sem("coeff_done")
        mixv_ready = sem("mixv_ready")
        mix_ready = sem("mix_ready")
        mh_ready = sem("mh_ready")
        ml_ready = sem("ml_ready")
        rows_in = sem("rows_in")
        xr_in = sem("xr_in")
        res_ready = sem("res_ready")
        c_done = sem("c_done")
        x2_ready = sem("x2_ready")
        x2n_ready = sem("x2n_ready")
        x2n_mid = sem("x2n_mid")
        x2_turned = sem("x2_turned")
        x2_hi = sem("x2_hi")
        x2_done = sem("x2_done")
        x2_copied = sem("x2_copied")
        moment_done = sem("moment_done")
        loss_step = sem("loss_step")
        loss_sum = sem("loss_sum")
        idx_ready = sem("idx_ready")
        small_in = sem("small_in")
        convb_in = sem("convb_in")
        down_hi = sem("down_hi")
        down_ready = sem("down_ready")
        aug_hi = sem("aug_hi")
        aug_ready = sem("aug_ready")
        aug_zero = sem("aug_zero")
        hdown_done = sem("hdown_done")
        hlow_ready = sem("hlow_ready")
        h_step = sem("h_step")
        hT_hi = sem("hT_hi")
        hT_ready = sem("hT_ready")
        pc_hi = sem("pc_hi")
        pc_ready = sem("pc_ready")
        y_done = sem("y_done")
        y_ready = sem("y_ready")
        stored = sem("stored")

        block = ctx.enter_context(nc.Block())

        @block.sync
        def _(sp):
            def load_weights(slot, use, src):
                sp.wait_ge(lo_ready[slot], use + 1)
                sp.dma_start(raw[slot][:], src).then_inc(w_in[slot], 16)

            for t in range(NT):
                sp.dma_start(x_rows[:, t, :], x[t * P:(t + 1) * P, :]).then_inc(x_in[t], 16)
            for m in range(6):
                with sp.Fori(0, KB // 2) as i:
                    for s in range(2):
                        load_weights(s, A_BASE[m] + i, weights[ds(i * 2 + (8 * m + s), 1)]
                                     .rearrange("a p n -> (a p) n"))
                        if m < 4:
                            sp.wait_ge(key_out, 16)
                            sp.wait_ge(xt_done, NT)
                            sp.wait_ge(live_ready, i * 2 + (8 * m + s + 1))
                            sp.dma_start(key_row[:, s, :],
                                         key_dram[ds(i * 2 * CJ + CJ * (8 * m + s), CJ), :]
                                         .rearrange("c e -> (c e)").partition_broadcast(P)
                                         ).then_inc(key_in[s], 16)
            with sp.Fori(0, KB) as j:
                load_weights(0, B_BASE[0] + j, weights[ds(j + 48, 1)].rearrange("a p n -> (a p) n"))
                sp.wait_ge(v_turned, j + 1)
                for s in range(2):
                    sp.wait_ge(bank_free[s], 1 + 24)
                sp.dma_start(v_cur, V2[:, ds(j, 1), :].rearrange("p a n -> p (a n)")).then_inc(v_in, 16)
                for t in (1, 2):
                    load_weights(t, B_BASE[t] + j, weights[ds(j + (48 + 8 * t), 1)]
                                 .rearrange("a p n -> (a p) n"))
            with sp.Fori(0, 2) as half:
                for b in range(8):
                    load_weights(b % 2, half * 4 + (C_BASE + b // 2),
                                 weights[ds(half * 8 + (72 + b), 1)].rearrange("a p n -> (a p) n"))
            with sp.Fori(0, 2) as half:
                for b in range(4):
                    load_weights(b % 2, half * 2 + (E_BASE + b // 2),
                                 weights[ds(half * 4 + (88 + b), 1)].rearrange("a p n -> (a p) n"))
            sp.wait_ge(idx_ready, 1)
            expert = sp.value_load(pick_i[0:1, 0:1], min_val=0, max_val=EXPERTS - 1)
            sp.dma_start(raw_down, down[ds(expert, 1)].rearrange("a p k r -> (a p) k r")).then_inc(small_in, 16)
            sp.dma_start(raw_up, upT[ds(expert, 1)].rearrange("a p k r -> (a p) k r")).then_inc(small_in, 16)
            sp.dma_start(raw_upb, up_b[ds(expert, 1)].rearrange("a p k -> (a p) k")).then_inc(small_in, 16)
            sp.dma_start(raw_downb[0:R, :], down_b[ds(expert, 1)].rearrange("a r o -> (a r) o")).then_inc(small_in, 16)
            sp.dma_start(conv_row, conv_b[ds(expert, 1)].rearrange("a d -> (a d)").partition_broadcast(P)
                         ).then_inc(convb_in, 16)
            for b, (s, use) in enumerate(V_USES):
                load_weights(s, use, conv[ds(expert * 8 + b, 1)].rearrange("a p n -> (a p) n"))
            for half in range(2):
                c = slice(half * HALF, (half + 1) * HALF)
                for t in range(NT):
                    sp.wait_ge(y_ready, half * NT + t + 1)
                    sp.dma_start(out[t * P:(t + 1) * P, c], x_rows[:, t, c]).then_inc(stored, 16)
            sp.wait_ge(stored, 16 * 2 * NT)

        @block.gpsimd
        def _(pool):
            def split_lo(slot, use):
                pool.wait_ge(hi_ready[slot], use + 1)
                pool.tensor_tensor(w_lo[slot][:], raw[slot][:], w_hi[slot][:].bitcast(F32),
                                   ALU.subtract).then_inc(lo_ready[slot], 1)

            given = [(lo_ready[s], 1) for s in range(SLOTS)] + [(w_used[s], 1) for s in range(SLOTS)] + [
                (live_ready, 2), (bank_free[0], 1), (bank_free[1], 1), (hot_used, 2), (v_turned, 1), (score_read, 1),
                (mixv_ready, 1), (mix_ready, 1), (o_summed, 1)]
            for n, (s, k) in enumerate(given):
                pool.memset(tiny[:, n:n + 1], 0.0).then_inc(s, k)
            pool.wait_ge(key_calc, 1)
            pool.dma_start(key_dram, erow[:, 0:P]).then_inc(key_out, 16)
            split_lo(0, 0)
            for m in range(6):
                with pool.Fori(0, KB // 2) as i:
                    split_lo(1, A_BASE[m] + i)
                    split_lo(0, A_BASE[m] + i + 1)
            def split_q(j):
                pool.wait_ge(qk_hi, j * 3 + 1)
                pool.tensor_tensor(ql[:], Q2[:, ds(j, 1), :].rearrange("p a n -> p (a n)"),
                                   qh[:].bitcast(F32), ALU.subtract).then_inc(ql_ready, 1)

            def pair(j, last):
                split_lo(1, B_BASE[1] + j)
                split_lo(2, B_BASE[2] + j)
                pool.wait_ge(feat_hi, j + 1)
                pool.tensor_tensor(feat[1][:], sq_q, feat[0][:].bitcast(F32),
                                   ALU.subtract).then_inc(feat_ready, 1)
                split_lo(0, B_BASE[0] + j + 1)
                if not last:
                    split_q(j + 1)

            split_q(0)
            with pool.Fori(0, KB - 1) as j:
                pair(j, False)
            pair(KB - 1, True)
            pool.wait_ge(ql_ready, KB)
            pool.dma_start(row_bo, rows.partition_broadcast(P)).then_inc(rows_in, 16)
            pool.wait_ge(ol_ready, KB)
            pool.wait_ge(ml_ready, KB)
            pool.dma_start(x_rows, x.rearrange("(t p) d -> p t d", p=P)).then_inc(xr_in, 16)
            with pool.Fori(0, 2) as half:
                for b in range(1, 9):
                    split_lo(b % 2, half * 4 + (C_BASE + b // 2))
            with pool.Fori(0, 2) as half:
                for b in range(1, 4):
                    split_lo(b % 2, half * 2 + (E_BASE + b // 2))
                split_lo(0, half * 2 + (E_BASE + 2))
            for b in range(2, 8, 2):
                split_lo(*V_USES[b])

        @block.scalar
        def _(act):
            def split_hi(slot, use):
                act.wait_ge(w_in[slot], use * 16 + 16)
                act.wait_ge(w_used[slot], use + 1)
                act.activation(w_hi[slot][:], raw[slot][:], ACT.Copy).then_inc(hi_ready[slot], 1)

            def guess_rstd(n):
                t = n % NT
                act.wait_ge(var_ready, n + 1)
                act.activation(rstd[:, 1, t:t + 1], rstd[:, 0, t:t + 1], ACT.Ln).then_inc(rstd_guess, 1)
                act.wait_ge(rstd_guess, 2 * n + 1)
                act.activation(rstd[:, 1, t:t + 1], rstd[:, 1, t:t + 1], ACT.Exp, scale=-0.5).then_inc(rstd_guess, 1)

            def norm_rows(which, done):
                guess_rstd(NT * which)
                guess_rstd(NT * which + 1)
                act.wait_ge(rstd_ready, NT * which + 2)
                act.activation(xn_rows[:, 1, :], x_rows[:, 1, :], ACT.Identity, scale=rstd[:, 2, 1:2],
                               bias=rstd[:, 3, 1:2]).then_inc(done, 1)
                guess_rstd(NT * which + 2)

            def turned(t):
                b = LN_BANKS[t]
                return PS[:, b:b + 2, :].rearrange("p b (k n) -> p (b k) n", k=4), slice(t * P, (t + 1) * P)

            act.dma_start(cst[:], consts).then_inc(const_in, 16)
            act.dma_start(ew[:], edge_weights.partition_broadcast(P)).then_inc(const_in, 16)
            act.dma_start(erow_i, edge_rows).then_inc(edges_in, 16)
            act.dma_start(ecol_i, edge_cols).then_inc(edges_in, 16)
            act.dma_start(bias[:], bias_cols).then_inc(const_in, 16)
            act.dma_start(disc_in[:], disc).then_inc(const_in, 16)
            act.wait_ge(prep, 3)
            act.activation(ew_t[:, 0:4], ew_t[:, 0:4], ACT.Exp).then_inc(aprep, 1)
            act.wait_ge(aprep, 1)
            act.activation(ew_t[:, 0:4], ew_t[:, 0:4], ACT.Ln, bias=1.0).then_inc(aprep, 1)
            act.wait_ge(const_in, 64)
            act.activation(head_ones[:], cst[:, C_ONES:C_ONES + P], ACT.Copy).then_inc(aprep, 1)
            norm_rows(0, xn_mid)
            split_hi(0, 0)
            for t in range(NT):
                act.wait_ge(xt_turned, t + 1)
                src, r = turned(t)
                act.activation(xT[0][:, :, r], src, ACT.Copy).then_inc(xt_hi, 1)

            def table_out(dst, done):
                for t in range(NT):
                    last = act.activation(dst[:, t, :], PS[:, 2 + t, 0:N], ACT.Copy)
                last.then_inc(done, 1)

            for m in range(6):
                dst = [T0, T1, Q2, T0, K2, V2][m]
                with act.Fori(0, KB // 2) as i:
                    for s in range(2):
                        split_hi(1 - s, A_BASE[m] + i + s)
                        act.wait_ge(w_used[s], A_BASE[m] + i + 2)
                        plain = m in (2, 4, 5)
                        act.activation((dst if plain else dst[0])[:, ds(i * 2 + s, 1), :]
                                       .rearrange("p a n -> p (a n)"), PS[:, s, 0:N], ACT.Identity,
                                       bias=bias[:, ds(i * 2 + (8 * m + s), 1)]
                                       ).then_inc(bank_free[s] if plain else evac_hi, 1)
                if m == 1:
                    act.wait_ge(table_done, 1)
                    table_out(mask, table1_read)
                if m == 3:
                    act.wait_ge(table_done, 2)
                    table_out(table2, table2_read)

            def split_qk(j):
                act.activation(qh[:], Q2[:, ds(j, 1), :].rearrange("p a n -> p (a n)"), ACT.Copy).then_inc(qk_hi, 1)
                for h in range(2):
                    r = slice(64 * h, 64 * h + 64)
                    act.activation(kzh[h][r, :], K2[r, ds(j, 1), :].rearrange("p a n -> p (a n)"),
                                   ACT.Copy).then_inc(qk_hi, 1)

            def pair(j, last):
                split_hi(1, B_BASE[1] + j)
                act.wait_ge(w_used[0], B_BASE[0] + j + 2)
                act.activation(sq_q, PS[:, 0, 0:N], ACT.Square, bias=bias[:, ds(j + 6 * KB, 1)]).then_inc(sq_done, 1)
                act.wait_ge(v_turned, j + 2)
                act.activation(vs[:, :, :, 0:HD], PS[:, 7, 0:N].rearrange("p (t h d) -> p t h d", t=NT, h=2),
                               ACT.Copy).then_inc(vh_ready, 1)
                for h in range(2):
                    act.wait_ge(nmax_ready, j * 2 + (h + 1))
                    for t in range(NT):
                        act.activation(prob[:, h, t, :], prob[:, h, t, :], ACT.Exp, bias=nmax[:, h, t:t + 1],
                                       scale=SCALE, accum_out=ssum[:, h, t:t + 1]).then_inc(exp_done, 1)
                    if h == 0:
                        split_hi(2, B_BASE[2] + j)
                act.wait_ge(w_used[1], B_BASE[1] + j + 2)
                act.activation(sq_k, PS[:, 1, 0:N], ACT.Square, bias=bias[:, ds(j + 7 * KB, 1)]).then_inc(sq_done, 1)

                def turned_hi(h):
                    for t in range(NT):
                        act.wait_ge(prob_turned, j * 6 + (3 * h + t + 1))
                        if h:
                            act.wait_ge(pv_done, j * 2 + 1)
                        act.activation(probT[0][:, t, :], PS[:, TURN_BANKS[t], 0:N], ACT.Copy).then_inc(pT_hi, 1)

                def pv_copy(h):
                    act.wait_ge(pv_done, j * 2 + (h + 1))
                    rows_in_psum = slice(64 * (1 - h), 64 * (1 - h) + 64)
                    act.activation(pv_low[64 * h:64 * h + 64, :], PS[rows_in_psum, 7, 0:N],
                                   ACT.Copy).then_inc(pv_copied, 1)

                turned_hi(0)
                act.wait_ge(sq_summed, j + 1)
                act.activation(sq_q, sq_q, ACT.Exp, scale=-0.5).then_inc(feat_exp, 1)
                act.wait_ge(feat_exp, j + 1)
                act.activation(feat[0][:], sq_q, ACT.Copy).then_inc(feat_hi, 1)
                split_hi(0, B_BASE[0] + j + 1)
                pv_copy(0)
                turned_hi(1)
                if not last:
                    split_qk(j + 1)
                act.wait_ge(w_used[2], B_BASE[2] + j + 2)
                act.activation(mix_v, PS[:, 0, 0:N], ACT.Identity, bias=bias[:, ds(j + 8 * KB, 1)]).then_inc(mixv_ready, 1)
                act.wait_ge(mix_ready, j + 2)
                act.activation(T1[0][:, ds(j, 1), :].rearrange("p a n -> p (a n)"), mix_v, ACT.Copy).then_inc(mh_ready, 1)
                pv_copy(1)
                act.wait_ge(o_summed, j * 2 + 3)
                act.activation(T0[0][:, ds(j, 1), :].rearrange("p a n -> p (a n)"), attn_o, ACT.Copy).then_inc(oh_ready, 1)

            for s in range(2):
                act.wait_ge(bank_free[s], 1 + 24)
            split_qk(0)
            with act.Fori(0, KB - 1) as j:
                pair(j, False)
            pair(KB - 1, True)

            with act.Fori(0, 2) as half:
                for b in range(1, 9):
                    split_hi(b % 2, half * 4 + (C_BASE + b // 2))
            norm_rows(1, x2n_mid)
            for t in range(NT):
                act.wait_ge(x2_turned, t + 1)
                src, r = turned(t)
                act.activation(xT[0][:, :, r], src, ACT.Copy).then_inc(x2_hi, 1)
                act.activation(xn_T[:, :, r], src, ACT.Copy).then_inc(x2_copied, 1)
            with act.Fori(0, 2) as half:
                for b in range(1, 4):
                    split_hi(b % 2, half * 2 + (E_BASE + b // 2))
                split_hi(0, half * 2 + (E_BASE + 2))
            split_hi(*V_USES[1])
            split_hi(*V_USES[2])
            act.wait_ge(hdown_done, 1)
            act.activation(h_low[0:R, :], PS[R:2 * R, 7, 0:N], ACT.Copy).then_inc(hlow_ready, 1)
            split_hi(*V_USES[3])
            act.wait_ge(h_step, 2)
            act.activation(hT[0][0:R, :], h_sum[0:R, :], ACT.Copy).then_inc(hT_hi, 1)
            split_hi(*V_USES[4])
            split_hi(*V_USES[5])
            act.wait_ge(w_used[V_USES[3][0]], V_USES[3][1] + 2)
            act.activation(pc[0][:, 0:HALF], PS[:, 6, :], ACT.Copy).then_inc(pc_hi, 1)
            split_hi(*V_USES[6])
            split_hi(*V_USES[7])
            act.wait_ge(w_used[V_USES[7][0]], V_USES[7][1] + 2)
            act.activation(pc[0][:, HALF:D], PS[:, 7, :], ACT.Copy).then_inc(pc_hi, 1)

        @block.vector
        def _(dve):
            for h in range(2):
                z = slice(64 * (1 - h), 64 * (1 - h) + 64)
                dve.memset(kzh[h][z, :].bitcast(F32), 0.0)
                dve.memset(kzl[h][z, :].bitcast(F32), 0.0).then_inc(keys_zeroed, 1)
            dve.wait_ge(const_in, 64)
            dve.tensor_scalar(ew_t[:, 0:4], ew[:], -1.0, None, ALU.mult).then_inc(prep, 1)
            dve.wait_ge(prep, 1)
            dve.tensor_tensor(ew_t[:, 0:4], ew_t[:, 0:4], ew[:], ALU.min).then_inc(prep, 1)
            dve.tensor_scalar(ew_t[:, 4:8], ew[:], 0.0, None, ALU.max).then_inc(prep, 1)
            dve.tensor_copy(iota16[:], cst[:, C_IOTA:C_IOTA + N]).then_inc(prep, 1)
            dve.memset(zero16[:], 0.0)
            dve.memset(diag16, 0.0).then_inc(prep, 1)
            dve.tensor_scalar(diag_w, ident, 2.0 ** -96, None, ALU.mult).then_inc(prep, 1)
            dve.wait_ge(prep, 6)
            dve.tensor_copy(diag16[:, 2 * P:3 * P], ident).then_inc(prep, 1)

            normed = [0]

            def step(ins):
                normed[0] += 1
                ins.then_inc(norm_step, 1)
                dve.wait_ge(norm_step, normed[0])

            def row_stats(which, t):
                for c in range(2):
                    dve.bn_stats(stats[:, t, c, :], x_rows[:, t, c * HALF:(c + 1) * HALF]).then_inc(norm_step, 1)
                normed[0] += 2
                dve.wait_ge(norm_step, normed[0])
                step(dve.bn_aggr(mv[:, t, :], stats[:, t, :, :].rearrange("p c s -> p (c s)")))
                dve.tensor_scalar(rstd[:, 0, t:t + 1], mv[:, t, 1:2], EPS, None, ALU.add).then_inc(var_ready, 1)

            def row_norm(which, t, done):
                v, y, z, m = (rstd[:, c, t:t + 1] for c in range(4))
                dve.wait_ge(rstd_guess, 2 * (NT * which + t) + 2)
                step(dve.tensor_tensor(z, y, y, ALU.mult))
                step(dve.tensor_tensor(z, z, v, ALU.mult))
                step(dve.tensor_scalar(z, z, -0.5, 1.5, ALU.mult, ALU.add))
                step(dve.tensor_tensor(z, z, y, ALU.mult))
                dve.scalar_tensor_tensor(out=m, in0=mv[:, t, 0:1], scalar=-1.0, in1=z,
                                         op0=ALU.mult, op1=ALU.mult).then_inc(rstd_ready, 1)
                if t != 1:
                    dve.tensor_scalar(xn_rows[:, t, :], x_rows[:, t, :], mv[:, t, 0:1], z,
                                      ALU.subtract, ALU.mult).then_inc(done, 1)

            def turned(t):
                b = LN_BANKS[t]
                return PS[:, b:b + 2, :].rearrange("p b (k n) -> p (b k) n", k=4), slice(t * P, (t + 1) * P)

            dve.wait_ge(x_in[0], 16)
            row_stats(0, 0)
            dve.wait_ge(x_in[1], 16)
            row_stats(0, 1)
            row_norm(0, 0, xn_ready)
            row_norm(0, 1, xn_ready)
            dve.wait_ge(x_in[2], 16)
            row_stats(0, 2)
            row_norm(0, 2, xn_ready)
            dve.wait_ge(edges_in, 32)
            dve.tensor_copy(erow, erow_i).then_inc(prep, 1)
            dve.tensor_copy(ecol[:], ecol_i).then_inc(prep, 1)
            dve.wait_ge(prep, 9)
            dve.scalar_tensor_tensor(out=erow[:, 0:P], in0=erow[:, 0:P], scalar=float(N), in1=erow[:, P:2 * P],
                                     op0=ALU.mult, op1=ALU.add).then_inc(key_calc, 1)
            for t in range(NT):
                dve.wait_ge(xt_hi, t + 1)
                src, r = turned(t)
                dve.tensor_tensor(xT[1][:, :, r], src, xT[0][:, :, r].bitcast(F32),
                                  ALU.subtract).then_inc(xt_done, 1)
            src_c, dst_c, type_c = (ecol[:, c * CH:(c + 1) * CH] for c in range(3))
            dve.scalar_tensor_tensor(out=ekey[:], in0=src_c, scalar=float(N), in1=dst_c,
                                     op0=ALU.mult, op1=ALU.add).then_inc(prep, 1)
            dve.tensor_scalar(digit[0], type_c, 1.0, 1.0, ALU.is_equal, ALU.mult).then_inc(prep, 1)
            dve.tensor_scalar(digit[1], type_c, 2.0, 2.0, ALU.is_equal, ALU.mult).then_inc(prep, 1)
            dve.tensor_scalar(digit[2], type_c, 3.0, 4.0, ALU.is_equal, ALU.mult).then_inc(prep, 1)
            dve.tensor_scalar(digit[3], type_c, 4.0, 8.0, ALU.is_ge, ALU.mult).then_inc(prep, 1)
            dve.tensor_scalar(digit[4], type_c, 0.0, 8.0, ALU.is_le, ALU.mult).then_inc(prep, 1)
            for c in range(1, 5):
                dve.wait_ge(prep, 14 + c)
                dve.tensor_tensor(digit[0], digit[0], digit[c], ALU.add).then_inc(prep, 1)
            dve.wait_ge(prep, 19)
            dve.tensor_tensor(digit[0], digit[0], cst[:, C_POW:C_POW + CH], ALU.mult).then_inc(prep, 1)
            mu, sg = disc_in[:, 0], disc_in[:, 1]
            dve.tensor_tensor(dterm[:, 3], sg, sg, ALU.mult).then_inc(prep, 1)
            dve.wait_ge(prep, 21)
            dve.reciprocal(dterm[:, 0], dterm[:, 3]).then_inc(prep, 1)
            dve.wait_ge(prep, 22)
            dve.tensor_tensor(dterm[:, 1], dterm[:, 0], mu, ALU.mult).then_inc(prep, 1)
            dve.wait_ge(prep, 23)
            dve.tensor_tensor(dterm[:, 2], dterm[:, 1], mu, ALU.mult).then_inc(prep, 1)
            dve.wait_ge(aprep, 2)
            dve.tensor_tensor(ew[:], ew_t[:, 0:4], ew_t[:, 4:8], ALU.add).then_inc(prep, 1)
            dve.wait_ge(prep, 25)
            dve.tensor_scalar(ew[:], ew[:], 1.0 / SCALE, None, ALU.mult).then_inc(prep, 1)

            dve.wait_ge(prep, 26)
            for m in range(4):
                dst = [T0, T1, None, T0][m]
                splits_before = [0, 8, 0, 16][m]
                with dve.Fori(0, KB // 2) as i:
                    for s in range(2):
                        job = i * 2 + (8 * m + s)
                        ch0 = i * 2 * CJ + CJ * (8 * m + s)
                        dve.wait_ge(key_in[s], i * 16 + (64 * m + 16))
                        for c in range(CJ):
                            if c:
                                dve.wait_ge(dup_ready, job * CJ + c)
                            dve.scalar_tensor_tensor(
                                out=key_junk, in0=key_row[:, s, c * P:(c + 1) * P], scalar=ekey[:, ds(ch0 + c, 1)],
                                in1=tri, op0=ALU.is_equal, op1=ALU.mult,
                                accum_out=dup[:, ds(ch0 + c, 1)]).then_inc(dup_ready, 1)
                        dve.wait_ge(dup_ready, job * CJ + CJ)
                        these = ds(ch0, CJ)
                        dve.scalar_tensor_tensor(out=live_w[:, these], in0=dup[:, these], scalar=0.0,
                                                 in1=etype[:, these], op0=ALU.is_equal,
                                                 op1=ALU.mult).then_inc(live_ready, 1)
                        dve.wait_ge(hot_used, job + 1)
                        for c in range(CJ):
                            dve.tensor_scalar(dst_hot[:, s, c, :], iota16[:], ecol[:, ds(ch0 + (c + CH), 1)], None,
                                              ALU.is_equal).then_inc(hot_ready, 1)
                        dve.wait_ge(live_ready, job + 3)
                        for c in range(CJ):
                            dve.tensor_scalar(src_hot[:, s, c, :], iota16[:], ecol[:, ds(ch0 + c, 1)],
                                              live_w[:, ds(ch0 + c, 1)], ALU.is_equal,
                                              ALU.mult).then_inc(hot_ready, 1)
                        if dst:
                            dve.wait_ge(evac_hi, i * 2 + (splits_before + s + 1))
                            j1 = ds(i * 2 + s, 1)
                            dve.scalar_tensor_tensor(
                                out=dst[1][:, j1, :].rearrange("p a n -> p (a n)"), in0=PS[:, s, 0:N],
                                scalar=bias[:, ds(job, 1)],
                                in1=dst[0][:, j1, :].rearrange("p a n -> p (a n)").bitcast(F32),
                                op0=ALU.add, op1=ALU.subtract).then_inc(bank_free[s], 1)
            dve.wait_ge(table2_read, 1)
            dve.wait_ge(table1_read, 1)
            masks = [0]

            def masked(ins):
                masks[0] += 1
                ins.then_inc(mask_step, 1)
                dve.wait_ge(mask_step, masks[0])

            for t in range(NT):
                last = dve.copy_predicated(mask[:, t, :], PS[:, 2 + t, 0:N].bitcast(U32), table2[:, t, :])
            masked(last)
            masked(dve.tensor_scalar(codes.bitcast(I32), mask[:].bitcast(I32), 23, 3,
                                     ALU.logical_shift_right, ALU.bitwise_and))
            masked(dve.tensor_scalar(mask[:], mask[:], 0.0, ABSENT, ALU.is_equal, ALU.mult))
            for w in range(4):
                masked(dve.tensor_scalar(pick, codes.bitcast(I32), float(w), ew[:, w:w + 1],
                                         ALU.is_equal, ALU.mult))
                masked(dve.tensor_tensor(mask[:], mask[:], pick, ALU.add))

            def split_k(j):
                for h in range(2):
                    r = slice(64 * h, 64 * h + 64)
                    dve.wait_ge(qk_hi, j * 3 + (h + 2))
                    dve.tensor_tensor(kzl[h][r, :], K2[r, ds(j, 1), :].rearrange("p a n -> p (a n)"),
                                      kzh[h][r, :].bitcast(F32), ALU.subtract).then_inc(kl_ready, 1)

            def pair(j, last):
                def softmax_in(h):
                    for t in range(NT):
                        dve.wait_ge(score_done, j * 6 + (3 * h + t + 1))
                        dve.memset(tiny[:, 16 + 3 * h + t:17 + 3 * h + t], 0.0)
                        dve.tensor_tensor_reduce(prob[:, h, t, :], PS[:, 2 + t, 0:N], mask[:, t, :], 1.0,
                                                 3.0 * ABSENT, ALU.add, ALU.max,
                                                 smax[:, h, t:t + 1]).then_inc(score_read, 1)
                    dve.wait_ge(score_read, j * 6 + (3 * h + 4))
                    dve.tensor_scalar(nmax[:, h, :], smax[:, h, :], -SCALE, None, ALU.mult).then_inc(nmax_ready, 1)

                def normalise(h):
                    dve.wait_ge(exp_done, j * 6 + (3 * h + 3))
                    dve.reciprocal(rsum[:, h, :], ssum[:, h, :]).then_inc(recip_done, 1)
                    dve.wait_ge(recip_done, j * 2 + (h + 1))
                    for t in range(NT):
                        dve.tensor_scalar(prob[:, h, t, :], prob[:, h, t, :], rsum[:, h, t:t + 1], None,
                                          ALU.mult).then_inc(prob_ready, 1)

                def turned_lo(h):
                    for t in range(NT):
                        dve.wait_ge(pT_hi, j * 6 + (3 * h + t + 1))
                        dve.tensor_tensor(probT[1][:, t, :], PS[:, TURN_BANKS[t], 0:N],
                                          probT[0][:, t, :].bitcast(F32), ALU.subtract).then_inc(pT_ready, 1)

                def pv_sum(h):
                    r = slice(64 * h, 64 * h + 64)
                    dve.wait_ge(pv_copied, j * 2 + (h + 1))
                    dve.tensor_tensor(attn_o[r, :], PS[r, 7, 0:N], pv_low[r, :], ALU.add).then_inc(o_summed, 1)

                dve.wait_ge(vh_ready, j + 1)
                dve.tensor_tensor(vs[:, :, :, HD:P], PS[:, 7, 0:N].rearrange("p (t h d) -> p t h d", t=NT, h=2),
                                  vs[:, :, :, 0:HD].bitcast(F32), ALU.subtract).then_inc(vs_ready, 1)
                softmax_in(0)
                softmax_in(1)
                normalise(0)
                normalise(1)
                dve.wait_ge(sq_done, j * 2 + 2)
                dve.tensor_tensor(sq_q, sq_q, sq_k, ALU.add).then_inc(sq_summed, 1)
                turned_lo(0)
                pv_sum(0)
                turned_lo(1)
                if not last:
                    split_k(j + 1)
                dve.wait_ge(coeff_done, j + 1)
                dve.wait_ge(mixv_ready, j + 2)
                dve.tensor_tensor(mix_v, PS[:, 2, 0:N], mix_v, ALU.mult).then_inc(mix_ready, 1)
                dve.wait_ge(mh_ready, j + 1)
                j1 = ds(j, 1)
                dve.tensor_tensor(T1[1][:, j1, :].rearrange("p a n -> p (a n)"), mix_v,
                                  T1[0][:, j1, :].rearrange("p a n -> p (a n)").bitcast(F32),
                                  ALU.subtract).then_inc(ml_ready, 1)
                pv_sum(1)
                dve.wait_ge(oh_ready, j + 1)
                dve.tensor_tensor(T0[1][:, j1, :].rearrange("p a n -> p (a n)"), attn_o,
                                  T0[0][:, j1, :].rearrange("p a n -> p (a n)").bitcast(F32),
                                  ALU.subtract).then_inc(ol_ready, 1)

            split_k(0)
            with dve.Fori(0, KB - 1) as j:
                pair(j, False)
            pair(KB - 1, True)

            dve.wait_ge(rows_in, 16)
            dve.wait_ge(xr_in, 16)
            for r in range(2):
                if r:
                    dve.wait_ge(res_ready, NT)
                for t in range(NT):
                    dve.tensor_tensor(x_rows[:, t, :], x_rows[:, t, :], row_bo[:, r, :], ALU.add).then_inc(res_ready, 1)
            dve.wait_ge(res_ready, 2 * NT)

            def add_sums(half, t):
                c = slice(half * HALF, (half + 1) * HALF)
                if t < NT - 1:
                    dve.wait_ge(c_done, half * (NT - 1) + t + 1)
                else:
                    dve.wait_ge(w_used[1], 1 + C_BASE + 4 * half + 4)
                dve.tensor_tensor(x_rows[:, t, c], PS[:, 3 * half + t, :], x_rows[:, t, c],
                                  ALU.add).then_inc(x2_ready, 1)

            for t in range(NT):
                add_sums(0, t)
            for t in range(2):
                add_sums(1, t)
                dve.wait_ge(x2_ready, NT + t + 1)
                row_stats(1, t)
            row_norm(1, 0, x2n_ready)
            add_sums(1, 2)
            row_norm(1, 1, x2n_ready)
            dve.wait_ge(x2_ready, 2 * NT)
            row_stats(1, 2)
            row_norm(1, 2, x2n_ready)
            for t in range(NT):
                dve.wait_ge(x2_copied, t + 1)
                src, r = turned(t)
                dve.tensor_tensor(xT[1][:, :, r], src, xT[0][:, :, r].bitcast(F32),
                                  ALU.subtract).then_inc(x2_done, 1)
            dve.tensor_reduce(moments[:, 0, :], xn_T, X, ALU.add).then_inc(moment_done, 1)
            for k in range(KB):
                if k:
                    dve.wait_ge(moment_done, k + 1)
                dve.tensor_tensor_reduce(sq_junk, xn_T[:, k, :], xn_T[:, k, :], 1.0, 0.0, ALU.mult, ALU.add,
                                         moments[:, 1, k:k + 1]).then_inc(moment_done, 1)
            ls = [0]

            def lstep(ins):
                ls[0] += 1
                ins.then_inc(loss_step, 1)
                dve.wait_ge(loss_step, ls[0])

            dve.wait_ge(moment_done, KB + 1)
            lstep(dve.tensor_scalar(moments[:, 2, :], moments[:, 1, :], 1.0 / N, None, ALU.mult))
            lstep(dve.tensor_scalar(moments[:, 3, :], moments[:, 0, :], -2.0 / N, None, ALU.mult))
            m2 = moments[:, 2:3, :].broadcast_to([P, EXPERTS, KB])
            m1 = moments[:, 3:4, :].broadcast_to([P, EXPERTS, KB])
            lstep(dve.tensor_tensor(dterm[:, 3], dterm[:, 0], m2, ALU.mult))
            lstep(dve.tensor_tensor(dterm[:, 4], dterm[:, 1], m1, ALU.mult))
            lstep(dve.tensor_tensor(dterm[:, 3], dterm[:, 3], dterm[:, 4], ALU.add))
            lstep(dve.tensor_tensor(dterm[:, 3], dterm[:, 3], dterm[:, 2], ALU.add))
            lstep(dve.tensor_reduce(loss[:, 0, :], dterm[:, 3], X, ALU.add))
            dve.wait_ge(loss_sum, 1)
            lstep(dve.tensor_copy(loss[:, 1, :], PS[:, 7, 0:EXPERTS]))
            lstep(dve.tensor_reduce(loss[:, 2, 0:1], loss[:, 1, :], X, ALU.min))
            lstep(dve.tensor_scalar(loss[:, 3, :], loss[:, 1, :], loss[:, 2, 0:1], 100.0, ALU.is_gt, ALU.mult))
            lstep(dve.tensor_tensor(loss[:, 3, :], loss[:, 3, :], eidx, ALU.add))
            lstep(dve.tensor_reduce(loss[:, 4, 0:1], loss[:, 3, :], X, ALU.min))
            lstep(dve.tensor_scalar(loss[:, 4, 0:1], loss[:, 4, 0:1], float(EXPERTS - 1), None, ALU.min))
            dve.tensor_copy(pick_i[:], loss[:, 4, 0:1]).then_inc(idx_ready, 1)
            for t in range(NT):
                dve.tensor_tensor(x_rows[:, t, :], x_rows[:, t, :], row_bo[:, 2, :], ALU.add).then_inc(res_ready, 1)
            dve.memset(t0l[:, 0:2 * D].bitcast(F32), 0.0).then_inc(aug_zero, 1)
            dve.memset(hT[0][R:P, :].bitcast(F32), 0.0)
            dve.memset(hT[1][R:P, :].bitcast(F32), 0.0).then_inc(aug_zero, 1)
            dve.wait_ge(aug_zero, 2)
            dve.memset(hT[0][R:R + 1, :].bitcast(F32), 1.0).then_inc(aug_zero, 1)
            dve.wait_ge(small_in, 64)
            dve.tensor_copy(wd[:, :, 0:R], raw_down).then_inc(down_hi, 1)
            dve.tensor_copy(aug[0][:, :, 0:R], raw_up).then_inc(aug_hi, 1)
            dve.tensor_copy(aug[0][:, :, R:R + 1], raw_upb.unsqueeze(2)).then_inc(aug_hi, 1)
            dve.wait_ge(down_hi, 1)
            dve.tensor_tensor(wd[:, :, R:P], raw_down, wd[:, :, 0:R].bitcast(F32), ALU.subtract).then_inc(down_ready, 1)
            dve.wait_ge(aug_hi, 2)
            dve.tensor_tensor(aug[1][:, :, 0:R], raw_up, aug[0][:, :, 0:R].bitcast(F32), ALU.subtract).then_inc(aug_ready, 1)
            dve.tensor_tensor(aug[1][:, :, R:R + 1], raw_upb.unsqueeze(2), aug[0][:, :, R:R + 1].bitcast(F32),
                              ALU.subtract).then_inc(aug_ready, 1)
            dve.wait_ge(convb_in, 16)
            dve.wait_ge(res_ready, 3 * NT)
            for t in range(NT):
                dve.tensor_tensor(x_rows[:, t, :], x_rows[:, t, :], conv_row, ALU.add).then_inc(res_ready, 1)
            def split_lo(b):
                s, use = V_USES[b]
                dve.wait_ge(hi_ready[s], use + 1)
                dve.tensor_tensor(w_lo[s][:], raw[s][:], w_hi[s][:].bitcast(F32),
                                  ALU.subtract).then_inc(lo_ready[s], 1)

            def split_p(half):
                c = slice(half * HALF, (half + 1) * HALF)
                dve.wait_ge(pc_hi, half + 1)
                dve.tensor_tensor(pc[1][:, c], PS[:, 6 + half, :], pc[0][:, c].bitcast(F32), ALU.subtract).then_inc(pc_ready, 1)

            split_lo(1)
            dve.wait_ge(hlow_ready, 1)
            dve.tensor_tensor(h_sum[0:R, :], PS[0:R, 7, 0:N], h_low[0:R, :], ALU.add).then_inc(h_step, 1)
            dve.wait_ge(h_step, 1)
            dve.tensor_scalar(h_sum[0:R, :], h_sum[0:R, :], raw_downb[0:R, :], 0.0, ALU.add, ALU.max).then_inc(h_step, 1)
            split_lo(3)
            dve.wait_ge(hT_hi, 1)
            dve.tensor_tensor(hT[1][0:R, :], h_sum[0:R, :], hT[0][0:R, :].bitcast(F32), ALU.subtract).then_inc(hT_ready, 1)
            split_lo(5)
            split_p(0)
            split_lo(7)
            split_p(1)
            dve.wait_ge(res_ready, 4 * NT)
            for half in range(2):
                c = slice(half * HALF, (half + 1) * HALF)
                for t in range(NT):
                    dve.wait_ge(y_done, half * NT + t + 1)
                    dve.tensor_tensor(x_rows[:, t, c], PS[:, 3 * half + t, :], x_rows[:, t, c],
                                      ALU.add).then_inc(y_ready, 1)

        @block.tensor
        def _(pe):
            def turn(t, turned):
                for k in range(KB):
                    last = pe.transpose(PS[:, LN_BANKS[t] + k // 4, (k % 4) * P:(k % 4 + 1) * P],
                                        xn_rows[:, t, k * P:(k + 1) * P], ident)
                last.then_inc(turned, 1)

            def column_job(slot, use, src, bank, ks=range(KB)):
                o = PS[:, bank, 0:N]
                pe.wait_ge(hi_ready[slot], use + 1)
                for k in ks:
                    wh = w_hi[slot][:, k * P:(k + 1) * P]
                    pe.matmul(o, wh, src[0][:, k, :], start=(k == 0), stop=False)
                    pe.matmul(o, wh, src[1][:, k, :], start=False, stop=False)
                pe.wait_ge(lo_ready[slot], use + 2)
                for k in ks:
                    wl = w_lo[slot][:, k * P:(k + 1) * P]
                    last = pe.matmul(o, wl, src[0][:, k, :], start=False, stop=(k == KB - 1))
                if ks[-1] == KB - 1:
                    last.then_inc(w_used[slot], 1)

            def row_block(slot, use, src, half, kp, first, final, done=None):
                def go(part, weights_in, t, k2, start, stop):
                    if isinstance(half, int):
                        bank = PS[:, half * 3 + t, :]
                    else:
                        bank = PS[:, ds(half * 3 + t, 1), :].rearrange("p a n -> p (a n)")
                    return pe.matmul(bank, src[part][:, 2 * kp + k2, t * P:(t + 1) * P],
                                     weights_in[slot][:, k2 * HALF:(k2 + 1) * HALF], start=start, stop=stop)

                pe.wait_ge(hi_ready[slot], use + 1)
                if done is None:
                    for part in range(2):
                        for k2 in range(2):
                            for t in range(NT):
                                go(part, w_hi, t, k2, first and part == 0 and k2 == 0, False)
                    pe.wait_ge(lo_ready[slot], use + 2)
                    for k2 in range(2):
                        for t in range(NT):
                            last = go(0, w_lo, t, k2, False, final and k2 == 1)
                else:
                    pe.wait_ge(lo_ready[slot], use + 2)
                    for t in range(NT):
                        for k2 in range(2):
                            go(0, w_hi, t, k2, False, False)
                            go(1, w_hi, t, k2, False, False)
                        for k2 in range(2):
                            last = go(0, w_lo, t, k2, False, k2 == 1)
                        if t < NT - 1:
                            last.then_inc(done, 1)
                last.then_inc(w_used[slot], 1)

            pe.wait_ge(const_in, 64)
            pe.wait_ge(xn_ready, 1)
            turn(0, xt_turned)
            pe.wait_ge(xn_mid, 1)
            turn(1, xt_turned)
            pe.wait_ge(xn_ready, 2)
            turn(2, xt_turned)

            pe.wait_ge(xt_done, NT)
            for m in range(6):
                src = [xT, xT, T0, xT, T1, T0][m]
                if m == 0:
                    pe.wait_ge(prep, 7)
                    for t in range(NT):
                        pe.matmul(PS[:, 2 + t, 0:N], diag_w, diag16[:, (2 - t) * P:(5 - t) * P],
                                  start=True, stop=False)
                if m == 2:
                    pe.wait_ge(table1_read, 1)
                    for t in range(NT):
                        pe.matmul(PS[:, 2 + t, 0:N], diag16[:, 0:P], diag16[:, 0:N], start=True, stop=False)
                with pe.Fori(0, KB // 2) as i:
                    for s in range(2):
                        job = i * 2 + (8 * m + s)
                        pe.wait_ge(bank_free[s], i + (A_BASE[m] + 1))
                        column_job(s, A_BASE[m] + i, src, s)
                        if m < 4:
                            pe.wait_ge(hot_ready, job * 2 * CJ + 2 * CJ)
                            for c in range(CJ):
                                for t in range(NT):
                                    last = pe.matmul(PS[:, 2 + t, 0:N], src_hot[:, s, c, t * P:(t + 1) * P],
                                                     dst_hot[:, s, c, :], start=False, stop=False)
                            last.then_inc(hot_used, 1)
                if m in (1, 3):
                    for t in range(NT):
                        last = pe.matmul(PS[:, 2 + t, 0:N], zero16[:], diag16[:, 0:N], start=False,
                                         stop=True)
                    last.then_inc(table_done, 1)

            pe.wait_ge(keys_zeroed, 2)
            pe.wait_ge(aprep, 3)
            pe.wait_ge(mask_step, 11)
            for s in range(2):
                pe.wait_ge(bank_free[s], 1 + 24)
            with pe.Fori(0, KB) as j:
                pe.wait_ge(mixv_ready, j + 1)
                column_job(0, B_BASE[0] + j, xT, 0)
                pe.wait_ge(v_in, j * 16 + 16)
                pe.wait_ge(o_summed, j * 2 + 1)
                for t in range(NT):
                    last = pe.transpose(PS[:, 7, t * P:(t + 1) * P], v_cur[:, t * P:(t + 1) * P], ident)
                last.then_inc(v_turned, 1)
                pe.wait_ge(ql_ready, j + 1)
                pe.wait_ge(kl_ready, j * 2 + 2)
                pe.wait_ge(mix_ready, j + 1)
                for h in range(2):
                    for t in range(NT):
                        pe.wait_ge(score_read, j * 6 + (1 + (t + 1 if h else 0)))
                        r = slice(t * P, (t + 1) * P)
                        pe.matmul(PS[:, 2 + t, 0:N], qh[:, r], kzh[h][:], start=True, stop=False)
                        pe.matmul(PS[:, 2 + t, 0:N], ql[:, r], kzh[h][:], start=False, stop=False)
                        pe.matmul(PS[:, 2 + t, 0:N], qh[:, r], kzl[h][:], start=False,
                                  stop=True).then_inc(score_done, 1)
                column_job(1, B_BASE[1] + j, xT, 1)

                def turn_probs(h):
                    pe.wait_ge(prob_ready, j * 6 + (3 * h + 3))
                    for m in range(NT):
                        bank = TURN_BANKS[m]
                        if h:
                            pe.wait_ge(pT_ready, j * 6 + (m + 1))
                        for t in range(NT):
                            last = pe.transpose(PS[:, bank, t * P:(t + 1) * P],
                                                prob[:, h, t, m * P:(m + 1) * P], ident)
                        last.then_inc(prob_turned, 1)

                def pv(h):
                    pe.wait_ge(pT_ready, j * 6 + (3 * h + 3))
                    for m in range(NT):
                        for part in range(2):
                            last = pe.matmul(PS[:, 7, 0:N], vs[:, m, h, :], probT[part][:, m, :],
                                             start=(m == 0 and part == 0), stop=(m == NT - 1 and part == 1))
                    last.then_inc(pv_done, 1)

                pe.wait_ge(score_read, j * 6 + 7)
                turn_probs(0)
                pe.wait_ge(sq_done, j * 2 + 1)
                column_job(2, B_BASE[2] + j, xT, 0, range(0, KB // 2))
                pe.wait_ge(vs_ready, j + 1)
                pv(0)
                pe.wait_ge(feat_ready, j + 1)
                pe.matmul(PS[:, 2, 0:N], head_ones[:], feat[0][:], start=True, stop=False)
                pe.matmul(PS[:, 2, 0:N], head_ones[:], feat[1][:], start=False, stop=True).then_inc(coeff_done, 1)
                turn_probs(1)
                column_job(2, B_BASE[2] + j, xT, 0, range(KB // 2, KB))
                pe.wait_ge(o_summed, j * 2 + 2)
                pv(1)

            with pe.Fori(0, 2) as half:
                for b in range(8):
                    pe.wait_ge(ol_ready if b >= 4 else ml_ready, KB)
                    row_block(b % 2, half * 4 + (C_BASE + b // 2), T1 if b < 4 else T0, half, b % 4,
                              b == 0, b == 7, c_done if b == 7 else None)
            pe.wait_ge(x2n_ready, 1)
            turn(0, x2_turned)
            pe.wait_ge(x2n_mid, 1)
            turn(1, x2_turned)
            pe.wait_ge(x2n_ready, 2)
            turn(2, x2_turned)
            pe.wait_ge(x2_done, NT)
            for half in range(2):
                for b in range(4):
                    row_block(b % 2, half * 2 + (E_BASE + b // 2), xT, half, b, b == 0, False)
                if half == 0:
                    pe.wait_ge(loss_step, 7)
                    pe.matmul(PS[:, 7, 0:EXPERTS], ones_f32, loss[:, 0, :], start=True, stop=True).then_inc(loss_sum, 1)
            pe.wait_ge(down_ready, 1)
            for k in range(KB):
                for part in range(2):
                    last = pe.matmul(PS[:, 7, 0:N], wd[:, k, :], xT[part][:, k, :],
                                     start=(k == 0 and part == 0), stop=(k == KB - 1 and part == 1))
            last.then_inc(hdown_done, 1)
            pe.wait_ge(aug_ready, 2)
            for b, (s, use) in enumerate(V_USES):
                half, kp = b // 4, b % 4
                o = PS[:, 6 + half, :]
                if b == 4:
                    pe.wait_ge(h_step, 1)
                pe.wait_ge(hi_ready[s], use + 1)
                for k2 in range(2):
                    for part in range(2):
                        pe.matmul(o, aug[part][:, 2 * kp + k2, :], w_hi[s][:, k2 * HALF:(k2 + 1) * HALF],
                                  start=(kp == 0 and k2 == 0 and part == 0), stop=False)
                pe.wait_ge(lo_ready[s], use + 2)
                for k2 in range(2):
                    last = pe.matmul(o, aug[0][:, 2 * kp + k2, :], w_lo[s][:, k2 * HALF:(k2 + 1) * HALF],
                                     start=False, stop=(kp == 3 and k2 == 1))
                last.then_inc(w_used[s], 1)
            pe.wait_ge(hT_ready, 1)
            pe.wait_ge(aug_zero, 3)
            for half in range(2):
                c = slice(half * HALF, (half + 1) * HALF)
                pe.wait_ge(pc_ready, half + 1)
                for t in range(NT):
                    r = slice(t * P, (t + 1) * P)
                    o = PS[:, 3 * half + t, :]
                    pe.matmul(o, hT[0][:, r], pc[0][:, c], start=False, stop=False)
                    pe.matmul(o, hT[1][:, r], pc[0][:, c], start=False, stop=False)
                    pe.matmul(o, hT[0][:, r], pc[1][:, c], start=False, stop=True).then_inc(y_done, 1)


def columns(w):
    return w.reshape(KB, P, KB, P).transpose(2, 1, 0, 3).reshape(KB, P, D)


def halves(w):
    return w.reshape(4, 2, P, 2, HALF).transpose(3, 0, 2, 1, 4).reshape(8, P, D)


def kernel(**inputs):
    import numpy as np
    import concourse.bacc as bacc
    from concourse.bass_utils import run_bass_kernel_spmd

    a = {k.replace("L0_", ""): np.asarray(v) for k, v in inputs.items()}
    first = [columns(a["gnn_" + n].T) for n in ("wq", "wk", "wiq", "wv", "wik", "wiv")]
    mixer = [columns(a["mix_" + n]) for n in ("Wq", "Wk", "Wv")]
    wo, mo = halves(a["gnn_wo"].T), halves(a["mix_Wo"])
    outs = [mo[0:4], wo[0:4], mo[4:8], wo[4:8]]
    weights = np.concatenate(first + mixer + outs + [halves(a["ffn_base_W"].T)])
    conv = np.concatenate([halves(a["ffn_conv_W"][e].T) for e in range(EXPERTS)])
    names = ["gnn_bq", "gnn_bk", "gnn_biq", "gnn_bv", "gnn_bik", "gnn_biv", "mix_bq", "mix_bk", "mix_bv"]
    disc = np.stack([a["ffn_disc_mu"], a["ffn_disc_sigma"]]).reshape(2, EXPERTS, KB, P)
    edges = [a["src"], a["dst"], a["edge_type_5"]]
    lane = np.arange(P)
    consts = np.zeros((P, C_ALL), np.float32)
    consts[:, C_ID:C_ID + P] = np.eye(P)
    consts[:, C_IOTA:C_IOTA + N] = np.arange(N)
    consts[:, C_TRI:C_TRI + P] = lane[None, :] > lane[:, None]
    consts[:, C_POW:C_POW + CH] = 2.0 ** (4.0 * (np.arange(CH) % GCH) - 95)
    consts[:, C_ONES:C_ONES + P] = lane[None, :] // HD == lane[:, None] // HD
    consts[:, C_EIDX:C_EIDX + EXPERTS] = np.arange(EXPERTS)
    consts[:, C_ONE:C_ONE + P] = 1.0
    arrays = {
        "x": a["x"],
        "weights": weights,
        "conv": conv,
        "down": a["ffn_down_W"].reshape(EXPERTS, KB, P, R).transpose(0, 2, 1, 3),
        "upT": a["ffn_up_W"].reshape(EXPERTS, R, KB, P).transpose(0, 3, 2, 1),
        "up_b": a["ffn_up_b"].reshape(EXPERTS, KB, P).transpose(0, 2, 1),
        "down_b": a["ffn_down_b"].reshape(EXPERTS, R, 1),
        "conv_b": a["ffn_conv_b"],
        "disc": disc.transpose(3, 0, 1, 2),
        "bias_cols": np.concatenate([a[n].reshape(KB, P) for n in names]).T,
        "rows": np.stack([a["gnn_bo"], a["mix_bo"], a["ffn_base_b"]]),
        "edge_weights": a["gnn_edge_type_weights"],
        "edge_rows": np.concatenate([e.reshape(CH, P) for e in edges[:2]], axis=1),
        "edge_cols": np.concatenate([e.reshape(CH, P).T for e in edges], axis=1),
        "consts": consts,
    }
    arrays = {k: np.ascontiguousarray(v) for k, v in arrays.items()}
    nc = bacc.Bacc("TRN2", target_bir_lowering=False, num_devices=1)
    args = {k: nc.dram_tensor(k, v.shape, mybir.dt.from_np(v.dtype), kind="ExternalInput").ap()
            for k, v in arrays.items()}
    out = nc.dram_tensor("out", (N, D), F32, kind="ExternalOutput").ap()
    gps_layer(nc, out=out, **args)
    r = run_bass_kernel_spmd(nc, [arrays], core_ids=[0])
    return r.results[0]["out"]
```

```python
from contextlib import ExitStack

import concourse.bass as bass
from concourse import mybir

F32 = mybir.dt.float32
F32R = mybir.dt.float32r
BF16 = mybir.dt.bfloat16
F16 = mybir.dt.float16
I32 = mybir.dt.int32
U32 = mybir.dt.uint32
ALU = mybir.AluOpType
ACT = mybir.ActivationFunctionType
X = mybir.AxisListType.X
ds = bass.ds

P = 128
N = 384
D = 1024
NT = N // P
KB = D // P
HD = 64
HALF = 512
E = 12288
CH = E // P
GCH = CH // 2
CJ = 3
EXPERTS = 8
R = 64
EPS = 1e-5
SCALE = 1.0 / HD ** 0.5
ABSENT = -1e30
SLOTS = 3

A_BASE = [4 * m for m in range(6)]
B_BASE = [24, 24, 0]
TAIL = [(b % 3, (32, 32, 8)[b % 3] + b // 3) for b in range(32)]
E_AT = [16, 17, 18, 19, 20, 21, 22, 26]
V_AT = [23, 24, 25, 27, 28, 29, 30, 31]
DVE_SPLITS = (25, 28, 30, 31)
C_USES, E_USES, V_USES = TAIL[:16], [TAIL[i] for i in E_AT], [TAIL[i] for i in V_AT]
SCORE_BANKS = ((2, 3, 4), (5, 6, 2))
TURN_BANKS = (5, 6, 4)
C_BANKS = ((3, 4, 5), (0, 1, 2))
E_BANKS = ((4, 5, 3), (0, 1, 2))
LN_BANKS = (6, 0, 2)

C_ID, C_IOTA, C_TRI, C_POW, C_ONES, C_EIDX, C_ONE, C_ALL = 0, 128, 512, 640, 736, 864, 872, 1000


def gps_layer(nc, x, out, weights, conv, down, upT, up_b, down_b, conv_b, disc, bias_cols,
              rows, edge_weights, edge_rows, edge_cols, consts):
    with ExitStack() as ctx:
        def sb(name, shape, dt):
            return ctx.enter_context(nc.sbuf_tensor(name, shape, dt))

        def sem(name):
            return ctx.enter_context(nc.semaphore(name))

        key_dram = nc.dram_tensor("key_dram", [CH, P], F32, kind="Internal").ap()

        raw = [sb(f"raw{s}", [P, D], F32) for s in range(SLOTS)]
        w_hi = [sb(f"w_hi{s}", [P, D], F32R) for s in range(SLOTS)]
        w_lo = [sb(f"w_lo{s}", [P, D], F32R) for s in range(SLOTS)]
        xT = [sb(f"xT_{c}", [P, KB, N], F32R) for c in ("hi", "lo")]
        T0 = [sb(f"T0_{c}", [P, KB, N], F32R) for c in ("hi", "lo")]
        T1 = [sb(f"T1_{c}", [P, KB, N], F32R) for c in ("hi", "lo")]
        Q2 = sb("Q2", [P, KB, N], F32)
        K2 = sb("K2", [P, KB, N], F32)
        V2 = sb("V2", [P, KB, N], F32)
        mask = sb("mask", [P, NT, N], F32)
        U = sb("U", [P, 6 * D], F32)
        x_rows = U[:, 0:NT * D].rearrange("p (t d) -> p t d", t=NT)
        xn_rows = U[:, NT * D:2 * NT * D].rearrange("p (t d) -> p t d", t=NT)
        src_hot = U[:, 0:CJ * N].bitcast(BF16).rearrange("p (s c n) -> p s c n", s=2, c=CJ)
        dst_hot = U[:, CJ * N:2 * CJ * N].bitcast(BF16).rearrange("p (s c n) -> p s c n", s=2, c=CJ)
        key_row = U[:, 3456:3456 + 2 * CJ * P].rearrange("p (s n) -> p s n", s=2)
        key_junk = U[:, 4224:4352]
        table2 = U[:, 0:NT * N].rearrange("p (t n) -> p t n", t=NT)
        codes = U[:, NT * N:2 * NT * N].rearrange("p (t n) -> p t n", t=NT)
        pick = U[:, 4608:4608 + NT * N].rearrange("p (t n) -> p t n", t=NT)
        prob = U[:, 0:2 * NT * N].rearrange("p (h t n) -> p h t n", h=2, t=NT)
        sq_q = U[:, 2304:2688]
        sq_k = U[:, 2688:3072]
        mix_v = U[:, 3072:3456]
        pv_low = U[:, 3456:3840]
        attn_o = U[:, 3840:4224]
        v_cur = U[:, 4224:4608]
        q_both = [sb(f"q_both{h}", [P, N], F32R) for h in range(2)]
        k_hi2 = [sb(f"k_hi2{h}", [P, N], F32R) for h in range(2)]
        k_lo0 = [sb(f"k_lo0{h}", [P, N], F32R) for h in range(2)]
        vs = sb("vs", [P, NT, 2, P], F32R)
        probT = [sb(f"probT_{c}", [P, NT, N], F32R) for c in ("hi", "lo")]
        feat = [sb(f"feat_{c}", [P, N], F32R) for c in ("hi", "lo")]
        cst = sb("cst", [P, C_ALL], F32)
        ident = cst[:, C_ID:C_ID + P]
        tri = cst[:, C_TRI:C_TRI + P]
        eidx = cst[:, C_EIDX:C_EIDX + EXPERTS]
        ones_f32 = cst[:, C_ONE:C_ONE + P]
        iota16 = sb("iota16", [P, N], F16)
        zero16 = sb("zero16", [P, P], BF16)
        head_ones = sb("head_ones", [P, P], F32R)
        bias = sb("bias", [P, 9 * KB], F32)
        ew = sb("ew", [P, 4], F32)
        ew_t = sb("ew_t", [P, 8], F32)
        v2f = V2[:].rearrange("p k n -> p (k n)")
        erow_i = v2f[0:CH, 0:2 * P].bitcast(I32)
        erow = v2f[0:CH, 2 * P:4 * P]
        ecol_i = v2f[:, 4 * P:4 * P + 3 * CH].bitcast(I32)
        ecol = sb("ecol", [P, 3 * CH], F32)
        ekey = sb("ekey", [P, CH], F32)
        etype = sb("etype", [P, CH], F32)
        digit = [etype[:]] + [v2f[:, 1024 + c * CH:1024 + (c + 1) * CH] for c in range(4)]
        diag16 = v2f[:, 1408:1408 + 320].bitcast(BF16)
        diag_w = v2f[:, 1728:1728 + 64].bitcast(BF16)
        dup = sb("dup", [P, CH], F32)
        live_w = sb("live_w", [P, CH], F32)
        stats = sb("stats", [P, NT, 2, 6], F32)
        mv = sb("mv", [P, NT, 2], F32)
        rstd = sb("rstd", [P, 4, NT], F32)
        smax = sb("smax", [P, 2, NT], F32)
        nmax = sb("nmax", [P, 2, NT], F32)
        ssum = sb("ssum", [P, 2, NT], F32)
        rsum = sb("rsum", [P, 2, NT], F32)
        tiny = sb("tiny", [P, 24], F32)
        PS = ctx.enter_context(nc.psum_tensor("PS", [P, 8, HALF], F32))

        row_bo = Q2[:].rearrange("p k n -> p (k n)")[:, 0:3 * D].rearrange("p (r d) -> p r d", r=3)
        k2f = K2[:].rearrange("p k n -> p (k n)")
        conv_row = k2f[:, 0:D]
        raw_down = k2f[:, D:D + KB * R].rearrange("p (k r) -> p k r", k=KB)
        raw_up = k2f[:, D + 512:D + 512 + KB * R].rearrange("p (k r) -> p k r", k=KB)
        raw_upb = k2f[:, 2 * D:2 * D + KB]
        raw_downb = k2f[:, 2 * D + 8:2 * D + 9]
        h_low = k2f[:, 2 * D + 16:2 * D + 16 + N]
        h_sum = k2f[:, 2 * D + 400:2 * D + 400 + N]
        xn_T = V2[:]
        sq_junk = k2f[:, 2 * D + 16:2 * D + 16 + N]
        t0h = T0[0][:].rearrange("p k n -> p (k n)")
        t0l = T0[1][:].rearrange("p k n -> p (k n)")
        wd = t0h[:, 0:KB * P].rearrange("p (k m) -> p k m", k=KB)
        hT = [t0h[:, D:D + N], t0h[:, D + N:D + 2 * N]]
        aug = [t0l[:, c * D:(c + 1) * D].rearrange("p (k m) -> p k m", k=KB) for c in range(2)]
        pc = [T1[c][:].rearrange("p k n -> p (k n)")[:, 0:D] for c in range(2)]
        disc_in = sb("disc_in", [P, 2, EXPERTS, KB], F32)
        dterm = sb("dterm", [P, 5, EXPERTS, KB], F32)
        moments = sb("moments", [P, 4, KB], F32)
        loss = sb("loss", [P, 5, EXPERTS], F32)
        pick_i = sb("pick_i", [P, 1], I32)

        w_in = [sem(f"w_in{s}") for s in range(SLOTS)]
        hi_ready = [sem(f"hi_ready{s}") for s in range(SLOTS)]
        lo_ready = [sem(f"lo_ready{s}") for s in range(SLOTS)]
        w_used = [sem(f"w_used{s}") for s in range(SLOTS)]
        keys_zeroed = sem("keys_zeroed")
        cst_in = sem("cst_in")
        const_in = sem("const_in")
        edges_in = sem("edges_in")
        x_in = [sem(f"x_in{t}") for t in range(NT)]
        key_out = sem("key_out")
        key_calc = sem("key_calc")
        key_in = [sem(f"key_in{s}") for s in range(2)]
        prep = sem("prep")
        aprep = sem("aprep")
        norm_step = sem("norm_step")
        var_ready = sem("var_ready")
        rstd_guess = sem("rstd_guess")
        rstd_ready = sem("rstd_ready")
        xn_ready = sem("xn_ready")
        xn_mid = sem("xn_mid")
        xt_turned = sem("xt_turned")
        xt_hi = sem("xt_hi")
        xt_done = sem("xt_done")
        evac_hi = sem("evac_hi")
        bank_free = [sem(f"bank_free{s}") for s in range(2)]
        dup_ready = sem("dup_ready")
        live_ready = sem("live_ready")
        hot_ready = sem("hot_ready")
        hot_used = sem("hot_used")
        table_done = sem("table_done")
        table1_read = sem("table1_read")
        table2_read = sem("table2_read")
        mask_step = sem("mask_step")
        v_in = sem("v_in")
        v_turned = sem("v_turned")
        vh_ready = sem("vh_ready")
        vs_ready = sem("vs_ready")
        qk_hi = sem("qk_hi")
        k_flipped = sem("k_flipped")
        ql_ready = sem("ql_ready")
        kl_ready = sem("kl_ready")
        score_done = sem("score_done")
        score_read = sem("score_read")
        nmax_ready = sem("nmax_ready")
        exp_done = sem("exp_done")
        recip_done = sem("recip_done")
        prob_ready = sem("prob_ready")
        prob_turned = sem("prob_turned")
        pT_hi = sem("pT_hi")
        pT_ready = sem("pT_ready")
        pv_done = sem("pv_done")
        pv_copied = sem("pv_copied")
        o_summed = sem("o_summed")
        oh_ready = sem("oh_ready")
        ol_ready = sem("ol_ready")
        sq_done = sem("sq_done")
        k_step = sem("k_step")
        sq_summed = sem("sq_summed")
        feat_exp = sem("feat_exp")
        feat_hi = sem("feat_hi")
        feat_ready = sem("feat_ready")
        coeff_done = sem("coeff_done")
        mixv_ready = sem("mixv_ready")
        mix_ready = sem("mix_ready")
        mh_ready = sem("mh_ready")
        ml_ready = sem("ml_ready")
        rows_in = sem("rows_in")
        xr_in = sem("xr_in")
        res_ready = sem("res_ready")
        c_done = sem("c_done")
        x2_ready = sem("x2_ready")
        x2n_ready = sem("x2n_ready")
        x2n_mid = sem("x2n_mid")
        x2_turned = sem("x2_turned")
        x2_hi = sem("x2_hi")
        x2_done = sem("x2_done")
        x2_copied = sem("x2_copied")
        moment_done = sem("moment_done")
        loss_step = sem("loss_step")
        loss_sum = sem("loss_sum")
        idx_ready = sem("idx_ready")
        small_in = sem("small_in")
        convb_in = sem("convb_in")
        down_hi = sem("down_hi")
        down_ready = sem("down_ready")
        aug_hi = sem("aug_hi")
        aug_ready = sem("aug_ready")
        aug_zero = sem("aug_zero")
        hdown_done = sem("hdown_done")
        hlow_ready = sem("hlow_ready")
        h_step = sem("h_step")
        hT_hi = sem("hT_hi")
        hT_ready = sem("hT_ready")
        pc_hi = sem("pc_hi")
        pc_ready = sem("pc_ready")
        y_done = sem("y_done")
        y_ready = sem("y_ready")
        stored = sem("stored")

        block = ctx.enter_context(nc.Block())

        @block.sync
        def _(sp):
            def load_weights(slot, use, src):
                sp.wait_ge(lo_ready[slot], use + 1)
                sp.dma_start(raw[slot][:], src).then_inc(w_in[slot], 16)

            for t in range(NT):
                sp.dma_start(x_rows[:, t, :], x[t * P:(t + 1) * P, :]).then_inc(x_in[t], 16)
            for m in range(6):
                with sp.Fori(0, KB // 2) as i:
                    for s in range(2):
                        load_weights(s, A_BASE[m] + i, weights[ds(i * 2 + (8 * m + s), 1)]
                                     .rearrange("a p n -> (a p) n"))
                    if m < 4:
                        for s in range(2):
                            sp.wait_ge(key_out, 16)
                            sp.wait_ge(xt_done, NT)
                            sp.wait_ge(live_ready, i * 2 + (8 * m + s + 1))
                            sp.dma_start(key_row[:, s, :],
                                         key_dram[ds(i * 2 * CJ + CJ * (8 * m + s), CJ), :]
                                         .rearrange("c e -> (c e)").partition_broadcast(P)
                                         ).then_inc(key_in[s], 16)
            with sp.Fori(0, KB) as j:
                load_weights(0, B_BASE[0] + j, weights[ds(j + 48, 1)].rearrange("a p n -> (a p) n"))
                sp.wait_ge(v_turned, j + 1)
                for s in range(2):
                    sp.wait_ge(bank_free[s], 1 + 24)
                sp.dma_start(v_cur, V2[:, ds(j, 1), :].rearrange("p a n -> p (a n)")).then_inc(v_in, 16)
                for t in (1, 2):
                    load_weights(t, B_BASE[t] + j, weights[ds(j + (48 + 8 * t), 1)]
                                 .rearrange("a p n -> (a p) n"))
            for b, (s, use) in enumerate(C_USES + E_USES[:7]):
                load_weights(s, use, weights[72 + b])
            sp.wait_ge(idx_ready, 1)
            expert = sp.value_load(pick_i[0:1, 0:1], min_val=0, max_val=EXPERTS - 1)
            sp.dma_start(raw_down, down[ds(expert, 1)].rearrange("a p k r -> (a p) k r")).then_inc(small_in, 16)
            sp.dma_start(raw_up, upT[ds(expert, 1)].rearrange("a p k r -> (a p) k r")).then_inc(small_in, 16)
            sp.dma_start(raw_upb, up_b[ds(expert, 1)].rearrange("a p k -> (a p) k")).then_inc(small_in, 16)
            sp.dma_start(raw_downb[0:R, :], down_b[ds(expert, 1)].rearrange("a r o -> (a r) o")).then_inc(small_in, 16)
            for b, (s, use) in enumerate(V_USES):
                if b == 3:
                    sp.dma_start(conv_row, conv_b[ds(expert, 1)].rearrange("a d -> (a d)").partition_broadcast(P)
                                 ).then_inc(convb_in, 16)
                    load_weights(*E_USES[7], weights[72 + 23])
                load_weights(s, use, conv[ds(expert * 8 + b, 1)].rearrange("a p n -> (a p) n"))
            for half in range(2):
                c = slice(half * HALF, (half + 1) * HALF)
                for t in range(NT):
                    sp.wait_ge(y_ready, half * NT + t + 1)
                    sp.dma_start(out[t * P:(t + 1) * P, c], x_rows[:, t, c]).then_inc(stored, 16)
            sp.wait_ge(stored, 16 * 2 * NT)

        @block.gpsimd
        def _(pool):
            def split_lo(slot, use):
                pool.wait_ge(hi_ready[slot], use + 1)
                pool.tensor_tensor(w_lo[slot][:], raw[slot][:], w_hi[slot][:].bitcast(F32),
                                   ALU.subtract).then_inc(lo_ready[slot], 1)

            given = [(lo_ready[s], 1) for s in range(SLOTS)] + [(w_used[s], 1) for s in range(SLOTS)] + [
                (live_ready, 2), (bank_free[0], 1), (bank_free[1], 1), (hot_used, 2), (v_turned, 1), (score_read, 1),
                (mixv_ready, 1), (mix_ready, 1), (o_summed, 1)]
            for n, (s, k) in enumerate(given):
                pool.memset(tiny[:, n:n + 1], 0.0).then_inc(s, k)
            split_lo(0, 0)
            pool.wait_ge(key_calc, 1)
            pool.dma_start(key_dram, erow[:, 0:P]).then_inc(key_out, 16)
            for m in range(6):
                with pool.Fori(0, KB // 2) as i:
                    split_lo(1, A_BASE[m] + i)
                    split_lo(0, A_BASE[m] + i + 1)
            def flip_k(j):
                pool.wait_ge(lo_ready[0], B_BASE[0] + j + 2)
                for h in range(2):
                    pool.tensor_copy(k_hi2[h][64 * (1 - h):64 * (2 - h), :],
                                     K2[64 * h:64 * h + 64, ds(j, 1), :].rearrange("p a n -> p (a n)")
                                     ).then_inc(k_flipped, 1)
                    pool.wait_ge(k_flipped, j * 2 + (h + 1))

            def pair(j, last):
                split_lo(1, B_BASE[1] + j)
                split_lo(2, B_BASE[2] + j)
                pool.wait_ge(feat_hi, j + 1)
                pool.tensor_tensor(feat[1][:], sq_q, feat[0][:].bitcast(F32),
                                   ALU.subtract).then_inc(feat_ready, 1)
                split_lo(0, B_BASE[0] + j + 1)
                if not last:
                    pool.wait_ge(score_done, j * 6 + 6)
                    flip_k(j + 1)

            for s in range(2):
                pool.wait_ge(bank_free[s], 1 + 24)
            flip_k(0)
            with pool.Fori(0, KB - 1) as j:
                pair(j, False)
            pair(KB - 1, True)
            pool.wait_ge(ql_ready, 2 * KB)
            pool.dma_start(row_bo, rows.partition_broadcast(P)).then_inc(rows_in, 16)
            pool.wait_ge(ol_ready, KB)
            pool.wait_ge(ml_ready, KB)
            pool.dma_start(x_rows, x.rearrange("(t p) d -> p t d", p=P)).then_inc(xr_in, 16)
            for b in range(1, 32):
                if b not in DVE_SPLITS:
                    split_lo(*TAIL[b])

        @block.scalar
        def _(act):
            def split_hi(slot, use):
                act.wait_ge(w_in[slot], use * 16 + 16)
                act.wait_ge(w_used[slot], use + 1)
                act.activation(w_hi[slot][:], raw[slot][:], ACT.Copy).then_inc(hi_ready[slot], 1)

            def guess_rstd(n):
                t = n % NT
                act.wait_ge(var_ready, n + 1)
                act.activation(rstd[:, 1, t:t + 1], rstd[:, 0, t:t + 1], ACT.Sqrt).then_inc(rstd_guess, 1)

            def norm_rows(which, done):
                guess_rstd(NT * which)
                if which:
                    split_hi(*E_USES[1])
                guess_rstd(NT * which + 1)
                act.wait_ge(rstd_ready, NT * which + 2)
                act.activation(xn_rows[:, 1, :], x_rows[:, 1, :], ACT.Identity, scale=rstd[:, 2, 1:2],
                               bias=rstd[:, 3, 1:2]).then_inc(done, 1)
                guess_rstd(NT * which + 2)

            def turned(t):
                b = LN_BANKS[t]
                return PS[:, b:b + 2, :].rearrange("p b (k n) -> p (b k) n", k=4), slice(t * P, (t + 1) * P)

            act.dma_start(cst[:], consts).then_inc(cst_in, 16)
            act.dma_start(ew[:], edge_weights.partition_broadcast(P)).then_inc(const_in, 16)
            act.dma_start(erow_i, edge_rows).then_inc(edges_in, 16)
            act.dma_start(ecol_i, edge_cols).then_inc(edges_in, 16)
            act.dma_start(bias[:], bias_cols).then_inc(const_in, 16)
            act.dma_start(disc_in[:], disc).then_inc(const_in, 16)
            norm_rows(0, xn_mid)
            split_hi(0, 0)
            for t in range(NT):
                act.wait_ge(xt_turned, t + 1)
                src, r = turned(t)
                act.activation(xT[0][:, :, r], src, ACT.Copy).then_inc(xt_hi, 1)

            def table_out(dst, done):
                for t in range(NT):
                    last = act.activation(dst[:, t, :], PS[:, 2 + t, 0:N], ACT.Copy)
                last.then_inc(done, 1)

            act.wait_ge(const_in, 48)
            for m in range(6):
                dst = [T0, T1, Q2, T0, K2, V2][m]
                with act.Fori(0, KB // 2) as i:
                    for s in range(2):
                        split_hi(1 - s, A_BASE[m] + i + s)
                        act.wait_ge(w_used[s], A_BASE[m] + i + 2)
                        plain = m in (2, 4, 5)
                        act.activation((dst if plain else dst[0])[:, ds(i * 2 + s, 1), :]
                                       .rearrange("p a n -> p (a n)"), PS[:, s, 0:N], ACT.Identity,
                                       bias=bias[:, ds(i * 2 + (8 * m + s), 1)]
                                       ).then_inc(bank_free[s] if plain else evac_hi, 1)
                if m == 0:
                    act.wait_ge(prep, 9)
                    act.activation(ew_t[:, 0:4], ew_t[:, 0:4], ACT.Exp).then_inc(aprep, 1)
                    act.wait_ge(aprep, 1)
                    act.activation(ew_t[:, 0:4], ew_t[:, 0:4], ACT.Ln, bias=1.0).then_inc(aprep, 1)
                    act.wait_ge(cst_in, 16)
                    act.activation(head_ones[:], cst[:, C_ONES:C_ONES + P], ACT.Copy).then_inc(aprep, 1)
                if m == 1:
                    act.wait_ge(table_done, 1)
                    table_out(mask, table1_read)
                if m == 3:
                    act.wait_ge(table_done, 2)
                    table_out(table2, table2_read)

            def split_qk(j):
                own = [slice(64 * h, 64 * h + 64) for h in range(2)]
                for dst, src in ((q_both, Q2), (k_hi2, K2)):
                    for h in range(2):
                        act.activation(dst[h][own[h], :],
                                       src[own[h], ds(j, 1), :].rearrange("p a n -> p (a n)"),
                                       ACT.Copy).then_inc(qk_hi, 1)

            def pair(j, last):
                split_hi(1, B_BASE[1] + j)
                act.wait_ge(w_used[0], B_BASE[0] + j + 2)
                act.activation(sq_q, PS[:, 0, 0:N], ACT.Square, bias=bias[:, ds(j + 6 * KB, 1)]).then_inc(sq_done, 1)
                act.wait_ge(v_turned, j + 2)
                act.activation(vs[:, :, :, 0:HD], PS[:, 7, 0:N].rearrange("p (t h d) -> p t h d", t=NT, h=2),
                               ACT.Copy).then_inc(vh_ready, 1)
                for h in range(2):
                    act.wait_ge(nmax_ready, j * 2 + (h + 1))
                    for t in range(NT):
                        act.activation(prob[:, h, t, :], prob[:, h, t, :], ACT.Exp, bias=nmax[:, h, t:t + 1],
                                       scale=SCALE, accum_out=ssum[:, h, t:t + 1]).then_inc(exp_done, 1)
                    if h == 0:
                        split_hi(2, B_BASE[2] + j)

                def turned_hi(h):
                    for t in range(NT):
                        act.wait_ge(prob_turned, j * 6 + (3 * h + t + 1))
                        if h:
                            act.wait_ge(pv_done, j * 2 + 1)
                        act.activation(probT[0][:, t, :], PS[:, TURN_BANKS[t], 0:N], ACT.Copy).then_inc(pT_hi, 1)

                def pv_copy(h):
                    act.wait_ge(pv_done, j * 2 + (h + 1))
                    rows_in_psum = slice(64 * (1 - h), 64 * (1 - h) + 64)
                    act.activation(pv_low[64 * h:64 * h + 64, :], PS[rows_in_psum, 7, 0:N],
                                   ACT.Copy).then_inc(pv_copied, 1)

                turned_hi(0)
                act.wait_ge(sq_summed, j + 1)
                act.activation(sq_q, sq_q, ACT.Exp, scale=-0.5).then_inc(feat_exp, 1)
                act.wait_ge(feat_exp, j + 1)
                act.activation(feat[0][:], sq_q, ACT.Copy).then_inc(feat_hi, 1)
                split_hi(0, B_BASE[0] + j + 1)
                pv_copy(0)
                turned_hi(1)
                if not last:
                    split_qk(j + 1)
                act.wait_ge(w_used[2], B_BASE[2] + j + 2)
                act.activation(mix_v, PS[:, 0, 0:N], ACT.Identity, bias=bias[:, ds(j + 8 * KB, 1)]).then_inc(mixv_ready, 1)
                act.wait_ge(mix_ready, j + 2)
                act.activation(T1[0][:, ds(j, 1), :].rearrange("p a n -> p (a n)"), mix_v, ACT.Copy).then_inc(mh_ready, 1)
                pv_copy(1)
                act.wait_ge(o_summed, j * 2 + 3)
                act.activation(T0[0][:, ds(j, 1), :].rearrange("p a n -> p (a n)"), attn_o, ACT.Copy).then_inc(oh_ready, 1)

            for s in range(2):
                act.wait_ge(bank_free[s], 1 + 24)
            split_qk(0)
            with act.Fori(0, KB - 1) as j:
                pair(j, False)
            pair(KB - 1, True)

            for b in range(1, 17):
                split_hi(*TAIL[b])
            norm_rows(1, x2n_mid)
            for t in range(NT):
                act.wait_ge(x2_turned, t + 1)
                src, r = turned(t)
                act.activation(xT[0][:, :, r], src, ACT.Copy).then_inc(x2_hi, 1)
            for t in range(NT):
                act.wait_ge(x2_done, t + 1)
                src, r = turned(t)
                act.activation(xn_T[:, :, r], src, ACT.Copy).then_inc(x2_copied, 1)
            for b in range(18, 30):
                split_hi(*TAIL[b])
            act.wait_ge(hdown_done, 1)
            act.activation(h_low[0:R, :], PS[R:2 * R, 7, 0:N], ACT.Copy).then_inc(hlow_ready, 1)
            act.wait_ge(h_step, 2)
            act.activation(hT[0][0:R, :], h_sum[0:R, :], ACT.Copy).then_inc(hT_hi, 1)
            split_hi(*TAIL[30])
            act.wait_ge(w_used[V_USES[3][0]], V_USES[3][1] + 2)
            act.activation(pc[0][:, 0:HALF], PS[:, 6, :], ACT.Copy).then_inc(pc_hi, 1)
            split_hi(*TAIL[31])
            act.wait_ge(w_used[V_USES[7][0]], V_USES[7][1] + 2)
            act.activation(pc[0][:, HALF:D], PS[:, 7, :], ACT.Copy).then_inc(pc_hi, 1)

        @block.vector
        def _(dve):
            for h in range(2):
                z = slice(64 * (1 - h), 64 * (1 - h) + 64)
                dve.memset(k_lo0[h][z, :].bitcast(F32), 0.0).then_inc(keys_zeroed, 1)
            dve.memset(zero16[:], 0.0)
            dve.memset(diag16, 0.0).then_inc(prep, 1)
            normed = [0]

            def step(ins):
                normed[0] += 1
                ins.then_inc(norm_step, 1)
                dve.wait_ge(norm_step, normed[0])

            def row_stats(which, t):
                for c in range(2):
                    dve.bn_stats(stats[:, t, c, :], x_rows[:, t, c * HALF:(c + 1) * HALF]).then_inc(norm_step, 1)
                normed[0] += 2
                dve.wait_ge(norm_step, normed[0])
                step(dve.bn_aggr(mv[:, t, :], stats[:, t, :, :].rearrange("p c s -> p (c s)")))
                dve.tensor_scalar(rstd[:, 0, t:t + 1], mv[:, t, 1:2], EPS, None, ALU.add).then_inc(var_ready, 1)

            def row_norm(which, t, done):
                v, y, z, m = (rstd[:, c, t:t + 1] for c in range(4))
                dve.wait_ge(rstd_guess, NT * which + t + 1)
                step(dve.reciprocal(y, y))
                step(dve.tensor_tensor(z, y, y, ALU.mult))
                step(dve.tensor_tensor(z, z, v, ALU.mult))
                step(dve.tensor_scalar(z, z, -0.5, 1.5, ALU.mult, ALU.add))
                step(dve.tensor_tensor(z, z, y, ALU.mult))
                dve.scalar_tensor_tensor(out=m, in0=mv[:, t, 0:1], scalar=-1.0, in1=z,
                                         op0=ALU.mult, op1=ALU.mult).then_inc(rstd_ready, 1)
                if t != 1:
                    dve.tensor_scalar(xn_rows[:, t, :], x_rows[:, t, :], mv[:, t, 0:1], z,
                                      ALU.subtract, ALU.mult).then_inc(done, 1)

            def turned(t):
                b = LN_BANKS[t]
                return PS[:, b:b + 2, :].rearrange("p b (k n) -> p (b k) n", k=4), slice(t * P, (t + 1) * P)

            dve.wait_ge(x_in[0], 16)
            row_stats(0, 0)
            dve.wait_ge(cst_in, 16)
            dve.tensor_copy(iota16[:], cst[:, C_IOTA:C_IOTA + N]).then_inc(prep, 1)
            dve.tensor_scalar(diag_w, ident, 2.0 ** -96, None, ALU.mult).then_inc(prep, 1)
            dve.wait_ge(prep, 3)
            dve.tensor_copy(diag16[:, 2 * P:3 * P], ident).then_inc(prep, 1)
            dve.wait_ge(x_in[1], 16)
            row_stats(0, 1)
            row_norm(0, 0, xn_ready)
            row_norm(0, 1, xn_ready)
            dve.wait_ge(x_in[2], 16)
            row_stats(0, 2)
            row_norm(0, 2, xn_ready)
            dve.wait_ge(edges_in, 32)
            dve.tensor_copy(erow, erow_i).then_inc(prep, 1)
            dve.tensor_copy(ecol[:], ecol_i).then_inc(prep, 1)
            dve.wait_ge(prep, 6)
            dve.scalar_tensor_tensor(out=erow[:, 0:P], in0=erow[:, 0:P], scalar=float(N), in1=erow[:, P:2 * P],
                                     op0=ALU.mult, op1=ALU.add).then_inc(key_calc, 1)
            for t in range(NT):
                dve.wait_ge(xt_hi, t + 1)
                src, r = turned(t)
                dve.tensor_tensor(xT[1][:, :, r], src, xT[0][:, :, r].bitcast(F32),
                                  ALU.subtract).then_inc(xt_done, 1)
            dve.wait_ge(const_in, 48)
            dve.tensor_scalar(ew_t[:, 0:4], ew[:], -1.0, None, ALU.mult).then_inc(prep, 1)
            dve.wait_ge(prep, 7)
            dve.tensor_tensor(ew_t[:, 0:4], ew_t[:, 0:4], ew[:], ALU.min).then_inc(prep, 1)
            dve.tensor_scalar(ew_t[:, 4:8], ew[:], 0.0, None, ALU.max).then_inc(prep, 1)
            src_c, dst_c, type_c = (ecol[:, c * CH:(c + 1) * CH] for c in range(3))
            dve.scalar_tensor_tensor(out=ekey[:], in0=src_c, scalar=float(N), in1=dst_c,
                                     op0=ALU.mult, op1=ALU.add).then_inc(prep, 1)
            dve.tensor_scalar(digit[0], type_c, 1.0, 1.0, ALU.is_equal, ALU.mult).then_inc(prep, 1)
            dve.tensor_scalar(digit[1], type_c, 2.0, 2.0, ALU.is_equal, ALU.mult).then_inc(prep, 1)
            dve.tensor_scalar(digit[2], type_c, 3.0, 4.0, ALU.is_equal, ALU.mult).then_inc(prep, 1)
            dve.tensor_scalar(digit[3], type_c, 4.0, 8.0, ALU.is_ge, ALU.mult).then_inc(prep, 1)
            dve.tensor_scalar(digit[4], type_c, 0.0, 8.0, ALU.is_le, ALU.mult).then_inc(prep, 1)
            for c in range(1, 5):
                dve.wait_ge(prep, 14 + c)
                dve.tensor_tensor(digit[0], digit[0], digit[c], ALU.add).then_inc(prep, 1)
            dve.wait_ge(prep, 19)
            dve.tensor_tensor(digit[0], digit[0], cst[:, C_POW:C_POW + CH], ALU.mult).then_inc(prep, 1)
            mu, sg = disc_in[:, 0], disc_in[:, 1]
            dve.tensor_tensor(dterm[:, 3], sg, sg, ALU.mult).then_inc(prep, 1)
            dve.wait_ge(prep, 21)
            dve.reciprocal(dterm[:, 0], dterm[:, 3]).then_inc(prep, 1)
            dve.wait_ge(prep, 22)
            dve.tensor_tensor(dterm[:, 1], dterm[:, 0], mu, ALU.mult).then_inc(prep, 1)
            dve.wait_ge(prep, 23)
            dve.tensor_tensor(dterm[:, 2], dterm[:, 1], mu, ALU.mult).then_inc(prep, 1)
            dve.wait_ge(prep, 24)
            for m in range(4):
                dst = [T0, T1, None, T0][m]
                splits_before = [0, 8, 0, 16][m]
                with dve.Fori(0, KB // 2) as i:
                    for s in range(2):
                        job = i * 2 + (8 * m + s)
                        ch0 = i * 2 * CJ + CJ * (8 * m + s)
                        dve.wait_ge(key_in[s], i * 16 + (64 * m + 16))
                        for c in range(CJ):
                            if c:
                                dve.wait_ge(dup_ready, job * CJ + c)
                            dve.scalar_tensor_tensor(
                                out=key_junk, in0=key_row[:, s, c * P:(c + 1) * P], scalar=ekey[:, ds(ch0 + c, 1)],
                                in1=tri, op0=ALU.is_equal, op1=ALU.mult,
                                accum_out=dup[:, ds(ch0 + c, 1)]).then_inc(dup_ready, 1)
                        dve.wait_ge(dup_ready, job * CJ + CJ)
                        these = ds(ch0, CJ)
                        dve.scalar_tensor_tensor(out=live_w[:, these], in0=dup[:, these], scalar=0.0,
                                                 in1=etype[:, these], op0=ALU.is_equal,
                                                 op1=ALU.mult).then_inc(live_ready, 1)
                        dve.wait_ge(hot_used, job + 1)
                        for c in range(CJ):
                            dve.tensor_scalar(dst_hot[:, s, c, :], iota16[:], ecol[:, ds(ch0 + (c + CH), 1)], None,
                                              ALU.is_equal).then_inc(hot_ready, 1)
                        dve.wait_ge(live_ready, job + 3)
                        for c in range(CJ):
                            dve.tensor_scalar(src_hot[:, s, c, :], iota16[:], ecol[:, ds(ch0 + c, 1)],
                                              live_w[:, ds(ch0 + c, 1)], ALU.is_equal,
                                              ALU.mult).then_inc(hot_ready, 1)
                        if dst:
                            dve.wait_ge(evac_hi, i * 2 + (splits_before + s + 1))
                            j1 = ds(i * 2 + s, 1)
                            dve.scalar_tensor_tensor(
                                out=dst[1][:, j1, :].rearrange("p a n -> p (a n)"), in0=PS[:, s, 0:N],
                                scalar=bias[:, ds(job, 1)],
                                in1=dst[0][:, j1, :].rearrange("p a n -> p (a n)").bitcast(F32),
                                op0=ALU.add, op1=ALU.subtract).then_inc(bank_free[s], 1)
            dve.wait_ge(table2_read, 1)
            dve.wait_ge(table1_read, 1)
            dve.wait_ge(aprep, 2)
            dve.tensor_tensor(ew[:], ew_t[:, 0:4], ew_t[:, 4:8], ALU.add).then_inc(prep, 1)
            dve.wait_ge(prep, 25)
            dve.tensor_scalar(ew[:], ew[:], 1.0 / SCALE, None, ALU.mult).then_inc(prep, 1)
            dve.wait_ge(prep, 26)
            masks = [0]

            def masked(ins):
                masks[0] += 1
                ins.then_inc(mask_step, 1)
                dve.wait_ge(mask_step, masks[0])

            for t in range(NT):
                last = dve.copy_predicated(mask[:, t, :], PS[:, 2 + t, 0:N].bitcast(U32), table2[:, t, :])
            masked(last)
            masked(dve.tensor_scalar(codes.bitcast(I32), mask[:].bitcast(I32), 23, 3,
                                     ALU.logical_shift_right, ALU.bitwise_and))
            masked(dve.tensor_scalar(mask[:], mask[:], 0.0, ABSENT, ALU.is_equal, ALU.mult))
            for w in range(4):
                masked(dve.tensor_scalar(pick, codes.bitcast(I32), float(w), ew[:, w:w + 1],
                                         ALU.is_equal, ALU.mult))
                masked(dve.tensor_tensor(mask[:], mask[:], pick, ALU.add))

            def split_qk(j):
                own = [slice(64 * h, 64 * h + 64) for h in range(2)]
                for h in range(2):
                    dve.wait_ge(qk_hi, j * 4 + (h + 1))
                    dve.tensor_tensor(q_both[h][own[1 - h], :], Q2[own[h], ds(j, 1), :].rearrange("p a n -> p (a n)"),
                                      q_both[h][own[h], :].bitcast(F32), ALU.subtract).then_inc(ql_ready, 1)
                for h in range(2):
                    dve.wait_ge(qk_hi, j * 4 + (h + 3))
                    dve.tensor_tensor(k_lo0[h][own[h], :], K2[own[h], ds(j, 1), :].rearrange("p a n -> p (a n)"),
                                      k_hi2[h][own[h], :].bitcast(F32), ALU.subtract).then_inc(kl_ready, 1)

            def pair(j, last):
                def softmax_in(h):
                    for t in range(NT):
                        dve.wait_ge(score_done, j * 6 + (3 * h + t + 1))
                        dve.memset(tiny[:, 16 + 3 * h + t:17 + 3 * h + t], 0.0)
                        dve.tensor_tensor_reduce(prob[:, h, t, :], PS[:, SCORE_BANKS[h][t], 0:N], mask[:, t, :], 1.0,
                                                 3.0 * ABSENT, ALU.add, ALU.max,
                                                 smax[:, h, t:t + 1]).then_inc(score_read, 1)
                    dve.wait_ge(score_read, j * 6 + (3 * h + 4))
                    dve.tensor_scalar(nmax[:, h, :], smax[:, h, :], -SCALE, None, ALU.mult).then_inc(nmax_ready, 1)

                def normalise(h):
                    dve.wait_ge(exp_done, j * 6 + (3 * h + 3))
                    dve.reciprocal(rsum[:, h, :], ssum[:, h, :]).then_inc(recip_done, 1)
                    dve.wait_ge(recip_done, j * 2 + (h + 1))
                    for t in range(NT):
                        dve.tensor_scalar(prob[:, h, t, :], prob[:, h, t, :], rsum[:, h, t:t + 1], None,
                                          ALU.mult).then_inc(prob_ready, 1)

                def turned_lo(h):
                    for t in range(NT):
                        dve.wait_ge(pT_hi, j * 6 + (3 * h + t + 1))
                        dve.tensor_tensor(probT[1][:, t, :], PS[:, TURN_BANKS[t], 0:N],
                                          probT[0][:, t, :].bitcast(F32), ALU.subtract).then_inc(pT_ready, 1)

                def pv_sum(h):
                    r = slice(64 * h, 64 * h + 64)
                    dve.wait_ge(pv_copied, j * 2 + (h + 1))
                    dve.tensor_tensor(attn_o[r, :], PS[r, 7, 0:N], pv_low[r, :], ALU.add).then_inc(o_summed, 1)

                softmax_in(0)
                softmax_in(1)
                dve.wait_ge(vh_ready, j + 1)
                dve.tensor_tensor(vs[:, :, :, HD:P], PS[:, 7, 0:N].rearrange("p (t h d) -> p t h d", t=NT, h=2),
                                  vs[:, :, :, 0:HD].bitcast(F32), ALU.subtract).then_inc(vs_ready, 1)
                normalise(0)
                dve.wait_ge(w_used[1], B_BASE[1] + j + 2)
                dve.tensor_scalar(sq_k, PS[:, 1, 0:N], bias[:, ds(j + 7 * KB, 1)], None, ALU.add).then_inc(k_step, 1)
                dve.wait_ge(k_step, j * 2 + 1)
                dve.tensor_tensor(sq_k, sq_k, sq_k, ALU.mult).then_inc(k_step, 1)
                dve.wait_ge(k_step, j * 2 + 2)
                dve.wait_ge(sq_done, j + 1)
                dve.tensor_tensor(sq_q, sq_q, sq_k, ALU.add).then_inc(sq_summed, 1)
                turned_lo(0)
                normalise(1)
                pv_sum(0)
                turned_lo(1)
                if not last:
                    split_qk(j + 1)
                dve.wait_ge(coeff_done, j + 1)
                dve.wait_ge(mixv_ready, j + 2)
                dve.tensor_tensor(mix_v, PS[:, 2, 0:N], mix_v, ALU.mult).then_inc(mix_ready, 1)
                dve.wait_ge(mh_ready, j + 1)
                j1 = ds(j, 1)
                dve.tensor_tensor(T1[1][:, j1, :].rearrange("p a n -> p (a n)"), mix_v,
                                  T1[0][:, j1, :].rearrange("p a n -> p (a n)").bitcast(F32),
                                  ALU.subtract).then_inc(ml_ready, 1)
                pv_sum(1)
                dve.wait_ge(oh_ready, j + 1)
                dve.tensor_tensor(T0[1][:, j1, :].rearrange("p a n -> p (a n)"), attn_o,
                                  T0[0][:, j1, :].rearrange("p a n -> p (a n)").bitcast(F32),
                                  ALU.subtract).then_inc(ol_ready, 1)

            split_qk(0)
            with dve.Fori(0, KB - 1) as j:
                pair(j, False)
            pair(KB - 1, True)

            dve.wait_ge(rows_in, 16)
            dve.wait_ge(xr_in, 16)
            for r in range(2):
                if r:
                    dve.wait_ge(res_ready, NT)
                for t in range(NT):
                    dve.tensor_tensor(x_rows[:, t, :], x_rows[:, t, :], row_bo[:, r, :], ALU.add).then_inc(res_ready, 1)
            dve.wait_ge(res_ready, 2 * NT)

            def add_sums(half, t):
                c = slice(half * HALF, (half + 1) * HALF)
                if t < NT - 1:
                    dve.wait_ge(c_done, half * (NT - 1) + t + 1)
                else:
                    slot, use = C_USES[8 * half + 7]
                    dve.wait_ge(w_used[slot], use + 2)
                dve.tensor_tensor(x_rows[:, t, c], PS[:, C_BANKS[half][t], :], x_rows[:, t, c],
                                  ALU.add).then_inc(x2_ready, 1)

            for t in range(NT):
                add_sums(0, t)
            for t in range(2):
                add_sums(1, t)
                dve.wait_ge(x2_ready, NT + t + 1)
                row_stats(1, t)
                if t == 0:
                    row_norm(1, 0, x2n_ready)
            add_sums(1, 2)
            row_norm(1, 1, x2n_ready)
            dve.wait_ge(x2_ready, 2 * NT)
            row_stats(1, 2)
            row_norm(1, 2, x2n_ready)
            for t in range(NT):
                dve.wait_ge(x2_hi, t + 1)
                src, r = turned(t)
                dve.tensor_tensor(xT[1][:, :, r], src, xT[0][:, :, r].bitcast(F32),
                                  ALU.subtract).then_inc(x2_done, 1)
            dve.memset(t0l[:, 0:2 * D].bitcast(F32), 0.0).then_inc(aug_zero, 1)
            dve.memset(hT[0][R:P, :].bitcast(F32), 0.0)
            dve.memset(hT[1][R:P, :].bitcast(F32), 0.0).then_inc(aug_zero, 1)
            dve.wait_ge(aug_zero, 2)
            dve.memset(hT[0][R:R + 1, :].bitcast(F32), 1.0).then_inc(aug_zero, 1)
            dve.wait_ge(x2_copied, NT)
            dve.tensor_reduce(moments[:, 0, :], xn_T, X, ALU.add).then_inc(moment_done, 1)
            for k in range(KB):
                if k:
                    dve.wait_ge(moment_done, k + 1)
                dve.tensor_tensor_reduce(sq_junk, xn_T[:, k, :], xn_T[:, k, :], 1.0, 0.0, ALU.mult, ALU.add,
                                         moments[:, 1, k:k + 1]).then_inc(moment_done, 1)
            ls = [0]

            def lstep(ins):
                ls[0] += 1
                ins.then_inc(loss_step, 1)
                dve.wait_ge(loss_step, ls[0])

            dve.wait_ge(moment_done, KB + 1)
            lstep(dve.tensor_scalar(moments[:, 2, :], moments[:, 1, :], 1.0 / N, None, ALU.mult))
            lstep(dve.tensor_scalar(moments[:, 3, :], moments[:, 0, :], -2.0 / N, None, ALU.mult))
            m2 = moments[:, 2:3, :].broadcast_to([P, EXPERTS, KB])
            m1 = moments[:, 3:4, :].broadcast_to([P, EXPERTS, KB])
            lstep(dve.tensor_tensor(dterm[:, 3], dterm[:, 0], m2, ALU.mult))
            lstep(dve.tensor_tensor(dterm[:, 4], dterm[:, 1], m1, ALU.mult))
            lstep(dve.tensor_tensor(dterm[:, 3], dterm[:, 3], dterm[:, 4], ALU.add))
            lstep(dve.tensor_tensor(dterm[:, 3], dterm[:, 3], dterm[:, 2], ALU.add))
            lstep(dve.tensor_reduce(loss[:, 0, :], dterm[:, 3], X, ALU.add))
            dve.wait_ge(loss_sum, 1)
            lstep(dve.tensor_copy(loss[:, 1, :], PS[:, 7, 0:EXPERTS]))
            lstep(dve.tensor_reduce(loss[:, 2, 0:1], loss[:, 1, :], X, ALU.min))
            lstep(dve.tensor_scalar(loss[:, 3, :], loss[:, 1, :], loss[:, 2, 0:1], 100.0, ALU.is_gt, ALU.mult))
            lstep(dve.tensor_tensor(loss[:, 3, :], loss[:, 3, :], eidx, ALU.add))
            lstep(dve.tensor_reduce(loss[:, 4, 0:1], loss[:, 3, :], X, ALU.min))
            lstep(dve.tensor_scalar(loss[:, 4, 0:1], loss[:, 4, 0:1], float(EXPERTS - 1), None, ALU.min))
            dve.tensor_copy(pick_i[:], loss[:, 4, 0:1]).then_inc(idx_ready, 1)
            for t in range(NT):
                dve.tensor_tensor(x_rows[:, t, :], x_rows[:, t, :], row_bo[:, 2, :], ALU.add).then_inc(res_ready, 1)
            dve.wait_ge(small_in, 64)
            dve.tensor_copy(wd[:, :, 0:R], raw_down).then_inc(down_hi, 1)
            dve.tensor_copy(aug[0][:, :, 0:R], raw_up).then_inc(aug_hi, 1)
            dve.tensor_copy(aug[0][:, :, R:R + 1], raw_upb.unsqueeze(2)).then_inc(aug_hi, 1)
            dve.wait_ge(down_hi, 1)
            dve.tensor_tensor(wd[:, :, R:P], raw_down, wd[:, :, 0:R].bitcast(F32), ALU.subtract).then_inc(down_ready, 1)
            dve.wait_ge(aug_hi, 2)
            dve.tensor_tensor(aug[1][:, :, 0:R], raw_up, aug[0][:, :, 0:R].bitcast(F32), ALU.subtract).then_inc(aug_ready, 1)
            dve.tensor_tensor(aug[1][:, :, R:R + 1], raw_upb.unsqueeze(2), aug[0][:, :, R:R + 1].bitcast(F32),
                              ALU.subtract).then_inc(aug_ready, 1)
            def split_lo(b):
                s, use = TAIL[b]
                dve.wait_ge(hi_ready[s], use + 1)
                dve.tensor_tensor(w_lo[s][:], raw[s][:], w_hi[s][:].bitcast(F32),
                                  ALU.subtract).then_inc(lo_ready[s], 1)

            split_lo(25)
            dve.wait_ge(convb_in, 16)
            dve.wait_ge(res_ready, 3 * NT)
            for t in range(NT):
                dve.tensor_tensor(x_rows[:, t, :], x_rows[:, t, :], conv_row, ALU.add).then_inc(res_ready, 1)
            def split_p(half):
                c = slice(half * HALF, (half + 1) * HALF)
                dve.wait_ge(pc_hi, half + 1)
                dve.tensor_tensor(pc[1][:, c], PS[:, 6 + half, :], pc[0][:, c].bitcast(F32), ALU.subtract).then_inc(pc_ready, 1)

            split_lo(28)
            dve.wait_ge(hlow_ready, 1)
            dve.tensor_tensor(h_sum[0:R, :], PS[0:R, 7, 0:N], h_low[0:R, :], ALU.add).then_inc(h_step, 1)
            dve.wait_ge(h_step, 1)
            dve.tensor_scalar(h_sum[0:R, :], h_sum[0:R, :], raw_downb[0:R, :], 0.0, ALU.add, ALU.max).then_inc(h_step, 1)
            dve.wait_ge(hT_hi, 1)
            dve.tensor_tensor(hT[1][0:R, :], h_sum[0:R, :], hT[0][0:R, :].bitcast(F32), ALU.subtract).then_inc(hT_ready, 1)
            split_lo(30)
            split_p(0)
            split_lo(31)

            def final_rows(half):
                c = slice(half * HALF, (half + 1) * HALF)
                for t in range(NT):
                    dve.wait_ge(y_done, half * NT + t + 1)
                    dve.tensor_tensor(x_rows[:, t, c], PS[:, E_BANKS[half][t], :], x_rows[:, t, c],
                                      ALU.add).then_inc(y_ready, 1)

            dve.wait_ge(res_ready, 4 * NT)
            final_rows(0)
            split_p(1)
            final_rows(1)

        @block.tensor
        def _(pe):
            def turn(t, turned):
                for k in range(KB):
                    last = pe.transpose(PS[:, LN_BANKS[t] + k // 4, (k % 4) * P:(k % 4 + 1) * P],
                                        xn_rows[:, t, k * P:(k + 1) * P], ident)
                last.then_inc(turned, 1)

            def column_job(slot, use, src, bank, ks=range(KB)):
                o = PS[:, bank, 0:N]
                pe.wait_ge(hi_ready[slot], use + 1)
                for k in ks:
                    wh = w_hi[slot][:, k * P:(k + 1) * P]
                    pe.matmul(o, wh, src[0][:, k, :], start=(k == 0), stop=False)
                    pe.matmul(o, wh, src[1][:, k, :], start=False, stop=False)
                pe.wait_ge(lo_ready[slot], use + 2)
                for k in ks:
                    wl = w_lo[slot][:, k * P:(k + 1) * P]
                    last = pe.matmul(o, wl, src[0][:, k, :], start=False, stop=(k == KB - 1))
                if ks[-1] == KB - 1:
                    last.then_inc(w_used[slot], 1)

            def rows_of(bank, src, weights_in, part, slot, kp, k2, t, start, stop):
                return pe.matmul(bank, src[part][:, 2 * kp + k2, t * P:(t + 1) * P],
                                 weights_in[slot][:, k2 * HALF:(k2 + 1) * HALF], start=start, stop=stop)

            def row_block(slot, use, src, banks, kp, first):
                pe.wait_ge(hi_ready[slot], use + 1)
                for part in range(2):
                    for k2 in range(2):
                        for t in range(NT):
                            rows_of(banks[t], src, w_hi, part, slot, kp, k2, t,
                                    first and part == 0 and k2 == 0, False)
                pe.wait_ge(lo_ready[slot], use + 2)
                for k2 in range(2):
                    for t in range(NT):
                        last = rows_of(banks[t], src, w_lo, 0, slot, kp, k2, t, False, False)
                last.then_inc(w_used[slot], 1)

            def row_tile(bank, src, t, kp, slots, first, final):
                lasts = []
                for n, slot in enumerate(slots):
                    for k2 in range(2):
                        for part in range(2):
                            rows_of(bank, src, w_hi, part, slot, kp + n, k2, t,
                                    first and n == 0 and k2 == 0 and part == 0, False)
                    for k2 in range(2):
                        last = rows_of(bank, src, w_lo, 0, slot, kp + n, k2, t, False,
                                       final and n == 1 and k2 == 1)
                    lasts.append(last)
                return lasts

            def split_ready(slots_and_uses):
                for slot, use in slots_and_uses:
                    pe.wait_ge(hi_ready[slot], use + 1)
                    pe.wait_ge(lo_ready[slot], use + 2)

            pe.wait_ge(cst_in, 16)
            pe.wait_ge(xn_ready, 1)
            turn(0, xt_turned)
            pe.wait_ge(xn_mid, 1)
            turn(1, xt_turned)
            pe.wait_ge(xn_ready, 2)
            turn(2, xt_turned)

            pe.wait_ge(xt_done, NT)
            for m in range(6):
                src = [xT, xT, T0, xT, T1, T0][m]
                if m == 0:
                    pe.wait_ge(prep, 4)
                    for t in range(NT):
                        pe.matmul(PS[:, 2 + t, 0:N], diag_w, diag16[:, (2 - t) * P:(5 - t) * P],
                                  start=True, stop=False)
                if m == 2:
                    pe.wait_ge(table1_read, 1)
                    for t in range(NT):
                        pe.matmul(PS[:, 2 + t, 0:N], diag16[:, 0:P], diag16[:, 0:N], start=True, stop=False)
                with pe.Fori(0, KB // 2) as i:
                    for s in range(2):
                        job = i * 2 + (8 * m + s)
                        pe.wait_ge(bank_free[s], i + (A_BASE[m] + 1))
                        column_job(s, A_BASE[m] + i, src, s)
                        if m < 4:
                            pe.wait_ge(hot_ready, job * 2 * CJ + 2 * CJ)
                            for c in range(CJ):
                                for t in range(NT):
                                    last = pe.matmul(PS[:, 2 + t, 0:N], src_hot[:, s, c, t * P:(t + 1) * P],
                                                     dst_hot[:, s, c, :], start=False, stop=False)
                            last.then_inc(hot_used, 1)
                if m in (1, 3):
                    for t in range(NT):
                        last = pe.matmul(PS[:, 2 + t, 0:N], zero16[:], diag16[:, 0:N], start=False,
                                         stop=True)
                    last.then_inc(table_done, 1)

            pe.wait_ge(keys_zeroed, 2)
            pe.wait_ge(aprep, 3)
            pe.wait_ge(mask_step, 11)
            pe.wait_ge(bank_free[0], 1 + 24)
            with pe.Fori(0, KB) as j:
                pe.wait_ge(mixv_ready, j + 1)
                column_job(0, B_BASE[0] + j, xT, 0)
                pe.wait_ge(v_in, j * 16 + 16)
                pe.wait_ge(o_summed, j * 2 + 1)
                for t in range(NT):
                    last = pe.transpose(PS[:, 7, t * P:(t + 1) * P], v_cur[:, t * P:(t + 1) * P], ident)
                last.then_inc(v_turned, 1)
                pe.wait_ge(k_flipped, j * 2 + 2)
                pe.wait_ge(ql_ready, j * 2 + 2)
                pe.wait_ge(kl_ready, j * 2 + 2)
                pe.wait_ge(mix_ready, j + 1)
                for h in range(2):
                    for t in range(NT):
                        pe.wait_ge(score_read, j * 6 + (2 if h and t == NT - 1 else 1))
                        r = slice(t * P, (t + 1) * P)
                        bank = PS[:, SCORE_BANKS[h][t], 0:N]
                        pe.matmul(bank, q_both[h][:, r], k_hi2[h][:], start=True, stop=False)
                        pe.matmul(bank, q_both[h][:, r], k_lo0[h][:], start=False,
                                  stop=True).then_inc(score_done, 1)
                column_job(1, B_BASE[1] + j, xT, 1)

                def turn_probs(h):
                    pe.wait_ge(prob_ready, j * 6 + (3 * h + 3))
                    for m in range(NT):
                        bank = TURN_BANKS[m]
                        if h:
                            pe.wait_ge(pT_ready, j * 6 + (m + 1))
                        for t in range(NT):
                            last = pe.transpose(PS[:, bank, t * P:(t + 1) * P],
                                                prob[:, h, t, m * P:(m + 1) * P], ident)
                        last.then_inc(prob_turned, 1)

                def pv(h):
                    pe.wait_ge(pT_ready, j * 6 + (3 * h + 3))
                    for m in range(NT):
                        for part in range(2):
                            last = pe.matmul(PS[:, 7, 0:N], vs[:, m, h, :], probT[part][:, m, :],
                                             start=(m == 0 and part == 0), stop=(m == NT - 1 and part == 1))
                    last.then_inc(pv_done, 1)

                pe.wait_ge(score_read, j * 6 + 7)
                turn_probs(0)
                pe.wait_ge(sq_done, j + 1)
                column_job(2, B_BASE[2] + j, xT, 0, range(0, KB // 2 + 1))
                pe.wait_ge(vs_ready, j + 1)
                pv(0)
                pe.wait_ge(feat_hi, j + 1)
                pe.matmul(PS[:, 2, 0:N], head_ones[:], feat[0][:], start=True, stop=False)
                pe.wait_ge(feat_ready, j + 1)
                pe.matmul(PS[:, 2, 0:N], head_ones[:], feat[1][:], start=False, stop=True).then_inc(coeff_done, 1)
                turn_probs(1)
                column_job(2, B_BASE[2] + j, xT, 0, range(KB // 2 + 1, KB))
                pe.wait_ge(o_summed, j * 2 + 2)
                pv(1)

            for half in range(2):
                banks = [PS[:, b, :] for b in C_BANKS[half]]
                uses = C_USES[8 * half:8 * half + 8]
                for b in range(6):
                    pe.wait_ge(ol_ready if b >= 4 else ml_ready, 2 * (b % 4) + 2)
                    row_block(*uses[b], T1 if b < 4 else T0, banks, b % 4, b == 0)
                split_ready(uses[6:8])
                pe.wait_ge(ol_ready, KB)
                slots = (uses[6][0], uses[7][0])
                for t in range(NT):
                    lasts = row_tile(banks[t], T0, t, 2, slots, False, True)
                    if t < NT - 1:
                        lasts[1].then_inc(c_done, 1)
                for slot, last in zip(slots, lasts):
                    last.then_inc(w_used[slot], 1)
            pe.wait_ge(x2n_ready, 1)
            turn(0, x2_turned)
            pe.wait_ge(x2n_mid, 1)
            turn(1, x2_turned)
            pe.wait_ge(x2n_ready, 2)
            turn(2, x2_turned)
            split_ready(E_USES[0:2])
            slots = (E_USES[0][0], E_USES[1][0])
            for t in range(NT):
                pe.wait_ge(x2_done, t + 1)
                if t == NT - 1:
                    pe.wait_ge(x2_copied, NT)
                lasts = row_tile(PS[:, E_BANKS[0][t], :], xT, t, 0, slots, True, False)
            for slot, last in zip(slots, lasts):
                last.then_inc(w_used[slot], 1)
            for b in (2, 3):
                row_block(*E_USES[b], xT, [PS[:, n, :] for n in E_BANKS[0]], b, False)
            pe.wait_ge(loss_step, 7)
            pe.matmul(PS[:, 7, 0:EXPERTS], ones_f32, loss[:, 0, :], start=True, stop=True).then_inc(loss_sum, 1)
            for b in range(3):
                row_block(*E_USES[4 + b], xT, [PS[:, n, :] for n in E_BANKS[1]], b, b == 0)

            def y_sums(half):
                c = slice(half * HALF, (half + 1) * HALF)
                pe.wait_ge(pc_ready, half + 1)
                for t in range(NT):
                    r = slice(t * P, (t + 1) * P)
                    o = PS[:, E_BANKS[half][t], :]
                    pe.matmul(o, hT[0][:, r], pc[0][:, c], start=False, stop=False)
                    pe.matmul(o, hT[1][:, r], pc[0][:, c], start=False, stop=False)
                    pe.matmul(o, hT[0][:, r], pc[1][:, c], start=False, stop=True).then_inc(y_done, 1)

            def x_down():
                pe.wait_ge(down_ready, 1)
                for k in range(KB):
                    for part in range(2):
                        last = pe.matmul(PS[:, 7, 0:N], wd[:, k, :], xT[part][:, k, :],
                                         start=(k == 0 and part == 0), stop=(k == KB - 1 and part == 1))
                last.then_inc(hdown_done, 1)

            pe.wait_ge(aug_ready, 2)
            for b, (s, use) in enumerate(V_USES):
                half, kp = b // 4, b % 4
                o = PS[:, 6 + half, :]
                if b == 3:
                    row_block(*E_USES[7], xT, [PS[:, n, :] for n in E_BANKS[1]], 3, False)
                    x_down()
                if b == 7:
                    pe.wait_ge(hT_ready, 1)
                    pe.wait_ge(aug_zero, 3)
                    y_sums(0)
                if b == 4:
                    pe.wait_ge(h_step, 1)
                pe.wait_ge(hi_ready[s], use + 1)
                for k2 in range(2):
                    for part in range(2):
                        pe.matmul(o, aug[part][:, 2 * kp + k2, :], w_hi[s][:, k2 * HALF:(k2 + 1) * HALF],
                                  start=(kp == 0 and k2 == 0 and part == 0), stop=False)
                pe.wait_ge(lo_ready[s], use + 2)
                for k2 in range(2):
                    last = pe.matmul(o, aug[0][:, 2 * kp + k2, :], w_lo[s][:, k2 * HALF:(k2 + 1) * HALF],
                                     start=False, stop=(kp == 3 and k2 == 1))
                last.then_inc(w_used[s], 1)
            y_sums(1)


def columns(w):
    return w.reshape(KB, P, KB, P).transpose(2, 1, 0, 3).reshape(KB, P, D)


def halves(w):
    return w.reshape(4, 2, P, 2, HALF).transpose(3, 0, 2, 1, 4).reshape(8, P, D)


def kernel(**inputs):
    import numpy as np
    import concourse.bacc as bacc
    from concourse.bass_utils import run_bass_kernel_spmd

    a = {k.replace("L0_", ""): np.asarray(v) for k, v in inputs.items()}
    first = [columns(a["gnn_" + n].T) for n in ("wq", "wk", "wiq", "wv", "wik", "wiv")]
    mixer = [columns(a["mix_" + n]) for n in ("Wq", "Wk", "Wv")]
    wo, mo = halves(a["gnn_wo"].T), halves(a["mix_Wo"])
    outs = [mo[0:4], wo[0:4], mo[4:8], wo[4:8]]
    weights = np.concatenate(first + mixer + outs + [halves(a["ffn_base_W"].T)])
    conv = np.concatenate([halves(a["ffn_conv_W"][e].T) for e in range(EXPERTS)])
    names = ["gnn_bq", "gnn_bk", "gnn_biq", "gnn_bv", "gnn_bik", "gnn_biv", "mix_bq", "mix_bk", "mix_bv"]
    disc = np.stack([a["ffn_disc_mu"], a["ffn_disc_sigma"]]).reshape(2, EXPERTS, KB, P)
    edges = [a["src"], a["dst"], a["edge_type_5"]]
    lane = np.arange(P)
    consts = np.zeros((P, C_ALL), np.float32)
    consts[:, C_ID:C_ID + P] = np.eye(P)
    consts[:, C_IOTA:C_IOTA + N] = np.arange(N)
    consts[:, C_TRI:C_TRI + P] = lane[None, :] > lane[:, None]
    consts[:, C_POW:C_POW + CH] = 2.0 ** (4.0 * (np.arange(CH) % GCH) - 95)
    consts[:, C_ONES:C_ONES + P] = lane[None, :] // HD == lane[:, None] // HD
    consts[:, C_EIDX:C_EIDX + EXPERTS] = np.arange(EXPERTS)
    consts[:, C_ONE:C_ONE + P] = 1.0
    arrays = {
        "x": a["x"],
        "weights": weights,
        "conv": conv,
        "down": a["ffn_down_W"].reshape(EXPERTS, KB, P, R).transpose(0, 2, 1, 3),
        "upT": a["ffn_up_W"].reshape(EXPERTS, R, KB, P).transpose(0, 3, 2, 1),
        "up_b": a["ffn_up_b"].reshape(EXPERTS, KB, P).transpose(0, 2, 1),
        "down_b": a["ffn_down_b"].reshape(EXPERTS, R, 1),
        "conv_b": a["ffn_conv_b"],
        "disc": disc.transpose(3, 0, 1, 2),
        "bias_cols": np.concatenate([a[n].reshape(KB, P) for n in names]).T,
        "rows": np.stack([a["gnn_bo"], a["mix_bo"], a["ffn_base_b"]]),
        "edge_weights": a["gnn_edge_type_weights"],
        "edge_rows": np.concatenate([e.reshape(CH, P) for e in edges[:2]], axis=1),
        "edge_cols": np.concatenate([e.reshape(CH, P).T for e in edges], axis=1),
        "consts": consts,
    }
    arrays = {k: np.ascontiguousarray(v) for k, v in arrays.items()}
    nc = bacc.Bacc("TRN2", target_bir_lowering=False, num_devices=1)
    args = {k: nc.dram_tensor(k, v.shape, mybir.dt.from_np(v.dtype), kind="ExternalInput").ap()
            for k, v in arrays.items()}
    out = nc.dram_tensor("out", (N, D), F32, kind="ExternalOutput").ap()
    gps_layer(nc, out=out, **args)
    r = run_bass_kernel_spmd(nc, [arrays], core_ids=[0])
    return r.results[0]["out"]
```
